# Optimizing a Trainium2 kernel written in Bass

```python
import numpy as np
import jax
import jax.numpy as jnp

def _softmax(x, axis=-1):
    return jax.nn.softmax(x, axis=axis)

def _gelu(x):
    return jax.nn.gelu(x, approximate=True)

def _silu(x):
    return jax.nn.silu(x)

def _sigmoid(x):
    return jax.nn.sigmoid(x)

def _layernorm(x, axis=-1, eps=1e-05):
    m = jnp.mean(x, axis=axis, keepdims=True)
    v = jnp.var(x, axis=axis, keepdims=True)
    return (x - m) / jnp.sqrt(v + eps)

def _scatter_add(tgt, idx, src, axis=0):
    return tgt.at[idx].add(src)

def _segment_sum(src, seg, n):
    return jax.ops.segment_sum(src, seg, n)
kernel_name = 'mk_sandwich_d1_jaxref_r8_8c529c'

def setup_inputs(seed: int=0):
    np.random.seed(seed)
    _w = jnp.asarray

    def _L0_attn_setup():
        import jax, jax.numpy as jnp
        import numpy as np
        B, S, H, NH = (1, 512, 128, 16)
        DH = H // NH

        def _split_heads(x):
            b, s, h = x.shape
            return jnp.transpose(x.reshape(b, s, NH, DH), (0, 2, 1, 3))
        key = jax.random.key(seed)
        ks = jax.random.split(key, 9)
        sc = 0.02
        return {'queries': jax.random.normal(ks[0], (B, S, H), jnp.float32), 'keys': jax.random.normal(ks[1], (B, S, H), jnp.float32), 'values': jax.random.normal(ks[2], (B, S, H), jnp.float32), 'Wq_w': jax.random.normal(ks[3], (H, H), jnp.float32) * sc, 'Wq_b': jax.random.normal(ks[4], (H,), jnp.float32) * sc, 'Wk_w': jax.random.normal(ks[5], (H, H), jnp.float32) * sc, 'Wk_b': jax.random.normal(ks[6], (H,), jnp.float32) * sc, 'Wv_w': jax.random.normal(ks[7], (H, H), jnp.float32) * sc, 'Wv_b': jax.random.normal(ks[8], (H,), jnp.float32) * sc}
    _L0_attn_in = _L0_attn_setup()

    def _L0_ffn_setup():
        import jax, jax.numpy as jnp
        import numpy as np
        D = 128
        H = 4
        HD = D // H
        E = 8
        FF = 512
        CAP_FACTOR = 1.0

        def _ln(x, g, b, eps=1e-05):
            mu = jnp.mean(x, -1, keepdims=True)
            v = jnp.mean((x - mu) ** 2, -1, keepdims=True)
            return (x - mu) * jax.lax.rsqrt(v + eps) * g + b

        def _mha(x, w, b, ow, ob):
            L, N, _ = x.shape
            qkv = x @ w.T + b
            q, k, v = jnp.split(qkv, 3, axis=-1)
            rh = lambda t: t.reshape(L, N, H, HD).transpose(1, 2, 0, 3)
            q, k, v = (rh(q), rh(k), rh(v))
            scores = jnp.einsum('nhld,nhmd->nhlm', q, k) / np.float32(np.sqrt(HD))
            attn = jax.nn.softmax(scores, axis=-1)
            o = jnp.einsum('nhlm,nhmd->nhld', attn, v).transpose(2, 0, 1, 3).reshape(L, N, D)
            return o @ ow.T + ob

        def _moe(x, wg, w1, b1, w2, b2):
            L, N, _ = x.shape
            S = L * N
            cap = int(CAP_FACTOR * S) // E
            xf = x.reshape(S, D)
            gates = jax.nn.softmax(xf @ wg, axis=-1)
            idx = jnp.argmax(gates, axis=-1)
            mask1 = jax.nn.one_hot(idx, E, dtype=x.dtype)
            loc = jnp.sum((jnp.cumsum(mask1, 0) - 1.0) * mask1, -1).astype(jnp.int32)
            keep = loc < cap
            gate_val = jnp.take_along_axis(gates, idx[:, None], -1)[:, 0]
            slot = jnp.where(keep, idx.astype(jnp.int32) * cap + loc, E * cap)
            disp = jnp.zeros((E * cap, D), x.dtype).at[slot].set(xf, mode='drop')
            disp = disp.reshape(E, cap, D)
            h = jnp.einsum('ecd,edf->ecf', disp, w1) + b1[:, None, :]
            y = (jnp.einsum('ecf,efd->ecd', h, w2) + b2[:, None, :]).reshape(E * cap, D)
            out = jnp.where(keep[:, None], gate_val[:, None] * y[jnp.minimum(slot, E * cap - 1)], 0.0)
            return out.reshape(L, N, D)
        key = jax.random.key(seed)
        ks = jax.random.split(key, 8)
        L, N = (128, 16)
        s = 0.02
        return {'x': jax.random.normal(ks[0], (L, N, D), jnp.float32), 'in_proj_w': jax.random.normal(ks[1], (3 * D, D), jnp.float32) * s, 'in_proj_b': jnp.zeros((3 * D,), jnp.float32), 'out_proj_w': jax.random.normal(ks[2], (D, D), jnp.float32) * s, 'out_proj_b': jnp.zeros((D,), jnp.float32), 'ln1_g': jnp.ones((D,), jnp.float32), 'ln1_b': jnp.zeros((D,), jnp.float32), 'ln2_g': jnp.ones((D,), jnp.float32), 'ln2_b': jnp.zeros((D,), jnp.float32), 'wg': jax.random.normal(ks[3], (D, E), jnp.float32) * s, 'w1': jax.random.normal(ks[4], (E, D, FF), jnp.float32) * s, 'b1': jnp.zeros((E, FF), jnp.float32), 'w2': jax.random.normal(ks[5], (E, FF, D), jnp.float32) * s, 'b2': jnp.zeros((E, D), jnp.float32)}
    _L0_ffn_in = _L0_ffn_setup()
    _d = {'L0_attn_queries': _L0_attn_in['queries'], 'L0_attn_keys': _L0_attn_in['keys'], 'L0_attn_values': _L0_attn_in['values'], 'L0_attn_Wq_w': _L0_attn_in['Wq_w'], 'L0_attn_Wq_b': _L0_attn_in['Wq_b'], 'L0_attn_Wk_w': _L0_attn_in['Wk_w'], 'L0_attn_Wk_b': _L0_attn_in['Wk_b'], 'L0_attn_Wv_w': _L0_attn_in['Wv_w'], 'L0_attn_Wv_b': _L0_attn_in['Wv_b'], 'L0_ffn_in_proj_w': _L0_ffn_in['in_proj_w'], 'L0_ffn_in_proj_b': _L0_ffn_in['in_proj_b'], 'L0_ffn_out_proj_w': _L0_ffn_in['out_proj_w'], 'L0_ffn_out_proj_b': _L0_ffn_in['out_proj_b'], 'L0_ffn_ln1_g': _L0_ffn_in['ln1_g'], 'L0_ffn_ln1_b': _L0_ffn_in['ln1_b'], 'L0_ffn_ln2_g': _L0_ffn_in['ln2_g'], 'L0_ffn_ln2_b': _L0_ffn_in['ln2_b'], 'L0_ffn_wg': _L0_ffn_in['wg'], 'L0_ffn_w1': _L0_ffn_in['w1'], 'L0_ffn_b1': _L0_ffn_in['b1'], 'L0_ffn_w2': _L0_ffn_in['w2'], 'L0_ffn_b2': _L0_ffn_in['b2']}
    _x0 = _d['L0_attn_queries']
    _d['L0_attn_queries'] = jax.random.normal(jax.random.fold_in(jax.random.key(seed), 1), (8, 512, 128), dtype=_x0.dtype)
    del _x0
    return _d

def reference(L0_attn_queries, L0_attn_keys, L0_attn_values, L0_attn_Wq_w, L0_attn_Wq_b, L0_attn_Wk_w, L0_attn_Wk_b, L0_attn_Wv_w, L0_attn_Wv_b, L0_ffn_in_proj_w, L0_ffn_in_proj_b, L0_ffn_out_proj_w, L0_ffn_out_proj_b, L0_ffn_ln1_g, L0_ffn_ln1_b, L0_ffn_ln2_g, L0_ffn_ln2_b, L0_ffn_wg, L0_ffn_w1, L0_ffn_b1, L0_ffn_w2, L0_ffn_b2):

    def _L0_attn_ref(queries, keys, values, Wq_w, Wq_b, Wk_w, Wk_b, Wv_w, Wv_b):
        import jax, jax.numpy as jnp
        import numpy as np
        B, S, H, NH = (1, 512, 128, 16)
        DH = H // NH

        def _split_heads(x):
            b, s, h = x.shape
            return jnp.transpose(x.reshape(b, s, NH, DH), (0, 2, 1, 3))
        q = jax.nn.relu(queries @ Wq_w.T + Wq_b)
        k = jax.nn.relu(keys @ Wk_w.T + Wk_b)
        v = jax.nn.relu(values @ Wv_w.T + Wv_b)
        qh, kh, vh = (_split_heads(q), _split_heads(k), _split_heads(v))
        score = jnp.einsum('bhsd,bhtd->bhst', qh, kh) / jnp.sqrt(jnp.float32(DH))
        attn = jax.nn.softmax(score, axis=-1)
        a = jnp.einsum('bhst,bhtd->bhsd', attn, vh)
        a = jnp.transpose(a, (0, 1, 3, 2)).reshape(q.shape[0], q.shape[1], q.shape[2])
        return a + queries

    def _L0_ffn_ref(x, in_proj_w, in_proj_b, out_proj_w, out_proj_b, ln1_g, ln1_b, ln2_g, ln2_b, wg, w1, b1, w2, b2):
        import jax, jax.numpy as jnp
        import numpy as np
        D = 128
        H = 4
        HD = D // H
        E = 8
        FF = 512
        CAP_FACTOR = 1.0

        def _ln(x, g, b, eps=1e-05):
            mu = jnp.mean(x, -1, keepdims=True)
            v = jnp.mean((x - mu) ** 2, -1, keepdims=True)
            return (x - mu) * jax.lax.rsqrt(v + eps) * g + b

        def _mha(x, w, b, ow, ob):
            L, N, _ = x.shape
            qkv = x @ w.T + b
            q, k, v = jnp.split(qkv, 3, axis=-1)
            rh = lambda t: t.reshape(L, N, H, HD).transpose(1, 2, 0, 3)
            q, k, v = (rh(q), rh(k), rh(v))
            scores = jnp.einsum('nhld,nhmd->nhlm', q, k) / np.float32(np.sqrt(HD))
            attn = jax.nn.softmax(scores, axis=-1)
            o = jnp.einsum('nhlm,nhmd->nhld', attn, v).transpose(2, 0, 1, 3).reshape(L, N, D)
            return o @ ow.T + ob

        def _moe(x, wg, w1, b1, w2, b2):
            L, N, _ = x.shape
            S = L * N
            cap = int(CAP_FACTOR * S) // E
            xf = x.reshape(S, D)
            gates = jax.nn.softmax(xf @ wg, axis=-1)
            idx = jnp.argmax(gates, axis=-1)
            mask1 = jax.nn.one_hot(idx, E, dtype=x.dtype)
            loc = jnp.sum((jnp.cumsum(mask1, 0) - 1.0) * mask1, -1).astype(jnp.int32)
            keep = loc < cap
            gate_val = jnp.take_along_axis(gates, idx[:, None], -1)[:, 0]
            slot = jnp.where(keep, idx.astype(jnp.int32) * cap + loc, E * cap)
            disp = jnp.zeros((E * cap, D), x.dtype).at[slot].set(xf, mode='drop')
            disp = disp.reshape(E, cap, D)
            h = jnp.einsum('ecd,edf->ecf', disp, w1) + b1[:, None, :]
            y = (jnp.einsum('ecf,efd->ecd', h, w2) + b2[:, None, :]).reshape(E * cap, D)
            out = jnp.where(keep[:, None], gate_val[:, None] * y[jnp.minimum(slot, E * cap - 1)], 0.0)
            return out.reshape(L, N, D)
        y1 = _ln(x + _mha(x, in_proj_w, in_proj_b, out_proj_w, out_proj_b), ln1_g, ln1_b)
        y2 = _ln(y1 + _moe(y1, wg, w1, b1, w2, b2), ln2_g, ln2_b)
        return y2
    x = L0_attn_queries
    x = x + _layernorm(_L0_attn_ref(_layernorm(x, axis=-1), L0_attn_keys, L0_attn_values, L0_attn_Wq_w, L0_attn_Wq_b, L0_attn_Wk_w, L0_attn_Wk_b, L0_attn_Wv_w, L0_attn_Wv_b), axis=-1)
    x = x + _layernorm(_L0_ffn_ref(_layernorm(x, axis=-1), L0_ffn_in_proj_w, L0_ffn_in_proj_b, L0_ffn_out_proj_w, L0_ffn_out_proj_b, L0_ffn_ln1_g, L0_ffn_ln1_b, L0_ffn_ln2_g, L0_ffn_ln2_b, L0_ffn_wg, L0_ffn_w1, L0_ffn_b1, L0_ffn_w2, L0_ffn_b2), axis=-1)
    return x

_drawn_inputs = setup_inputs


def setup_inputs(seed=0):
    import zlib

    import numpy as np

    out = dict(_drawn_inputs(seed))
    spreads = {'L0_ffn_in_proj_b': (0.0, 0.8),
     'L0_ffn_out_proj_b': (0.0, 0.1),
     'L0_ffn_ln1_g': (1.0, 0.2),
     'L0_ffn_ln1_b': (0.0, 0.1),
     'L0_ffn_ln2_g': (1.0, 0.2),
     'L0_ffn_ln2_b': (0.0, 0.1),
     'L0_ffn_b1': (0.0, 0.8),
     'L0_ffn_b2': (0.0, 0.8)}
    factors = {'L0_attn_keys': 8.0,
     'L0_attn_values': 8.0,
     'L0_attn_Wq_w': 8.0,
     'L0_attn_Wq_b': 8.0,
     'L0_attn_Wk_w': 8.0,
     'L0_attn_Wk_b': 8.0,
     'L0_attn_Wv_w': 8.0,
     'L0_attn_Wv_b': 8.0,
     'L0_ffn_in_proj_w': 8.0,
     'L0_ffn_out_proj_w': 5.873,
     'L0_ffn_wg': 7.622,
     'L0_ffn_w1': 8.0,
     'L0_ffn_w2': 8.0}
    for name, (base, spread) in spreads.items():
        noise = np.random.default_rng([zlib.crc32(name.encode()), seed]).standard_normal(out[name].shape)
        drawn = base * np.exp(spread * noise) if base else spread * noise
        out[name] = jnp.asarray(drawn.astype(out[name].dtype))
    for name, factor in factors.items():
        out[name] = (out[name] * factor).astype(out[name].dtype)
    return out
```

```python
import math

import numpy as np

P = 128
D = 128
B = 8
S = 512
G = S // P
NH, DH = 16, 8
NH2, HD2 = 4, 32
E, FF = 8, 512
FC = FF // P
CAP = B * S // E
T = G * B
QB = 4
NQ = NH * B // QB
TC = S // P
PARTS = 3
PRODUCTS = [(0, 0), (1, 0), (2, 0), (0, 1), (1, 1), (0, 2)]
KROWS = DH * len(PRODUCTS)
SHIFT_ROW = KROWS
KPAD = 96
EPS = 1e-5
IT = NQ // 4
NT = P // 16
QPG = 2


def hold(engine, sem, value, passed):
    engine.wait_ge(sem, value)
    engine.sem_inc(passed, 1)


class Chain:

    def __init__(self, engine, sem, passed):
        self.engine, self.sem, self.passed, self.base, self.n = engine, sem, passed, 0, 0

    def done(self, ins):
        ins.then_inc(self.sem, 1)
        self.n += 1
        return ins

    def wait(self):
        if isinstance(self.base, int):
            self.engine.wait_ge(self.sem, self.base + self.n)
        else:
            hold(self.engine, self.sem, self.base + self.n, self.passed)

    def enter(self, i, per):
        self.fixed, self.per, self.base, self.n = self.base + self.n, per, i * per + (self.base + self.n), 0

    def leave(self, times):
        assert self.n == self.per, (self.n, self.per)
        self.base, self.n = self.fixed + times * self.per, 0


def build(nc, x, keys, values, wq, bq, wk, bk, wv, bv, win, bin_, wout, bout,
          ln1g, ln1b, ln2g, ln2b, wg, w1, b1, w2, b2, out):
    from contextlib import ExitStack
    from concourse import mybir
    from concourse.bass import ds as bass_ds

    F32, BF16 = mybir.dt.float32, mybir.dt.bfloat16
    ALU, ACT, AX = mybir.AluOpType, mybir.ActivationFunctionType, mybir.AxisListType
    ADD, SUB, MUL, MAX = ALU.add, ALU.subtract, ALU.mult, ALU.max

    with ExitStack() as ctx:
        def sb(name, shape, dt=F32):
            return ctx.enter_context(nc.sbuf_tensor(name, shape, dt))

        def sem(name):
            return ctx.enter_context(nc.semaphore(name))

        q_dram = nc.dram_tensor("q_parts_dram", (PARTS, P, B * S), BF16, kind="Internal").ap()
        k_dram = nc.dram_tensor("k_rows_dram", (NH, KROWS, S), BF16, kind="Internal").ap()
        a_dram = nc.dram_tensor("attended_dram", (2, B, P, S), F32, kind="Internal").ap()
        a_tok = a_dram.rearrange("w b (g q) (j f) -> w g (q j) b f", g=G, j=S // D)

        ps = ctx.enter_context(nc.psum_tensor("ps", [P, 8, 512], F32))

        X = sb("X", [P, G, B, D])
        XN = sb("XN", [P, G, B, D])
        w_in = sb("w_in", [P, 7, D])
        wT = sb("wT", [P, 7, D])
        bias_col = sb("bias_col", [P, 6])
        bv_row = sb("bv_row", [P, D])
        rows = sb("rows", [P, 5, D])
        wg_sb = sb("wg_sb", [P, E])
        w1T = sb("w1T", [P, 2, FC, D])
        b1_sb = sb("b1_sb", [E, FF])
        b1T = sb("b1T", [P, FC, E])
        W = sb("W", [P, E, D])
        c_parts = sb("c_parts", [1, PARTS, E * D], BF16)
        c_stack = sb("c_stack", [KPAD, E * D], BF16)
        ones_stack = sb("ones_stack", [KPAD, P], BF16)
        ident = sb("ident", [P, P])
        ident16 = sb("ident16", [P, P], BF16)
        upper = sb("upper", [P, P], BF16)
        all_ones = sb("all_ones", [P, P], BF16)
        same_row = sb("same_row", [P, P])
        first_e = sb("first_e", [P, T * E])
        first_t = sb("first_t", [P, T * E])

        space1, space2, space3 = sb("space1", [P, 4096]), sb("space2", [P, 6144]), sb("space3", [P, 4096])
        space4, space5, space6 = sb("space4", [P, 4096]), sb("space5", [P, 4096]), sb("space6", [P, 4096])
        space7, space8 = sb("space7", [P, 2048]), sb("space8", [P, 2048])

        def view(space, lo, dims, dt=F32, parts=P):
            n = int(np.prod(dims))
            words = n if dt == F32 else n // 2
            v = space[0:parts, lo:lo + words]
            if dt != F32:
                v = v.bitcast(dt)
            names = "abcd"[:len(dims)]
            if len(dims) == 1:
                return v
            return v.rearrange(f"p ({' '.join(names)}) -> p {' '.join(names)}", **dict(zip(names[1:], dims[1:])))

        featT = view(space1, 0, [B, S])
        w2_sb = view(space1, 0, [E, FC, D])
        YT = view(space1, 0, [G, B, P])
        YT_tiles = view(space1, 0, [G, NT, B, 16])
        ET = view(space1, 0, [QPG, 16, P])
        q_parts = view(space2, 0, [PARTS, B * S], BF16)
        w1_sb = view(space2, 0, [E, FF])
        QF = view(space2, 0, [G, NT, P])
        SE = view(space2, 0, [4, E, D])
        q_stack = view(space3, 0, [4, QB * S], BF16, KPAD)
        KF = view(space3, 0, [G, NT, P])
        probs = view(space4, 0, [2, QB, S])
        VT = view(space4, 0, [G, NT, D])
        qf = view(space5, 0, [2, S])
        rest = view(space5, 1024, [2, S])
        v_heads = view(space5, 2048, [TC, NH, 32])
        b2_sb = view(space5, 0, [E * D], F32, 1)
        c_row = view(space5, 1024, [E * D], F32, 1)
        c_rest = view(space5, 2048, [E * D], F32, 1)
        OT = view(space5, 0, [G, B, P])
        kv_in = view(space6, 0, [2, TC, D])
        kvT = view(space6, 1024, [2, S])
        k_rest = view(space6, 2048, [2, S])
        k_parts = view(space6, 3072, [PARTS, S], BF16)
        A = view(space6, 0, [G, B, D])
        EX = view(space6, 0, [QPG, 16, P])
        k_plain = view(space7, 0, [4, S], BF16, KPAD)
        k_shift = view(space7, 1024, [4, S], BF16, KPAD)
        DEN = view(space7, 0, [2, B, D])

        SM = view(space8, 0, [16, P])
        lsub, gexp, eq, cum, place = (view(space8, k * T * E, [T * E]) for k in range(5))
        tot, incl = (view(space8, k * T * E, [E, B, G]) for k in (5, 6))

        v_tmp = sb("v_tmp", [P, TC, D])
        v_head = sb("v_head", [P, 2, TC, 32])
        row_max = sb("row_max", [P, 2, QB * TC])
        max_rest = sb("max_rest", [P, 2, QB * TC])
        max_parts = sb("max_parts", [P, 2, PARTS, QB * TC], BF16)
        max_turned = sb("max_turned", [PARTS * QB * TC, 2, P], BF16)
        attended = sb("attended", [P, 2, S])
        st6 = sb("st6", [P, B, 6])
        small = sb("small", [P, 5, B])
        SC = sb("SC", [P, 2 * G, 16, B])
        PC = sb("PC", [P, 2 * G, 16, B])
        mx, sm2 = sb("mx", [P, 2 * G, 16]), sb("sm2", [P, 2 * G, 16])
        lmax, gate = sb("lmax", [P, T]), sb("gate", [P, T])
        weight = sb("weight", [P, T * E])
        mask1 = sb("mask1", [P, T * E], BF16)

        s_x = [sem(f"x_loaded{g}") for g in range(G)]
        s_kv, s_w, s_b, s_w1, s_w2, s_bc = sem("kv_loaded"), sem("w_loaded"), sem("b_loaded"), sem("w1_loaded"), sem("w2_loaded"), sem("rows_loaded")
        s_b2 = sem("b2_loaded")
        s_passed_pool, s_passed_dve, s_passed_pe = sem("passed_pool"), sem("passed_dve"), sem("passed_pe")
        s_const = sem("constants_set")
        s_pc, s_dc, s_ac = sem("pool_chain"), sem("dve_chain"), sem("act_chain")
        s_wt, s_wtc = sem("w_turned"), sem("wT_copied")
        s_kvt, s_kvtc = sem("kv_turned"), sem("kvT_copied")
        s_kp, s_kpe = sem("k_projected"), sem("k_evacuated")
        s_vp, s_vpe = sem("v_projected"), sem("v_evacuated")
        s_ks, s_kst = sem("k_split"), sem("k_stored")
        s_xn, s_xt, s_xtc = sem("x_normed"), sem("x_turned"), sem("xT_copied")
        s_qp, s_qe, s_qs, s_qst = sem("q_projected"), sem("q_evacuated"), sem("q_split"), sem("q_stored")
        s_var, s_sd = sem("variance_ready"), sem("deviation_ready")
        s_vb = sem("v_biased")
        s_vset = sem("v_heads_set")
        s_ql = [sem(f"stack_loaded{j}") for j in range(4)]
        s_full, s_free = sem("rows_scored"), sem("rows_reduced")
        s_split, s_shift = sem("max_split"), sem("shift_loaded")
        s_sc, s_pr = sem("columns_scored"), sem("probs_ready")
        s_v = sem("v_head_ready")
        s_pv, s_pve = sem("pv_ready"), sem("pv_evacuated")
        s_ast = [sem("attended_stored0"), sem("attended_stored1")]

        (s_al, s_rec, s_r1, s_n1, s_r2, s_n2, s_r3) = ([sem(f"attended_loaded{g}") for g in range(G)], sem("attention_divided"),
            sem("residual1_added"), sem("norm1_done"), sem("residual2_added"), sem("encoder_input_ready"), sem("out_bias_added"))
        (s_b1t, s_b1c, s_w1t, s_w1c, s_W, s_Wc) = (sem(n) for n in
            ("b1_turned", "b1T_copied", "w1_turned", "w1T_copied", "w12_multiplied", "W_copied"))
        (s_crow, s_csplit, s_cl) = (sem(n) for n in ("c_row_ready", "c_split", "c_loaded"))
        (s_t, s_yt, s_pj, s_qkv) = (sem(n) for n in ("tokens_turned", "tokensT_copied", "qkv_projected", "qkv_copied"))
        (s_s2, s_msk, s_sub, s_e2, s_soft) = (sem(n) for n in
            ("scores2_ready", "scores2_masked", "scores2_less_max", "exp2_done", "softmax2_done"))
        (s_ex, s_ext, s_et, s_av, s_ot) = (sem(n) for n in
            ("probs2_spread", "probs2_turned", "probs2T_copied", "attended2_ready", "attended2_copied"))
        (s_op, s_n3, s_y1, s_lg, s_oh, s_ge, s_cnt, s_gate) = (sem(n) for n in
            ("out_projected", "norm3_done", "y1_ready", "logits_ready", "expert_masks_ready", "gate_exp_done",
             "tokens_counted", "weights_ready"))
        (s_xp, s_we, s_moe, s_n4, s_aff, s_n5, s_y2, s_out) = (sem(n) for n in
            ("experts_done", "experts_weighed", "experts_summed", "norm4_done", "affine2_done", "norm5_done",
             "output_ready", "output_stored"))

        same = lambda t: t.rearrange("p a b -> p (a b)")

        x_tok = x.rearrange("b (g p) f -> g p b f", p=P)
        out_tok = out.rearrange("b (g p) f -> g p b f", p=P)

        def norm(dve, ch, k, src, dst):
            for b in range(B):
                ins = dve.bn_stats(st6[:, b, :], src[:, b, :])
            ch.done(ins)
            ch.wait()
            me, m2e, mo, m2o = (st6[:, :, j] for j in (1, 2, 4, 5))
            mean, diff, var, inv = (small[:, j, :] for j in range(4))
            ch.done(dve.tensor_tensor(mean, me, mo, ADD))
            ch.done(dve.tensor_tensor(diff, me, mo, SUB))
            ch.done(dve.tensor_tensor(var, m2e, m2o, ADD))
            ch.wait()
            ch.done(dve.scalar_tensor_tensor(small[:, 4, :], diff, D / 4.0, diff, MUL, MUL))
            ch.done(dve.tensor_scalar(mean, mean, 0.5, None, MUL))
            ch.wait()
            ch.done(dve.tensor_tensor(var, var, small[:, 4, :], ADD))
            ch.wait()
            dve.tensor_scalar(var, var, 1.0 / D, EPS, MUL, ADD).then_inc(s_var, 1)
            dve.wait_ge(s_sd, k + 1)
            ch.done(dve.reciprocal(inv, var))
            ch.wait()
            for b in range(B):
                ins = dve.tensor_scalar(dst[:, b, :], src[:, b, :], small[:, 0, b:b + 1], small[:, 3, b:b + 1], SUB, MUL)
            return ins

        NORM = 8

        def root(act, k):
            act.wait_ge(s_var, k + 1)
            act.activation(small[:, 2, :], small[:, 2, :], ACT.Sqrt).then_inc(s_sd, 1)


        def project_q(act, b):
            act.wait_ge(s_qp, b + 1)
            if b >= 2:
                act.wait_ge(s_qs, b - 1)
            act.activation(qf[:, b % 2], ps[:, b, :], ACT.Relu, bias=bias_col[:, 0:1]).then_inc(s_ac, 1)
            act.activation(q_parts[:, 0, b * S:(b + 1) * S], ps[:, b, :], ACT.Relu,
                           bias=bias_col[:, 0:1]).then_inc(s_qe, 1)


        def bcast(row, k):
            return row.rearrange("p (o f) -> p o f", o=1).broadcast_to([P, k, D])

        def back_end_sp(sp):
            for g in range(G):
                sp.dma_start(A[:, g], a_tok[0, g]).then_inc(s_al[g], 16)
                if g >= 2:
                    sp.wait_ge(s_rec, g - 1)
                sp.dma_start(DEN[:, g % 2], a_tok[1, g]).then_inc(s_al[g], 16)
            sp.wait_ge(s_csplit, 1)
            sp.dma_start(c_stack[0:PARTS, :], c_parts[0:1, :, :]).then_inc(s_cl, 16)
            for g in range(G):
                sp.wait_ge(s_y2, g + 1)
                sp.dma_start(out_tok[g], A[:, g]).then_inc(s_out, 16)
            sp.wait_ge(s_out, 16 * G)

        def back_end_pool(pool, ch):
            with pool.Fori(0, G) as g:
                hold(pool, s_rec, g + 1, s_passed_pool)
                pool.tensor_tensor(same(A[:, g]), same(A[:, g]), same(XN[:, g]), ADD).then_inc(s_r1, 1)
            pool.wait_ge(s_crow, 1)
            ch.done(pool.tensor_copy(c_parts[:, 0], c_row))
            ch.wait()
            ch.done(pool.tensor_tensor(c_rest, c_row, c_parts[:, 0], SUB))
            ch.wait()
            ch.done(pool.tensor_copy(c_parts[:, 1], c_rest))
            ch.wait()
            pool.tensor_tensor(c_parts[:, 2], c_rest, c_parts[:, 1], SUB).then_inc(s_csplit, 1)
            with pool.Fori(0, G) as g:
                hold(pool, s_n1, g + 1, s_passed_pool)
                pool.tensor_tensor(same(X[:, g]), same(X[:, g]), same(A[:, g]), ADD).then_inc(s_r2, 1)
            with pool.Fori(0, G) as g:
                hold(pool, s_n2, g + 1, s_passed_pool)
                pool.tensor_tensor(XN[:, g], A[:, g], bcast(rows[:, 4, :], B), ADD).then_inc(s_r3, 1)
            pool.wait_ge(s_yt, 2 * G)
            pool.wait_ge(s_r3, G)

            def spread(g, half):
                q = QPG * g + half
                hold(pool, s_soft, q + 1, s_passed_pool)
                if not isinstance(g, int):
                    hold(pool, s_ext, 2 * q - 2, s_passed_pool)
                for h in range(NH2):
                    pool.tensor_tensor(
                        EX[:, half, 4 * h:4 * h + 4, :].rearrange("p t (m n) -> p t m n", n=16),
                        PC[:, q, 4 * h:4 * h + 4, :].rearrange("p t (m o) -> p t m o", o=1).broadcast_to([P, 4, B, 16]),
                        same_row[:].rearrange("p (o m n) -> p o m n", o=1, n=16).broadcast_to([P, 4, B, 16]),
                        MUL).then_inc(s_ex, 1)

            for half in range(QPG):
                spread(0, half)
            with pool.Fori(1, G) as g:
                for half in range(QPG):
                    spread(g, half)
            with pool.Fori(0, G) as g:
                hold(pool, s_n3, g + 1, s_passed_pool)
                ch.enter(g, 1)
                ch.done(pool.tensor_tensor(A[:, g], A[:, g], bcast(rows[:, 0, :], B), MUL))
                ch.wait()
                pool.tensor_tensor(A[:, g], A[:, g], bcast(rows[:, 1, :], B), ADD).then_inc(s_y1, 1)
            ch.leave(G)
            with pool.Fori(0, G) as g:
                ch.enter(g, 3 * B)
                for b in range(B):
                    hold(pool, s_we, B * g + b + 1, s_passed_pool)
                    e = SE[:, b % 4]
                    ch.done(pool.tensor_tensor(e[:, 0:4, :], e[:, 0:4, :], e[:, 4:8, :], ADD))
                    ch.wait()
                    ch.done(pool.tensor_tensor(e[:, 0:2, :], e[:, 0:2, :], e[:, 2:4, :], ADD))
                    ch.wait()
                    ch.done(pool.tensor_tensor(e[:, 0, :], e[:, 0, :], e[:, 1, :], ADD))
                    ch.wait()
                    pool.tensor_tensor(A[:, g, b, :], A[:, g, b, :], e[:, 0, :], ADD).then_inc(s_moe, 1)
            ch.leave(G)
            with pool.Fori(0, G) as g:
                hold(pool, s_n4, g + 1, s_passed_pool)
                ch.enter(g, 1)
                ch.done(pool.tensor_tensor(A[:, g], A[:, g], bcast(rows[:, 2, :], B), MUL))
                ch.wait()
                pool.tensor_tensor(A[:, g], A[:, g], bcast(rows[:, 3, :], B), ADD).then_inc(s_aff, 1)
            ch.leave(G)
            with pool.Fori(0, G) as g:
                hold(pool, s_n5, g + 1, s_passed_pool)
                pool.tensor_tensor(same(A[:, g]), same(A[:, g]), same(X[:, g]), ADD).then_inc(s_y2, 1)

        def back_end_pe(pe):
            pe.wait_ge(s_pve, NQ)
            pe.wait_ge(s_bc, 16 * 8)
            for c in range(FC):
                mm = pe.transpose(ps[:, 4, c * E:(c + 1) * E], b1_sb[:, c * P:(c + 1) * P], ident[0:E, 0:E])
            mm.then_inc(s_b1t, 1)
            pe.wait_ge(s_w1, 16)
            pe.wait_ge(s_w2, 16)

            def turn_w1(e):
                if e >= 2:
                    pe.wait_ge(s_w1c, e - 1)
                for c in range(FC):
                    mm = pe.transpose(ps[:, e % 2, c * P:(c + 1) * P], w1_sb[:, e, c * P:(c + 1) * P], ident[:])
                mm.then_inc(s_w1t, 1)

            turn_w1(0)
            pe.wait_ge(s_b1c, 1)
            for e in range(E):
                if e + 1 < E:
                    turn_w1(e + 1)
                pe.wait_ge(s_w1c, e + 1)
                lo = (e % 4) * D
                for c in range(FC):
                    pe.matmul(ps[:, 2 + e // 4, lo:lo + D], w1T[:, e % 2, c, :], w2_sb[:, e, c, :],
                              start=(c == 0), stop=(c == FC - 1))
                for c in range(FC):
                    mm = pe.matmul(ps[0:1, 5 + e // 4, lo:lo + D], b1T[:, c, e:e + 1], w2_sb[:, e, c, :],
                                   start=(c == 0), stop=(c == FC - 1))
            mm.then_inc(s_W, 1)

            def turn(src, banks, ready, done):
                for b in range(B):
                    mm = pe.transpose(ps[:, banks + b // 4, (b % 4) * P:(b % 4 + 1) * P], src[:, b, :], ident[:])
                mm.then_inc(done, 1)

            for g in range(G):
                pe.wait_ge(s_n2, g + 1)
                if g == 0:
                    pe.wait_ge(s_Wc, 1)
                    pe.wait_ge(s_crow, 1)
                else:
                    pe.wait_ge(s_yt, 2 * g)
                turn(A[:, g], 0, None, s_t)
                pe.wait_ge(s_yt, 2 * g + 2)
                for j, first in ((3, 2), (4, 4)):
                    if g >= 1:
                        pe.wait_ge(s_qkv, 3 * (g - 1) + j - 2)
                    for half in range(2):
                        mm = pe.matmul(ps[:, first + half, :], wT[:, j, :], same(YT[:, g])[:, half * 512:half * 512 + 512],
                                       start=True, stop=True)
                    mm.then_inc(s_pj, 1)
                if g >= 1:
                    pe.wait_ge(s_qkv, 3 * g)
                for t in range(NT):
                    mm = pe.matmul(ps[:, 6 + t // 4, (t % 4) * P:(t % 4 + 1) * P], YT[:, g, t, :],
                                   wT[:, 5, :], start=True, stop=True)
                mm.then_inc(s_pj, 1)

            def scores2(q):
                g, half = q // QPG, q % QPG
                if q >= 1:
                    pe.wait_ge(s_msk, q)
                for t in range(4):
                    for h in range(NH2):
                        rows_h = slice(HD2 * h, HD2 * h + HD2)
                        mm = pe.matmul(ps[:, h, t * P:(t + 1) * P], QF[rows_h, g, 4 * half + t, :],
                                       KF[rows_h, g, 4 * half + t, :], start=True, stop=True)
                mm.then_inc(s_s2, 1)

            pe.wait_ge(s_qkv, 3 * G)
            scores2(0)
            for q in range(2 * G):
                g, half = q // QPG, q % QPG
                if q + 1 < 2 * G:
                    scores2(q + 1)
                pe.wait_ge(s_ex, NH2 * (q + 1))
                for pair in range(2):
                    if q + pair >= 1:
                        pe.wait_ge(s_et, 2 * q + pair)
                    for k in range(8):
                        mm = pe.transpose(ps[:, 4 + k // 4, (k % 4) * P:(k % 4 + 1) * P],
                                          EX[:, half, 8 * pair + k, :], ident[:])
                    mm.then_inc(s_ext, 1)
                pe.wait_ge(s_et, 2 * q + 2)
                if q >= 2:
                    pe.wait_ge(s_ot, q - 1)
                for t in range(4):
                    for h in range(NH2):
                        mm = pe.matmul(ps[HD2 * h:HD2 * h + HD2, 6 + half, t * P:(t + 1) * P],
                                       VT[:, g, 4 * half + t, HD2 * h:HD2 * h + HD2], ET[:, half, 4 * h + t, :],
                                       start=True, stop=True)
                mm.then_inc(s_av, 1)
            pe.wait_ge(s_ot, 2 * G)
            pe.wait_ge(s_msk, 2 * G)
            for g in range(G):
                for b in range(B):
                    mm = pe.matmul(ps[:, 2 * g + b // 4, (b % 4) * P:(b % 4 + 1) * P], OT[:, g, b, :], wT[:, 6, :],
                                   start=True, stop=True)
                mm.then_inc(s_op, 1)
            for g in range(G):
                pe.wait_ge(s_y1, g + 1)
                turn(A[:, g], 2 * g, None, s_t)
            for g in range(G):
                pe.wait_ge(s_yt, 2 * G + 2 * g + 2)
                for b in range(B):
                    col = (g * B + b) * E
                    mm = pe.matmul(ps[:, 0, col:col + E], YT[:, g, b, :], wg_sb[:], start=True, stop=True)
            mm.then_inc(s_lg, 1)
            pe.wait_ge(s_oh, 1)
            pe.matmul(ps[:, 1, 0:T * E], upper[:], mask1[:], start=True, stop=True)
            pe.matmul(ps[:, 2, 0:T * E], all_ones[:], mask1[:], start=True, stop=True).then_inc(s_cnt, 1)
            pe.wait_ge(s_cl, 16)
            for t in range(T):
                bank = 2 * ((t + 2) % 4)
                if t == 2:
                    pe.wait_ge(s_gate, 1)
                if t >= 4:
                    pe.wait_ge(s_we, t - 3)
                for half in range(2):
                    pe.matmul(ps[:, bank + half, :], ones_stack[:], c_stack[:, half * 512:half * 512 + 512],
                              start=True, stop=False)
                    mm = pe.matmul(ps[:, bank + half, :], YT[:, t // B, t % B, :],
                                   W[:].rearrange("p e d -> p (e d)")[:, half * 512:half * 512 + 512],
                                   start=False, stop=True)
                mm.then_inc(s_xp, 1)

        def back_end_act(act):
            act.wait_ge(s_b1t, 1)
            act.copy(b1T[:].rearrange("p c e -> p (c e)"), ps[:, 4, 0:FC * E]).then_inc(s_b1c, 1)
            for e in range(E):
                act.wait_ge(s_w1t, e + 1)
                act.copy(w1T[:, e % 2], ps[:, e % 2, :]).then_inc(s_w1c, 1)
                if e % 2:
                    root(act, G + e // 2)
            act.wait_ge(s_W, 1)
            act.copy(W[:].rearrange("p e d -> p (e d)"), ps[:, 2:4, :].rearrange("p a b -> p (a b)")).then_inc(s_Wc, 1)
            for g in range(G):
                root(act, 2 * G + g)
            with act.Fori(0, G) as g:
                act.wait_ge(s_t, g + 1)
                for half in range(2):
                    act.copy(YT_tiles[:, g, :, 4 * half:4 * half + 4, :].rearrange("p t b n -> p b t n"),
                             ps[:, half, :].rearrange("p (b t n) -> p b t n", b=4, n=16)).then_inc(s_yt, 1)
                for j, dst in ((0, QF), (1, KF)):
                    act.wait_ge(s_pj, 3 * g + j + 1)
                    act.activation(same(dst[:, g]), ps[:, 2 + 2 * j:4 + 2 * j, :].rearrange("p a b -> p (a b)"),
                                   ACT.Identity, bias=bias_col[:, 3 + j:4 + j]).then_inc(s_qkv, 1)
                act.wait_ge(s_pj, 3 * g + 3)
                act.copy(same(VT[:, g]), ps[:, 6:8, :].rearrange("p a b -> p (a b)")).then_inc(s_qkv, 1)
            def softmax_exp(q):
                act.wait_ge(s_sub, q + 1)
                act.activation(PC[:, q].rearrange("p a b -> p (a b)"), SC[:, q].rearrange("p a b -> p (a b)"),
                               ACT.Exp, scale=1.0 / math.sqrt(HD2)).then_inc(s_e2, 1)

            softmax_exp(0)
            for q in range(2 * G):
                g, half = q // QPG, q % QPG
                if q + 1 < 2 * G:
                    softmax_exp(q + 1)
                for pair in range(2):
                    act.wait_ge(s_ext, 2 * q + pair + 1)
                    act.copy(ET[:, half, 8 * pair:8 * pair + 8, :].rearrange("p a b -> p (a b)"),
                             ps[:, 4:6, :].rearrange("p a b -> p (a b)")).then_inc(s_et, 1)
                act.wait_ge(s_av, q + 1)
                for t in range(4):
                    n0 = 16 * (4 * half + t)
                    ins = act.activation(OT[:, g, :, n0:n0 + 16], ps[:, 6 + half, t * P:(t + 1) * P].rearrange("p (l n) -> p l n", n=16),
                                         ACT.Identity, bias=bias_col[:, 5:6])
                ins.then_inc(s_ot, 1)
            for g in range(G):
                root(act, 3 * G + g)
            for g in range(G):
                act.wait_ge(s_t, G + g + 1)
                for half in range(2):
                    act.copy(same(YT[:, g, 4 * half:4 * half + 4]), ps[:, 2 * g + half, :]).then_inc(s_yt, 1)
            act.wait_ge(s_oh, 1)
            act.activation(gexp[:], lsub[:], ACT.Exp).then_inc(s_ge, 1)
            with act.Fori(4 * G, 6 * G) as k:
                root(act, k)

        def back_end_dve(dve, ch):
            for g in range(G):
                dve.wait_ge(s_al[g], 32)
                ch.done(dve.reciprocal(same(DEN[:, g % 2]), same(DEN[:, g % 2])))
                ch.wait()
                dve.tensor_tensor(same(A[:, g]), same(A[:, g]), same(DEN[:, g % 2]), MUL).then_inc(s_rec, 1)
            with dve.Fori(0, G) as g:
                ch.enter(g, NORM)
                dve.wait_ge(s_r1, g + 1)
                norm(dve, ch, g + G, A[:, g], A[:, g]).then_inc(s_n1, 1)
            ch.leave(G)
            dve.wait_ge(s_W, 1)
            dve.wait_ge(s_b2, 16)
            dve.tensor_tensor(c_row, ps[0:1, 5:7, :].rearrange("p a b -> p (a b)"), b2_sb, ADD).then_inc(s_crow, 1)
            with dve.Fori(0, G) as g:
                ch.enter(g, NORM)
                dve.wait_ge(s_r2, g + 1)
                norm(dve, ch, g + 2 * G, X[:, g], A[:, g]).then_inc(s_n2, 1)
            ch.leave(G)

            def compact(q):
                hold(dve, s_s2, q + 1, s_passed_dve)
                dve.tensor_tensor(SM[:], ps[:, 0:4, :].rearrange("p a (t f) -> p (a t) f", f=P),
                                  bcast(same_row[:], 16), MUL).then_inc(s_msk, 1)
                hold(dve, s_msk, q + 1, s_passed_dve)
                ch.done(dve.tensor_reduce(SC[:, q], SM[:].rearrange("p a (m n) -> p a m n", n=16), AX.X, ADD))
                ch.wait()
                ch.done(dve.tensor_reduce(mx[:, q], SC[:, q], AX.X, MAX))
                ch.wait()
                dve.tensor_tensor(SC[:, q], SC[:, q], mx[:, q].rearrange("p (a o) -> p a o", o=1).broadcast_to([P, 16, B]),
                                  SUB).then_inc(s_sub, 1)

            def normalise(q):
                hold(dve, s_e2, q + 1, s_passed_dve)
                ch.done(dve.tensor_reduce(sm2[:, q], PC[:, q], AX.X, ADD))
                ch.wait()
                ch.done(dve.reciprocal(sm2[:, q], sm2[:, q]))
                ch.wait()
                dve.tensor_tensor(PC[:, q], PC[:, q], sm2[:, q].rearrange("p (a o) -> p a o", o=1).broadcast_to([P, 16, B]),
                                  MUL).then_inc(s_soft, 1)

            with dve.Fori(0, 2 * G) as q:
                ch.enter(q, 4)
                compact(q)
                normalise(q)
            ch.leave(2 * G)
            for g in range(G):
                dve.wait_ge(s_op, g + 1)
                ch.done(dve.tensor_tensor(same(A[:, g]), ps[:, 2 * g:2 * g + 2, :].rearrange("p a b -> p (a b)"), same(XN[:, g]), ADD))
                ch.wait()
                norm(dve, ch, g + 3 * G, A[:, g], A[:, g]).then_inc(s_n3, 1)
            dve.wait_ge(s_lg, 1)
            L = ps[:, 0, 0:T * E].rearrange("p (t e) -> p t e", e=E)
            over_e = lambda v: v[:].rearrange("p (t o) -> p t o", o=1).broadcast_to([P, T, E])
            ch.done(dve.tensor_reduce(lmax[:], L, AX.X, MAX))
            ch.wait()
            ch.done(dve.tensor_tensor(lsub[:].rearrange("p (t e) -> p t e", e=E), L, over_e(lmax), SUB))
            ch.wait()
            ch.done(dve.tensor_scalar(eq[:], lsub[:], 0.0, None, ALU.is_equal))
            ch.wait()
            ch.done(dve.tensor_tensor_scan(cum[:], first_e[:], eq[:], 0.0, MUL, ADD))
            ch.wait()
            dve.scalar_tensor_tensor(mask1[:], cum[:], 1.0, eq[:], ALU.is_equal, MUL).then_inc(s_oh, 1)
            dve.wait_ge(s_ge, 1)
            ch.done(dve.tensor_reduce(gate[:], gexp[:].rearrange("p (t e) -> p t e", e=E), AX.X, ADD))
            ch.wait()
            ch.done(dve.reciprocal(gate[:], gate[:]))
            dve.wait_ge(s_cnt, 1)
            tot_src = ps[:, 2, 0:T * E].rearrange("p (g b e) -> p e b g", g=G, e=E)
            for e in range(E):
                ins = dve.tensor_copy(tot[:, e], tot_src[:, e])
            ch.done(ins)
            ch.wait()
            flat = lambda v: v[:].rearrange("p e b g -> p (e b g)")
            ch.done(dve.tensor_tensor_scan(flat(incl), first_t[:], flat(tot), 0.0, MUL, ADD))
            ch.wait()
            ch.done(dve.tensor_tensor(flat(incl), flat(incl), flat(tot), SUB))
            ch.wait()
            for g in range(G):
                ins = dve.tensor_tensor(place[:].rearrange("p (g b e) -> p g b e", g=G, e=E)[:, g],
                                        ps[:, 1, 0:T * E].rearrange("p (g b e) -> p g b e", g=G, e=E)[:, g],
                                        incl[:, :, :, g].rearrange("p e b -> p b e"), ADD)
            ch.done(ins)
            ch.wait()
            ch.done(dve.scalar_tensor_tensor(place[:], place[:], CAP + 0.5, mask1[:], ALU.is_lt, MUL))
            ch.wait()
            dve.tensor_tensor(weight[:].rearrange("p (t e) -> p t e", e=E), place[:].rearrange("p (t e) -> p t e", e=E),
                              over_e(gate), MUL).then_inc(s_gate, 1)
            dve.wait_ge(s_gate, 1)
            for t in range(T):
                dve.wait_ge(s_xp, t + 1)
                if t >= 4:
                    dve.wait_ge(s_moe, t - 3)
                bank = 2 * ((t + 2) % 4)
                dve.tensor_tensor(SE[:, t % 4], ps[:, bank:bank + 2, :].rearrange("p a (e d) -> p (a e) d", d=D),
                                  weight[:, t * E:(t + 1) * E].rearrange("p (e o) -> p e o", o=1).broadcast_to([P, E, D]),
                                  MUL).then_inc(s_we, 1)
            with dve.Fori(0, G) as g:
                ch.enter(g, NORM)
                dve.wait_ge(s_moe, B * g + B)
                norm(dve, ch, g + 4 * G, A[:, g], A[:, g]).then_inc(s_n4, 1)
            ch.leave(G)
            with dve.Fori(0, G) as g:
                ch.enter(g, NORM)
                dve.wait_ge(s_aff, g + 1)
                norm(dve, ch, g + 5 * G, A[:, g], A[:, g]).then_inc(s_n5, 1)
            ch.leave(G)

        block = ctx.enter_context(nc.Block())

        @block.sync
        def _(sp):
            for g in range(G):
                sp.dma_start(X[:, g], x_tok[g]).then_inc(s_x[g], 16)
            sp.dma_start(bias_col[:, 0:1], bq.rearrange("(p o) -> p o", o=1)).then_inc(s_b, 16)
            sp.dma_start(bias_col[:, 1:2], bk.rearrange("(p o) -> p o", o=1)).then_inc(s_b, 16)
            sp.dma_start(bias_col[:, 2:3], bv.rearrange("(p o) -> p o", o=1)).then_inc(s_b, 16)
            for j in range(3):
                sp.dma_start(bias_col[:, 3 + j:4 + j], bin_[j * P:(j + 1) * P].rearrange("(p o) -> p o", o=1)).then_inc(s_b, 16)
            sp.wait_ge(s_ks, 1)
            for r, (_, part) in enumerate(PRODUCTS):
                sp.dma_start(k_dram[:, r * DH:(r + 1) * DH, :].rearrange("h d t -> h d t"),
                             k_parts[:, part, :]).then_inc(s_kst, 16)
            for half in range(2):
                sp.wait_ge(s_qs, QB * (half + 1))
                cols = slice(half * QB * S, (half + 1) * QB * S)
                sp.dma_start(q_dram[:, :, cols].rearrange("r p s -> p r s"), q_parts[:, :, cols]).then_inc(s_qst, 16)
            sp.wait_ge(s_kst, 16 * len(PRODUCTS))
            sp.wait_ge(s_qst, 32)

            sp.wait_ge(s_qp, B)

            def load_stack(head, half, buf):
                lo = head * DH
                qs = slice(half * QB * S, (half + 1) * QB * S)
                r = 0
                for n in (3, 2, 1):
                    src = q_dram[0:n, bass_ds(lo, DH), qs]
                    sp.dma_start(q_stack[r * DH:(r + n) * DH, buf, :], src).then_inc(s_ql[buf], 16)
                    r += n
                src = k_dram[bass_ds(head, 1), :, :].rearrange("o r t -> (o r) t")
                sp.dma_start(k_plain[0:KROWS, buf, :], src).then_inc(s_ql[buf], 16)
                sp.dma_start(k_shift[0:KROWS, buf, :], src).then_inc(s_ql[buf], 16)

            def load_shift(par, buf):
                sp.dma_start(q_stack[SHIFT_ROW:SHIFT_ROW + PARTS, buf, :].rearrange("r (c s) -> r c s", s=P),
                             max_turned[:, par, :]).then_inc(s_shift, 16)

            def store_attended(head, half, par):
                for bb in range(QB):
                    b = half * QB + bb
                    sp.dma_start(a_dram[:, b, bass_ds(head * DH, DH), :],
                                 attended[32 * bb:32 * bb + 2 * DH, par, :]).then_inc(s_ast[par], 16)

            sp.wait_ge(s_const, 8)
            for kappa in range(3):
                load_stack(kappa // 2, kappa % 2, kappa)
            sp.wait_ge(s_free, 8 + 3)
            load_shift(0, 0)
            sp.dma_start(w1_sb, w1.rearrange("e p f -> p e f")).then_inc(s_w1, 16)
            sp.dma_start(w2_sb, w2.rearrange("e (c p) d -> p e c d", p=P)).then_inc(s_w2, 16)
            sp.dma_start(b2_sb, b2.rearrange("(o e) d -> o (e d)", o=1)).then_inc(s_b2, 16)

            def slot(i, kk, last):
                kappa = 4 * i + kk
                if not last or kk == 0:
                    if not (isinstance(i, int) and kappa == 0):
                        sp.wait_ge(s_sc, 64 * i + 16 * kk)
                    load_stack(2 * i + (kk + 3) // 2, (kk + 3) % 2, (kk + 3) % 4)
                if not (isinstance(i, int) and kappa == 0):
                    sp.wait_ge(s_pve, 4 * i + kk)
                    store_attended(2 * i + (kk - 1) // 2, (kk - 1) % 2, (kk - 1) % 2)
                if not last or kk < 3:
                    sp.wait_ge(s_free, 36 * i + 17 + 9 * kk + (1 if last and kk == 2 else 3))
                    load_shift((kk + 1) % 2, (kk + 1) % 4)

            for kk in range(4):
                slot(0, kk, False)
            with sp.Fori(1, IT - 1) as i:
                for kk in range(4):
                    slot(i, kk, False)
            for kk in range(4):
                slot(IT - 1, kk, True)
            sp.wait_ge(s_pve, NQ)
            store_attended(NH - 1, 1, 1)
            for par in range(2):
                sp.wait_ge(s_ast[par], 16 * QB * NQ // 2)
            back_end_sp(sp)

        @block.gpsimd
        def _(pool):
            ch = Chain(pool, s_pc, s_passed_pool)
            ch.done(pool.memset(ident[:], 0.0))
            ch.done(pool.memset(upper[:], 1.0))
            ch.done(pool.memset(same_row[:], 0.0))
            pool.memset(all_ones[:], 1.0).then_inc(s_const, 1)
            pool.memset(ones_stack[:], 1.0).then_inc(s_const, 1)
            ch.wait()
            ch.done(pool.affine_select(out=ident[:], in_=ident[:], compare_op=ALU.not_equal, fill=1.0, base=0,
                                       pattern=[[-1, P]], channel_multiplier=1))
            pool.affine_select(out=upper[:], in_=upper[:], compare_op=ALU.is_ge, fill=0.0, base=0,
                               pattern=[[1, P]], channel_multiplier=-1).then_inc(s_const, 1)
            ch.wait()
            pool.tensor_copy(ident16[:], ident[:]).then_inc(s_const, 1)
            for m in range(-7, 8):
                ch.done(pool.affine_select(out=same_row[:], in_=same_row[:], compare_op=ALU.not_equal, fill=1.0,
                                           base=16 * m, pattern=[[-1, P]], channel_multiplier=1))
                ch.wait()
            pool.memset(v_heads[:], 0.0).then_inc(s_vset, 1)
            pool.wait_ge(s_vset, 1)
            pool.memset(v_heads[:, :, :, DH:2 * DH], 1.0).then_inc(s_vset, 1)
            pool.memset(q_stack, 0.0).then_inc(s_const, 1)
            pool.memset(k_plain, 0.0).then_inc(s_const, 1)
            ch.done(pool.memset(k_shift[:], 0.0))
            ch.wait()
            ch.done(pool.affine_select(out=k_shift[:], in_=k_shift[:], compare_op=ALU.is_gt, fill=-1.0, base=SHIFT_ROW,
                                       pattern=[[0, 4], [0, S]], channel_multiplier=-1))
            ch.wait()
            pool.affine_select(out=k_shift[:], in_=k_shift[:], compare_op=ALU.is_gt, fill=0.0, base=SHIFT_ROW + PARTS,
                               pattern=[[0, 4], [0, S]], channel_multiplier=-1).then_inc(s_const, 1)
            pool.memset(c_stack[:], 0.0).then_inc(s_const, 1)

            def split_max(count, par):
                hold(pool, s_free, count, s_passed_pool)
                m, r, parts = row_max[:, par], max_rest[:, par], max_parts[:, par]
                ch.done(pool.tensor_copy(parts[:, 0], m))
                ch.wait()
                ch.done(pool.tensor_tensor(r, m, parts[:, 0], SUB))
                ch.wait()
                ch.done(pool.tensor_copy(parts[:, 1], r))
                ch.wait()
                pool.tensor_tensor(parts[:, 2], r, parts[:, 1], SUB).then_inc(s_split, 1)

            def pick_v(head, par):
                pool.tensor_copy(v_head[:, par], v_heads[:, :, head, :]).then_inc(s_v, 1)

            ch.done(pool.memset(first_e[:], 1.0))
            ch.done(pool.memset(first_t[:], 1.0))
            ch.wait()
            pool.memset(first_e[:].rearrange("p (t e) -> p t e", e=E)[:, :, 0:1], 0.0).then_inc(s_const, 1)
            pool.memset(first_t[:].rearrange("p (e t) -> p e t", t=T)[:, :, 0:1], 0.0).then_inc(s_const, 1)

            pool.wait_ge(s_vb, TC)
            pool.wait_ge(s_vset, 2)
            pick_v(0, 0)
            split_max(8, 0)

            def slot(i, kk, last):
                if not last or kk < 3:
                    split_max(36 * i + 9 * (kk + 1) + 8, (kk + 1) % 2)
                if kk % 2 == 0 and not (last and kk == 2):
                    if not (isinstance(i, int) and 4 * i + kk == 0):
                        hold(pool, s_pv, 4 * i + kk, s_passed_pool)
                    pick_v(2 * i + kk // 2 + 1, (kk // 2 + 1) % 2)

            for kk in range(4):
                slot(0, kk, False)
            with pool.Fori(1, IT - 1) as i:
                ch.enter(i - 1, 12)
                for kk in range(4):
                    slot(i, kk, False)
            ch.leave(IT - 2)
            for kk in range(4):
                slot(IT - 1, kk, True)
            back_end_pool(pool, ch)

        def ring(n):
            return ps[:, 2 * (n % 2):2 * (n % 2) + 2, :]

        col_bank = lambda u: 4 + u % 3
        PV = 7

        @block.tensor
        def _(pe):
            pe.wait_ge(s_const, 4)
            pe.wait_ge(s_w, 16 * 5)
            for j in range(7):
                mm = pe.transpose(ps[:, j // 4, (j % 4) * P:(j % 4 + 1) * P], w_in[:, j, :], ident[:])
            mm.then_inc(s_wt, 1)
            pe.wait_ge(s_kv, 32)
            for a in range(2):
                for c in range(TC):
                    mm = pe.transpose(ps[:, 2 + a, c * P:(c + 1) * P], kv_in[:, a, c, :], ident[:])
            mm.then_inc(s_kvt, 1)
            pe.wait_ge(s_wtc, 1)
            pe.wait_ge(s_kvtc, 1)
            pe.matmul(ps[:, 4, :], wT[:, 1, :], kvT[:, 0, :], start=True, stop=True).then_inc(s_kp, 1)
            for c in range(TC):
                mm = pe.matmul(ps[:, 5, c * P:(c + 1) * P], kvT[:, 1, c * P:(c + 1) * P], wT[:, 2, :],
                               start=True, stop=True)
            mm.then_inc(s_vp, 1)
            for g in range(G):
                pe.wait_ge(s_xn, g + 1)
                if g == 0:
                    pe.wait_ge(s_kpe, 1)
                    pe.wait_ge(s_vpe, 1)
                for b in range(B):
                    mm = pe.transpose(ps[:, b, g * P:(g + 1) * P], XN[:, g, b, :], ident[:])
                mm.then_inc(s_xt, 1)
            for b in range(B):
                pe.wait_ge(s_xtc, b + 1)
                pe.matmul(ps[:, b, :], wT[:, 0, :], featT[:, b, :], start=True, stop=True).then_inc(s_qp, 1)

            def score_rows(n, quad_buf, bb, pair, waits):
                if waits is not None:
                    pe.wait_ge(s_free, waits)
                for j in range(2):
                    lo = bb * S + (2 * pair + j) * P
                    mm = pe.matmul(ring(n)[:, j, :], q_stack[:, quad_buf, lo:lo + P], k_plain[:, quad_buf, :],
                                   start=True, stop=True)
                mm.then_inc(s_full, 1)

            def turn_max(n, par, waits, split):
                pe.wait_ge(s_free, waits)
                hold(pe, s_split, split, s_passed_pe)
                dst = ps[0:PARTS * QB * TC, 2 * (n % 2), 0:P // 2].bitcast(BF16)
                pe.transpose(dst, max_parts[:, par].rearrange("p r c -> p (r c)"), ident16[:]).then_inc(s_full, 1)

            def score_columns(u, quad_buf, tc, bb, waits):
                if waits is not None:
                    pe.wait_ge(s_pr, waits)
                pe.matmul(ps[:, col_bank(u), :], k_shift[:, quad_buf, tc * P:(tc + 1) * P],
                          q_stack[:, quad_buf, bb * S:(bb + 1) * S], start=True, stop=True).then_inc(s_sc, 1)

            def multiply_v(par, head_par, tc):
                for bb in range(QB):
                    mm = pe.matmul(ps[32 * bb:32 * bb + 32, PV, :], v_head[:, head_par, tc, :],
                                   probs[:, par, bb, :], start=(tc == 0), stop=(tc == TC - 1))
                if tc == TC - 1:
                    mm.then_inc(s_pv, 1)

            pe.wait_ge(s_ql[0], 80)
            pe.wait_ge(s_qe, B)
            n = 0
            for bb in range(QB):
                for pair in range(2):
                    score_rows(n, 0, bb, pair, n - 1 if n >= 2 else None)
                    n += 1
            pe.wait_ge(s_ql[1], 80)
            for bb in range(QB):
                for pair in range(2):
                    score_rows(n, 1, bb, pair, n - 1)
                    n += 1
                if bb == 0:
                    turn_max(n, 0, n - 1, 1)
                    n += 1
            assert n == 17
            pe.wait_ge(s_shift, 16)
            for bb in range(QB):
                score_columns(bb, 0, 0, bb, None if bb < 3 else 1)

            def slot(i, kk, last):
                n0 = 17 + 9 * kk
                rows_too = not (last and kk >= 2)
                n = n0
                for tc in range(TC):
                    final = last and kk == 3 and tc == TC - 1
                    for pair in range(2):
                        if rows_too:
                            if tc == 0 and pair == 0:
                                pe.wait_ge(s_ql[(kk + 2) % 4], 80 * (i + (kk + 2) // 4 + 1))
                            score_rows(n, (kk + 2) % 4, tc, pair, 36 * i + n - 1)
                            n += 1
                        if final:
                            continue
                        if tc == TC - 1 and pair == 0:
                            pe.wait_ge(s_shift, 64 * i + 16 * (kk + 2))
                        for bb in (2 * pair, 2 * pair + 1):
                            u = 16 * kk + 4 * (tc + 1) + bb
                            before = u - 3 + {64: 2, 65: -1, 66: -1}.get(u, 0)
                            score_columns(u % 64, (kk + 1) % 4 if tc == TC - 1 else kk % 4, (tc + 1) % TC, bb,
                                          64 * i + before + 1)
                    if tc == 0 and not (last and kk == 3):
                        turn_max(n, (kk + 1) % 2, 36 * i + n - 1, 4 * i + kk + 2)
                        n += 1
                    if tc == 0:
                        pe.wait_ge(s_v, 2 * i + kk // 2 + 1)
                        if not (isinstance(i, int) and 4 * i + kk == 0):
                            pe.wait_ge(s_pve, 4 * i + kk)
                    pe.wait_ge(s_pr, 64 * i + 16 * kk + 4 * tc + 4)
                    multiply_v(tc % 2, (kk // 2) % 2, tc)

            for kk in range(4):
                slot(0, kk, False)
            with pe.Fori(1, IT - 1) as i:
                for kk in range(4):
                    slot(i, kk, False)
            for kk in range(4):
                slot(IT - 1, kk, True)
            back_end_pe(pe)

        @block.scalar
        def _(act):
            w_row = [wq, wk, wv]
            for j in range(3):
                act.dma_start(w_in[:, j, :], w_row[j]).then_inc(s_w, 16)
            act.dma_start(kv_in[:, 0], keys.rearrange("o (c p) f -> p (o c) f", p=P)).then_inc(s_kv, 16)
            act.dma_start(kv_in[:, 1], values.rearrange("o (c p) f -> p (o c) f", p=P)).then_inc(s_kv, 16)
            act.dma_start(w_in[:, 3:6, :], win.rearrange("(j p) f -> p j f", p=P)).then_inc(s_w, 16)
            act.dma_start(w_in[:, 6, :], wout).then_inc(s_w, 16)
            act.dma_start(bv_row[:], bv.rearrange("(o f) -> o f", o=1).broadcast_to([P, D])).then_inc(s_bc, 16)
            for j, r in enumerate((ln1g, ln1b, ln2g, ln2b, bout)):
                act.dma_start(rows[:, j, :], r.rearrange("(o f) -> o f", o=1).broadcast_to([P, D])).then_inc(s_bc, 16)
            act.dma_start(wg_sb[:], wg).then_inc(s_bc, 16)
            act.dma_start(b1_sb[:], b1).then_inc(s_bc, 16)
            root(act, 0)
            root(act, 1)
            act.wait_ge(s_wt, 1)
            act.copy(wT[:].rearrange("p j f -> p (j f)"),
                     ps[:, 0:2, :].rearrange("p a b -> p (a b)")[:, 0:7 * P]).then_inc(s_wtc, 1)
            act.wait_ge(s_kvt, 1)
            act.copy(kvT, ps[:, 2:4, :]).then_inc(s_kvtc, 1)
            act.wait_ge(s_b, 96)
            act.wait_ge(s_kp, 1)
            act.activation(k_rest[:, 0], ps[:, 4, :], ACT.Relu, bias=bias_col[:, 1:2]).then_inc(s_kpe, 1)
            root(act, 2)
            root(act, 3)
            for b in range(B):
                if b == 0:
                    act.wait_ge(s_xt, G)
                act.copy(featT[:, b], ps[:, b, :]).then_inc(s_xtc, 1)
                if b >= 1:
                    project_q(act, b - 1)
            project_q(act, B - 1)

            def exps(par, tc, u, waits):
                for bb in range(QB):
                    act.wait_ge(s_sc, waits + bb + 1)
                    act.activation(probs[:, par, bb, :], ps[:, col_bank((u + bb) % 64), :], ACT.Exp,
                                   scale=1.0 / math.sqrt(DH)).then_inc(s_pr, 1)

            exps(0, 0, 0, 0)

            def slot(i, kk, last):
                for tc in range(TC):
                    u = 16 * kk + 4 * (tc + 1)
                    if not (last and kk == 3 and tc == TC - 1):
                        exps((tc + 1) % 2, (tc + 1) % TC, u, 64 * i + u)
                act.wait_ge(s_pv, 4 * i + kk + 1)
                if not (isinstance(i, int) and 4 * i + kk < 2):
                    act.wait_ge(s_ast[kk % 2], 16 * QB * (2 * i + kk // 2))
                act.copy(attended[:, kk % 2, :], ps[:, PV, :]).then_inc(s_pve, 1)

            for kk in range(4):
                slot(0, kk, False)
            with act.Fori(1, IT - 1) as i:
                for kk in range(4):
                    slot(i, kk, False)
            for kk in range(4):
                slot(IT - 1, kk, True)
            back_end_act(act)


        @block.vector
        def _(dve):
            ch = Chain(dve, s_dc, s_passed_dve)
            for g in range(2):
                dve.wait_ge(s_x[g], 16)
                norm(dve, ch, g, X[:, g], XN[:, g]).then_inc(s_xn, 1)
            dve.wait_ge(s_kpe, 1)
            ch.done(dve.tensor_copy(k_parts[:, 0], k_rest[:, 0]))
            ch.wait()
            ch.done(dve.tensor_tensor(k_rest[:, 1], k_rest[:, 0], k_parts[:, 0], SUB))
            ch.wait()
            ch.done(dve.tensor_copy(k_parts[:, 1], k_rest[:, 1]))
            ch.wait()
            dve.tensor_tensor(k_parts[:, 2], k_rest[:, 1], k_parts[:, 1], SUB).then_inc(s_ks, 1)
            dve.wait_ge(s_vp, 1)
            dve.wait_ge(s_bc, 16 * 8)
            dve.tensor_tensor(v_tmp[:], ps[:, 5, :].rearrange("p (c f) -> p c f", c=TC),
                              bv_row[:].rearrange("p (o f) -> p o f", o=1).broadcast_to([P, TC, D]), ADD).then_inc(s_vpe, 1)
            dve.wait_ge(s_vpe, 1)
            dve.wait_ge(s_vset, 2)
            for c in range(TC):
                dve.tensor_scalar(v_heads[:, c, :, 0:DH], v_tmp[:, c, :].rearrange("p (h d) -> p h d", d=DH),
                                  0.0, None, MAX).then_inc(s_vb, 1)
            for g in range(2, G):
                dve.wait_ge(s_x[g], 16)
                norm(dve, ch, g, X[:, g], XN[:, g]).then_inc(s_xn, 1)
            for b in range(B):
                cols = slice(b * S, (b + 1) * S)
                dve.wait_ge(s_qe, b + 1)
                ch.done(dve.tensor_tensor(rest[:, b % 2], qf[:, b % 2], q_parts[:, 0, cols], SUB))
                ch.wait()
                ch.done(dve.tensor_copy(q_parts[:, 1, cols], rest[:, b % 2]))
                ch.wait()
                dve.tensor_tensor(q_parts[:, 2, cols], rest[:, b % 2], q_parts[:, 1, cols], SUB).then_inc(s_qs, 1)

            def reduce_rows(n, par, bb, pair, waits):
                dve.wait_ge(s_full, waits)
                c = bb * TC + 2 * pair
                dve.tensor_reduce(row_max[:, par, c:c + 2], ring(n), AX.X, MAX).then_inc(s_free, 1)

            def copy_turned(n, par, waits):
                dve.wait_ge(s_full, waits)
                src = ps[0:PARTS * QB * TC, 2 * (n % 2), 0:P // 2].bitcast(BF16)
                dve.tensor_copy(max_turned[:, par, :], src).then_inc(s_free, 1)

            n = 0
            for bb in range(QB):
                for pair in range(2):
                    reduce_rows(n, 0, bb, pair, n + 1)
                    n += 1
            for bb in range(QB):
                for pair in range(2):
                    reduce_rows(n, 1, bb, pair, n + 1)
                    n += 1
                if bb == 0:
                    copy_turned(n, 0, n + 1)
                    n += 1

            def slot(i, kk, last):
                n = 17 + 9 * kk
                for tc in range(TC):
                    if not (last and kk >= 2):
                        if tc == 0:
                            dve.wait_ge(s_split, 4 * i + kk + 1)
                        for pair in range(2):
                            reduce_rows(n, kk % 2, tc, pair, 36 * i + n + 1)
                            n += 1
                    if tc == 0 and not (last and kk == 3):
                        if not (isinstance(i, int) and 4 * i + kk == 0):
                            dve.wait_ge(s_shift, 64 * i + 16 * kk)
                        copy_turned(n, (kk + 1) % 2, 36 * i + n + 1)
                        n += 1

            for kk in range(4):
                slot(0, kk, False)
            with dve.Fori(1, IT - 1) as i:
                for kk in range(4):
                    slot(i, kk, False)
            for kk in range(4):
                slot(IT - 1, kk, True)
            back_end_dve(dve, ch)



NAMES = ["L0_attn_queries", "L0_attn_keys", "L0_attn_values", "L0_attn_Wq_w", "L0_attn_Wq_b", "L0_attn_Wk_w",
         "L0_attn_Wk_b", "L0_attn_Wv_w", "L0_attn_Wv_b", "L0_ffn_in_proj_w", "L0_ffn_in_proj_b", "L0_ffn_out_proj_w",
         "L0_ffn_out_proj_b", "L0_ffn_ln1_g", "L0_ffn_ln1_b", "L0_ffn_ln2_g", "L0_ffn_ln2_b", "L0_ffn_wg",
         "L0_ffn_w1", "L0_ffn_b1", "L0_ffn_w2", "L0_ffn_b2"]


def kernel(**inputs):
    import concourse.bacc as bacc
    from concourse import mybir
    from concourse.bass_utils import run_bass_kernel_spmd

    nc = bacc.Bacc("TRN2", target_bir_lowering=False, num_devices=1)
    arrays, args = {}, []
    for name in NAMES:
        a = np.ascontiguousarray(inputs[name])
        arrays[f"in_{name}"] = a
        args.append(nc.dram_tensor(f"in_{name}", a.shape, mybir.dt.from_np(a.dtype), kind="ExternalInput").ap())
    args.append(nc.dram_tensor("out_0", (B, S, D), mybir.dt.float32, kind="ExternalOutput").ap())
    build(nc, *args)
    r = run_bass_kernel_spmd(nc, [arrays], core_ids=[0])
    return r.results[0]["out_0"]
```

```python
import math

import numpy as np

P = 128
D = 128
B = 8
S = 512
G = S // P
NH, DH = 16, 8
NH2, HD2 = 4, 32
E, FF = 8, 512
E2 = E // 2
FC = FF // P
CAP = B * S // E
T = G * B
QB = 4
NQ = NH * B // QB
TC = S // P
PARTS = 3
PRODUCTS = [(0, 0), (1, 0), (2, 0), (0, 1), (1, 1), (0, 2)]
KROWS = DH * len(PRODUCTS)
SHIFT_ROW = KROWS
KPAD = 96
EPS = 1e-5
IT = NQ // 4
NT = P // 16
QPG = 2


def hold(engine, sem, value, passed):
    engine.wait_ge(sem, value)
    engine.sem_inc(passed, 1)


class Chain:

    def __init__(self, engine, sem, passed):
        self.engine, self.sem, self.passed, self.base, self.n = engine, sem, passed, 0, 0

    def done(self, ins):
        ins.then_inc(self.sem, 1)
        self.n += 1
        return ins

    def wait(self):
        if isinstance(self.base, int):
            self.engine.wait_ge(self.sem, self.base + self.n)
        else:
            hold(self.engine, self.sem, self.base + self.n, self.passed)

    def enter(self, i, per):
        self.fixed, self.per, self.base, self.n = self.base + self.n, per, i * per + (self.base + self.n), 0

    def leave(self, times):
        assert self.n == self.per, (self.n, self.per)
        self.base, self.n = self.fixed + times * self.per, 0


def build(nc, x, keys, values, wq, bq, wk, bk, wv, bv, win, bin_, wout, bout,
          ln1g, ln1b, ln2g, ln2b, wg, w1, b1, w2, b2, out):
    from contextlib import ExitStack
    from concourse import mybir
    from concourse.bass import ds as bass_ds

    F32, BF16 = mybir.dt.float32, mybir.dt.bfloat16
    ALU, ACT, AX = mybir.AluOpType, mybir.ActivationFunctionType, mybir.AxisListType
    ADD, SUB, MUL, MAX = ALU.add, ALU.subtract, ALU.mult, ALU.max

    with ExitStack() as ctx:
        def sb(name, shape, dt=F32):
            return ctx.enter_context(nc.sbuf_tensor(name, shape, dt))

        def sem(name):
            return ctx.enter_context(nc.semaphore(name))

        q_dram = nc.dram_tensor("q_parts_dram", (PARTS, P, B * S), BF16, kind="Internal").ap()
        k_dram = nc.dram_tensor("k_rows_dram", (NH, KROWS, S), BF16, kind="Internal").ap()
        a_dram = nc.dram_tensor("attended_dram", (B, NH, DH + 1, S), F32, kind="Internal").ap()
        inv_dram = nc.dram_tensor("inverses_dram", (NH // G, S // D, B, D), F32, kind="Internal").ap()

        ps = ctx.enter_context(nc.psum_tensor("ps", [P, 8, 512], F32))

        X = sb("X", [P, G, B, D])
        XN = sb("XN", [P, G, B, D])
        w_in = sb("w_in", [P, 7, D])
        wT = sb("wT", [P, 7, D])
        bias_col = sb("bias_col", [P, 6])
        bv_row = sb("bv_row", [P, D])
        rows = sb("rows", [P, 5, D])
        wg_sb = sb("wg_sb", [P, E])
        w1T = sb("w1T", [P, 2, FC, D])
        b1_sb = sb("b1_sb", [E, FF])
        b1T = sb("b1T", [P, FC, E, 32])
        W = sb("W", [P, E, D])
        b2_sb = sb("b2_sb", [P, 2, D])
        c_row = sb("c_row", [P, 2, D])
        c_rest = sb("c_rest", [P, 2, D])
        c_parts = sb("c_parts", [P, PARTS, 2, D], BF16)
        c_stack = sb("c_stack", [KPAD, E * D], BF16)
        ones_stack = sb("ones_stack", [KPAD, P], BF16)
        ident = sb("ident", [P, P])
        ident16 = sb("ident16", [P, P], BF16)
        upper = sb("upper", [P, P], BF16)
        all_ones = sb("all_ones", [P, P], BF16)
        same_row = sb("same_row", [P, P])
        first_e = sb("first_e", [P, T * E])
        first_t = sb("first_t", [P, T * E])

        space1, space2, space3 = sb("space1", [P, 4096]), sb("space2", [P, 6144]), sb("space3", [P, 4096])
        space4, space5, space6 = sb("space4", [P, 4096]), sb("space5", [P, 4096]), sb("space6", [P, 4096])
        space7, space8 = sb("space7", [P, 2048]), sb("space8", [P, 2048])

        def view(space, lo, dims, dt=F32, parts=P):
            n = int(np.prod(dims))
            words = n if dt == F32 else n // 2
            v = space[0:parts, lo:lo + words]
            if dt != F32:
                v = v.bitcast(dt)
            names = "abcd"[:len(dims)]
            if len(dims) == 1:
                return v
            return v.rearrange(f"p ({' '.join(names)}) -> p {' '.join(names)}", **dict(zip(names[1:], dims[1:])))

        featT = view(space1, 0, [B, S])
        INV = view(space1, 3072, [B, D])
        YT = view(space1, 0, [G, B, P])
        YT_tiles = view(space1, 0, [G, NT, B, 16])
        q_parts = view(space2, 0, [PARTS, B * S], BF16)
        QF, KF, VT = (view(space2, k * 2 * B * P, [2, NT, P]) for k in range(3))
        SE = view(space2, 0, [4, E, D])
        q_stack = view(space3, 0, [4, QB * S], BF16, KPAD)
        EX = view(space3, 0, [QPG, 16, P])
        w1_sb = [view(space4, 0, [E2, FF]), view(space8, 0, [E2, FF])]
        w2_sb = [[view(space4, E2 * FF, [E2, FC, D])[:, j] for j in range(E2)],
                 [view(space3, 1024 * (1 + j // 2 * 2) + (j % 2) * FC * D, [FC, D]) for j in range(E2)]]
        probs = view(space4, 0, [2, QB, S])
        ET = view(space4, 0, [QPG, 16, P])
        qf = view(space5, 0, [2, S])
        rest = view(space5, 1024, [2, S])
        v_heads = view(space5, 2048, [TC, NH, 32])
        OT = view(space5, 0, [G, B, P])
        kv_in = view(space6, 0, [2, TC, D])
        kvT = view(space6, 1024, [2, S])
        k_rest = view(space6, 2048, [2, S])
        k_parts = view(space6, 3072, [PARTS, S], BF16)
        A = view(space6, 0, [G, B, D])
        k_plain = view(space7, 0, [4, S], BF16, KPAD)
        k_shift = view(space7, 1024, [4, S], BF16, KPAD)
        SM = view(space8, 0, [16, P])
        lsub, gexp, eq, cum, place = (view(space8, k * T * E, [T * E]) for k in range(5))
        tot, incl = (view(space8, k * T * E, [E, B, G]) for k in (5, 6))
        den_sb = sb("den_sb", [P, D])
        st6p = sb("st6p", [P, B, 6])
        smallp = sb("smallp", [P, 5, B])
        neg_half = sb("neg_half", [P, B])

        v_tmp = sb("v_tmp", [P, TC, D])
        v_head = sb("v_head", [P, 2, TC, 32])
        row_max = sb("row_max", [P, 2, QB * TC])
        max_rest = sb("max_rest", [P, 2, QB * TC])
        max_parts = sb("max_parts", [P, 2, PARTS, QB * TC], BF16)
        max_turned = sb("max_turned", [PARTS * QB * TC, 2, P], BF16)
        attended = sb("attended", [P, 2, S])
        st6 = sb("st6", [P, B, 6])
        small = sb("small", [P, 5, B])
        SC = sb("SC", [P, 2 * G, 16, B])
        PC = sb("PC", [P, 2 * G, 16, B])
        mx, sm2 = sb("mx", [P, 2 * G, 16]), sb("sm2", [P, 2 * G, 16])
        lmax, gate = sb("lmax", [P, T]), sb("gate", [P, T])
        weight = sb("weight", [P, T * E])
        mask1 = sb("mask1", [P, T * E], BF16)

        s_x = [sem(f"x_loaded{u}") for u in range(4)]
        s_kv, s_w, s_b, s_bc = (sem(n) for n in ("kv_loaded", "w_loaded", "b_loaded", "bv_row_loaded"))
        s_w12 = [sem("w12_loaded0"), sem("w12_loaded1")]
        s_bin, s_b1, s_b2, s_rows = sem("in_proj_b_loaded"), sem("b1_loaded"), sem("b2_loaded"), sem("rows_loaded")
        s_passed_pool, s_passed_dve, s_passed_pe = sem("passed_pool"), sem("passed_dve"), sem("passed_pe")
        s_const = sem("constants_set")
        s_pc, s_dc = sem("pool_chain"), sem("dve_chain")
        s_wt, s_wtc = sem("w_turned"), sem("wT_copied")
        s_kvt, s_kvtc = sem("kv_turned"), sem("kvT_copied")
        s_kp, s_kpe = sem("k_projected"), sem("k_evacuated")
        s_vp, s_vpe = sem("v_projected"), sem("v_evacuated")
        s_ks, s_kst = sem("k_split"), sem("k_stored")
        s_xn, s_xt, s_xtc = sem("x_normed"), sem("x_turned"), sem("xT_copied")
        s_qp, s_qe, s_qs, s_qst = sem("q_projected"), sem("q_evacuated"), sem("q_split"), [sem("q_stored0"), sem("q_stored1")]
        s_var, s_sd = sem("variance_ready"), sem("deviation_ready")
        s_vb = sem("v_biased")
        s_vset = sem("v_heads_set")
        s_ql = [sem(f"stack_loaded{j}") for j in range(4)]
        s_full, s_free = sem("rows_scored"), sem("rows_reduced")
        s_split, s_shift = sem("max_split"), sem("shift_loaded")
        s_sc, s_pr = sem("columns_scored"), sem("probs_ready")
        s_v = sem("v_head_ready")
        s_pv, s_pve = sem("pv_ready"), sem("pv_evacuated")
        s_ast = [sem("attended_stored0"), sem("attended_stored1")]

        (s_al, s_dl, s_rc, s_rs, s_rb, s_r1, s_st, s_r2, s_n2, s_r3) = (sem(n) for n in
            ("attended_loaded", "denominators_loaded", "inverses_ready", "inverses_stored", "inverses_loaded",
             "residual1_added", "statistics_ready", "residual2_added", "encoder_input_ready", "out_bias_added"))
        (s_b1t, s_b1c, s_w1t, s_w1c, s_wu, s_Wc) = (sem(n) for n in
            ("b1_turned", "b1T_copied", "w1_turned", "w1T_copied", "w12_multiplied", "W_copied"))
        (s_bw, s_csum, s_csplit, s_cl, s_q13) = (sem(n) for n in
            ("b1_w2_multiplied", "c_row_ready", "c_split", "c_loaded", "q_stack13_cleared"))
        (s_t, s_yt, s_pj, s_qkv) = (sem(n) for n in ("tokens_turned", "tokensT_copied", "qkv_projected", "qkv_copied"))
        (s_s2, s_msk, s_sub, s_e2, s_soft) = (sem(n) for n in
            ("scores2_ready", "scores2_masked", "scores2_less_max", "exp2_done", "softmax2_done"))
        (s_ex, s_ext, s_et, s_av, s_ot) = (sem(n) for n in
            ("probs2_spread", "probs2_turned", "probs2T_copied", "attended2_ready", "attended2_copied"))
        (s_op, s_n3, s_y1, s_lg, s_oh, s_ge, s_cnt, s_gate) = (sem(n) for n in
            ("out_projected", "norm3_done", "y1_ready", "logits_ready", "expert_masks_ready", "gate_exp_done",
             "tokens_counted", "weights_ready"))
        (s_xp, s_we, s_moe, s_n4, s_aff, s_n5, s_y2, s_out) = (sem(n) for n in
            ("experts_done", "experts_weighed", "experts_summed", "norm4_done", "affine2_done", "norm5_done",
             "output_ready", "output_stored"))

        same = lambda t: t.rearrange("p a b -> p (a b)")

        UNITS = [[(g, b) for g in gs for b in bs] for bs in (range(0, QB), range(QB, B)) for gs in (range(0, 2), range(2, 4))]
        x_tok = x.rearrange("b (g p) f -> g p b f", p=P)
        out_tok = out.rearrange("b (g p) f -> g p b f", p=P)

        def norm(dve, ch, k, src, dst):
            for b in range(B):
                ins = dve.bn_stats(st6[:, b, :], src(b))
            ch.done(ins)
            ch.wait()
            me, m2e, mo, m2o = (st6[:, :, j] for j in (1, 2, 4, 5))
            mean, diff, var, inv = (small[:, j, :] for j in range(4))
            ch.done(dve.tensor_tensor(mean, me, mo, ADD))
            ch.done(dve.tensor_tensor(diff, me, mo, SUB))
            ch.done(dve.tensor_tensor(var, m2e, m2o, ADD))
            ch.wait()
            ch.done(dve.scalar_tensor_tensor(small[:, 4, :], diff, D / 4.0, diff, MUL, MUL))
            ch.done(dve.tensor_scalar(mean, mean, 0.5, None, MUL))
            ch.wait()
            ch.done(dve.tensor_tensor(var, var, small[:, 4, :], ADD))
            ch.wait()
            dve.tensor_scalar(var, var, 1.0 / D, EPS, MUL, ADD).then_inc(s_var, 1)
            dve.wait_ge(s_sd, k + 1)
            ch.done(dve.reciprocal(inv, var))
            ch.wait()
            for b in range(B):
                ins = dve.tensor_scalar(dst(b), src(b), small[:, 0, b:b + 1], small[:, 3, b:b + 1], SUB, MUL)
            return ins

        def tiles(t, g):
            return lambda b: t[:, g, b, :]

        NORM = 8

        def root(act, k):
            act.wait_ge(s_var, k + 1)
            act.activation(small[:, 2, :], small[:, 2, :], ACT.Sqrt).then_inc(s_sd, 1)


        def project_q(act, b):
            act.wait_ge(s_qp, b + 1)
            if b >= 2:
                act.wait_ge(s_qs, b - 1)
            act.activation(qf[:, b % 2], ps[:, b % QB, :], ACT.Relu, bias=bias_col[:, 0:1])
            act.activation(q_parts[:, 0, b * S:(b + 1) * S], ps[:, b % QB, :], ACT.Relu,
                           bias=bias_col[:, 0:1]).then_inc(s_qe, 1)

        W1T_BANK, W_BANK, C_BANK = 6, 5, 4

        def turn_b1(pe):
            for c in range(FC):
                mm = pe.transpose(ps[:, C_BANK, c * E:(c + 1) * E], b1_sb[:, c * P:(c + 1) * P], ident[0:E, 0:E])
            mm.then_inc(s_b1t, 1)

        def fold_weights(pe, r):
            pe.wait_ge(s_w12[r], 32 + 16 * r)

            def turn_w1(e):
                if e >= 2:
                    pe.wait_ge(s_w1c, e - 1)
                for c in range(FC):
                    mm = pe.transpose(ps[:, W1T_BANK + e % 2, c * P:(c + 1) * P],
                                      w1_sb[r][:, e % E2, c * P:(c + 1) * P], ident[:])
                mm.then_inc(s_w1t, 1)

            turn_w1(E2 * r)
            pe.wait_ge(s_b1c, 1)
            for j in range(E2):
                e = E2 * r + j
                if j + 1 < E2:
                    turn_w1(e + 1)
                pe.wait_ge(s_w1c, e + 1)
                if j == 0 and r:
                    pe.wait_ge(s_Wc, r)
                for c in range(FC):
                    mm = pe.matmul(ps[:, W_BANK, j * D:(j + 1) * D], w1T[:, e % 2, c, :], w2_sb[r][j][:, c, :],
                                   start=(c == 0), stop=(c == FC - 1))
                mm.then_inc(s_wu, 1)
            for c in range(FC):
                for j in range(E2):
                    mm = pe.matmul(ps[32 * j:32 * j + 32, C_BANK, P * (1 + r):P * (2 + r)], b1T[:, c, E2 * r + j, :],
                                   w2_sb[r][j][:, c, :], start=(c == 0), stop=(c == FC - 1))
            mm.then_inc(s_bw, 1)

        def copy_weights(act, r):
            if r == 0:
                act.wait_ge(s_b1t, 1)
                act.wait_ge(s_const, 8)
                act.copy(b1T[:].rearrange("p c e z -> p (c e) z")[:, :, 0:1],
                         ps[:, C_BANK, 0:FC * E].rearrange("p (k o) -> p k o", o=1)).then_inc(s_b1c, 1)
            for e in range(E2 * r, E2 * r + E2):
                act.wait_ge(s_w1t, e + 1)
                if e >= 2:
                    act.wait_ge(s_wu, e - 1)
                act.copy(w1T[:, e % 2], ps[:, W1T_BANK + e % 2, :]).then_inc(s_w1c, 1)
                if e == 1:
                    root(act, 3)

        def copy_folded(act, r):
            act.wait_ge(s_wu, E2 * (r + 1))
            act.copy(W[:, E2 * r:E2 * r + E2].rearrange("p e d -> p (e d)"), ps[:, W_BANK, :]).then_inc(s_Wc, 1)

        def bcast(row, k):
            return row.rearrange("p (o f) -> p o f", o=1).broadcast_to([P, k, D])

        def back_end_sp(sp):
            for g in range(G):
                sp.wait_ge(s_y2, g + 1)
                sp.dma_start(out_tok[g], A[:, g]).then_inc(s_out, 16)
            sp.wait_ge(s_out, 16 * G)

        def pool_norm(pool, ch, src, dst):
            me, m2e, mo, m2o = (st6p[:, :, j] for j in (1, 2, 4, 5))
            mean, diff, var, inv, square = (smallp[:, j, :] for j in range(5))
            ch.done(pool.tensor_tensor(mean, me, mo, ADD))
            ch.done(pool.tensor_tensor(diff, me, mo, SUB))
            ch.done(pool.tensor_tensor(var, m2e, m2o, ADD))
            ch.wait()
            ch.done(pool.tensor_tensor(square, diff, diff, MUL))
            ch.done(pool.tensor_scalar(mean, mean, 0.5, None, MUL))
            ch.wait()
            ch.done(pool.tensor_scalar(square, square, D / 4.0, None, MUL))
            ch.wait()
            ch.done(pool.tensor_tensor(var, var, square, ADD))
            ch.wait()
            ch.done(pool.tensor_scalar(var, var, 1.0 / D, EPS, MUL, ADD))
            ch.wait()
            ch.done(pool.tensor_tensor(inv, var, neg_half[:], ALU.pow))
            ch.wait()
            over_f = lambda v: v.rearrange("p (b o) -> p b o", o=1).broadcast_to([P, B, D])
            ch.done(pool.tensor_tensor(dst, src, over_f(mean), SUB))
            ch.wait()
            return pool.tensor_tensor(dst, dst, over_f(inv), MUL)

        def pool_divide(pool, ch, g):
            hold(pool, s_al, 64 * (g + 1), s_passed_pool)
            hold(pool, s_rb, 64 * (g + 1), s_passed_pool)
            ch.done(pool.tensor_tensor(A[:, g], A[:, g], INV, MUL))
            ch.wait()
            pool.tensor_tensor(A[:, g], A[:, g], XN[:, g], ADD).then_inc(s_r1, 1)

        def pool_residual(pool, ch, g):
            hold(pool, s_st, 2 * g + 1, s_passed_pool)
            ch.done(pool_norm(pool, ch, A[:, g], A[:, g]))
            ch.wait()
            pool.tensor_tensor(X[:, g], X[:, g], A[:, g], ADD).then_inc(s_r2, 1)

        def pool_input(pool, ch, g):
            hold(pool, s_st, 2 * g + 2, s_passed_pool)
            pool_norm(pool, ch, X[:, g], A[:, g]).then_inc(s_n2, 1)
            hold(pool, s_n2, g + 1, s_passed_pool)
            pool.tensor_tensor(XN[:, g], A[:, g], bcast(rows[:, 4, :], B), ADD).then_inc(s_r3, 1)

        def dve_invert(dve, g):
            dve.wait_ge(s_dl, 64 * (g + 1))
            dve.reciprocal(den_sb[:], den_sb[:]).then_inc(s_rc, 1)

        def dve_statistics(dve, ready, g, src):
            hold(dve, ready, g + 1, s_passed_dve)
            for b in range(B):
                ins = dve.bn_stats(st6p[:, b, :], src[:, g, b, :])
            ins.then_inc(s_st, 1)

        def back_end_pool(pool, ch):

            def spread(g, half):
                q = QPG * g + half
                hold(pool, s_soft, q + 1, s_passed_pool)
                if not isinstance(g, int):
                    hold(pool, s_ext, 2 * q - 2, s_passed_pool)
                for h in range(NH2):
                    pool.tensor_tensor(
                        EX[:, half, 4 * h:4 * h + 4, :].rearrange("p t (m n) -> p t m n", n=16),
                        PC[:, q, 4 * h:4 * h + 4, :].rearrange("p t (m o) -> p t m o", o=1).broadcast_to([P, 4, B, 16]),
                        same_row[:].rearrange("p (o m n) -> p o m n", o=1, n=16).broadcast_to([P, 4, B, 16]),
                        MUL).then_inc(s_ex, 1)

            for half in range(QPG):
                spread(0, half)
            with pool.Fori(1, G) as g:
                for half in range(QPG):
                    spread(g, half)
            with pool.Fori(0, G) as g:
                hold(pool, s_n3, g + 1, s_passed_pool)
                ch.enter(g, 1)
                ch.done(pool.tensor_tensor(A[:, g], A[:, g], bcast(rows[:, 0, :], B), MUL))
                ch.wait()
                pool.tensor_tensor(A[:, g], A[:, g], bcast(rows[:, 1, :], B), ADD).then_inc(s_y1, 1)
            ch.leave(G)
            with pool.Fori(0, G) as g:
                ch.enter(g, 3 * B)
                for b in range(B):
                    hold(pool, s_we, B * g + b + 1, s_passed_pool)
                    e = SE[:, b % 4]
                    ch.done(pool.tensor_tensor(e[:, 0:4, :], e[:, 0:4, :], e[:, 4:8, :], ADD))
                    ch.wait()
                    ch.done(pool.tensor_tensor(e[:, 0:2, :], e[:, 0:2, :], e[:, 2:4, :], ADD))
                    ch.wait()
                    ch.done(pool.tensor_tensor(e[:, 0, :], e[:, 0, :], e[:, 1, :], ADD))
                    ch.wait()
                    pool.tensor_tensor(A[:, g, b, :], A[:, g, b, :], e[:, 0, :], ADD).then_inc(s_moe, 1)
            ch.leave(G)
            with pool.Fori(0, G) as g:
                hold(pool, s_n4, g + 1, s_passed_pool)
                ch.enter(g, 1)
                ch.done(pool.tensor_tensor(A[:, g], A[:, g], bcast(rows[:, 2, :], B), MUL))
                ch.wait()
                pool.tensor_tensor(A[:, g], A[:, g], bcast(rows[:, 3, :], B), ADD).then_inc(s_aff, 1)
            ch.leave(G)
            with pool.Fori(0, G) as g:
                hold(pool, s_n5, g + 1, s_passed_pool)
                pool.tensor_tensor(same(A[:, g]), same(A[:, g]), same(X[:, g]), ADD).then_inc(s_y2, 1)

        def back_end_pe(pe):
            def turn(src, banks, done):
                for b in range(B):
                    mm = pe.transpose(ps[:, banks + b // 4, (b % 4) * P:(b % 4 + 1) * P], src[:, b, :], ident[:])
                mm.then_inc(done, 1)

            def project(g):
                pe.wait_ge(s_n2, g + 1)
                turn(A[:, g], 4, s_t)
                pe.wait_ge(s_yt, 2 * g + 2)
                for j, first in ((3, 6), (4, 4)):
                    for half in range(2):
                        mm = pe.matmul(ps[:, first + half, :], wT[:, j, :], same(YT[:, g])[:, half * 512:half * 512 + 512],
                                       start=True, stop=True)
                    mm.then_inc(s_pj, 1)
                pe.wait_ge(s_qkv, 3 * g + 1)
                for t in range(NT):
                    mm = pe.matmul(ps[:, 6 + t // 4, (t % 4) * P:(t % 4 + 1) * P], YT[:, g, t, :],
                                   wT[:, 5, :], start=True, stop=True)
                mm.then_inc(s_pj, 1)
                pe.wait_ge(s_qkv, 3 * g + 3)

            def scores2(q):
                g, half = q // QPG, q % QPG
                if q >= 1:
                    pe.wait_ge(s_msk, q)
                for t in range(4):
                    for h in range(NH2):
                        rows_h = slice(HD2 * h, HD2 * h + HD2)
                        mm = pe.matmul(ps[:, h, t * P:(t + 1) * P], QF[rows_h, g % 2, 4 * half + t, :],
                                       KF[rows_h, g % 2, 4 * half + t, :], start=True, stop=True)
                mm.then_inc(s_s2, 1)

            pe.wait_ge(s_rows, 16 * 6)
            pe.wait_ge(s_pve, NQ)
            pe.wait_ge(s_pr, NQ * 16)
            project(0)
            project(1)
            scores2(0)
            for q in range(2 * G):
                g, half = q // QPG, q % QPG
                if q + 1 < 2 * G:
                    scores2(q + 1)
                for pair in range(2):
                    pe.wait_ge(s_ex, NH2 * q + 2 * (pair + 1))
                    if pair == 0 and q >= 1:
                        pe.wait_ge(s_ot, q)
                    for k in range(8):
                        mm = pe.transpose(ps[:, 4 + 2 * pair + k // 4, (k % 4) * P:(k % 4 + 1) * P],
                                          EX[:, half, 8 * pair + k, :], ident[:])
                    mm.then_inc(s_ext, 1)
                pe.wait_ge(s_et, 2 * q + 2)
                for t in range(4):
                    for h in range(NH2):
                        mm = pe.matmul(ps[HD2 * h:HD2 * h + HD2, 4, t * P:(t + 1) * P],
                                       VT[:, g % 2, 4 * half + t, HD2 * h:HD2 * h + HD2], ET[:, half, 4 * h + t, :],
                                       start=True, stop=True)
                mm.then_inc(s_av, 1)
                if q in (1, 3):
                    pe.wait_ge(s_ot, q + 1)
                    project(q // 2 + 2)
            pe.wait_ge(s_ot, 2 * G)
            pe.wait_ge(s_msk, 2 * G)
            for g in range(G):
                for b in range(B):
                    mm = pe.matmul(ps[:, 2 * g + b // 4, (b % 4) * P:(b % 4 + 1) * P], OT[:, g, b, :], wT[:, 6, :],
                                   start=True, stop=True)
                mm.then_inc(s_op, 1)
            for g in range(G):
                pe.wait_ge(s_y1, g + 1)
                turn(A[:, g], 2 * g, s_t)
            for g in range(G):
                pe.wait_ge(s_yt, 2 * G + 2 * g + 2)
                for b in range(B):
                    col = (g * B + b) * E
                    mm = pe.matmul(ps[:, 0, col:col + E], YT[:, g, b, :], wg_sb[:], start=True, stop=True)
            mm.then_inc(s_lg, 1)
            pe.wait_ge(s_oh, 1)
            pe.matmul(ps[:, 1, 0:T * E], upper[:], mask1[:], start=True, stop=True)
            pe.matmul(ps[:, 2, 0:T * E], all_ones[:], mask1[:], start=True, stop=True).then_inc(s_cnt, 1)
            pe.wait_ge(s_cl, 16 * E2)
            for t in range(T):
                bank = 2 * ((t + 2) % 4)
                if t == 2:
                    pe.wait_ge(s_gate, 1)
                if t >= 4:
                    pe.wait_ge(s_we, t - 3)
                for half in range(2):
                    pe.matmul(ps[:, bank + half, :], ones_stack[:], c_stack[:, half * 512:half * 512 + 512],
                              start=True, stop=False)
                    mm = pe.matmul(ps[:, bank + half, :], YT[:, t // B, t % B, :],
                                   W[:].rearrange("p e d -> p (e d)")[:, half * 512:half * 512 + 512],
                                   start=False, stop=True)
                mm.then_inc(s_xp, 1)

        def back_end_act(act):
            def project(g):
                act.wait_ge(s_t, g + 1)
                for half in range(2):
                    act.copy(YT_tiles[:, g, :, 4 * half:4 * half + 4, :].rearrange("p t b n -> p b t n"),
                             ps[:, 4 + half, :].rearrange("p (b t n) -> p b t n", b=4, n=16)).then_inc(s_yt, 1)
                for j, dst, first in ((0, QF, 6), (1, KF, 4)):
                    act.wait_ge(s_pj, 3 * g + j + 1)
                    act.activation(same(dst[:, g % 2]), ps[:, first:first + 2, :].rearrange("p a b -> p (a b)"),
                                   ACT.Identity, bias=bias_col[:, 3 + j:4 + j]).then_inc(s_qkv, 1)
                act.wait_ge(s_pj, 3 * g + 3)
                act.copy(same(VT[:, g % 2]), ps[:, 6:8, :].rearrange("p a b -> p (a b)")).then_inc(s_qkv, 1)

            project(0)
            project(1)
            def softmax_exp(q):
                act.wait_ge(s_sub, q + 1)
                act.activation(PC[:, q].rearrange("p a b -> p (a b)"), SC[:, q].rearrange("p a b -> p (a b)"),
                               ACT.Exp, scale=1.0 / math.sqrt(HD2)).then_inc(s_e2, 1)

            softmax_exp(0)
            for q in range(2 * G):
                g, half = q // QPG, q % QPG
                for pair in range(2):
                    act.wait_ge(s_ext, 2 * q + pair + 1)
                    act.copy(ET[:, half, 8 * pair:8 * pair + 8, :].rearrange("p a b -> p (a b)"),
                             ps[:, 4 + 2 * pair:6 + 2 * pair, :].rearrange("p a b -> p (a b)")).then_inc(s_et, 1)
                if q + 1 < 2 * G:
                    softmax_exp(q + 1)
                act.wait_ge(s_av, q + 1)
                for t in range(4):
                    n0 = 16 * (4 * half + t)
                    ins = act.activation(OT[:, g, :, n0:n0 + 16], ps[:, 4, t * P:(t + 1) * P].rearrange("p (l n) -> p l n", n=16),
                                         ACT.Identity, bias=bias_col[:, 5:6])
                ins.then_inc(s_ot, 1)
                if q in (1, 3):
                    project(q // 2 + 2)
            for g in range(G):
                root(act, G + g)
            for g in range(G):
                act.wait_ge(s_t, G + g + 1)
                for half in range(2):
                    act.copy(same(YT[:, g, 4 * half:4 * half + 4]), ps[:, 2 * g + half, :]).then_inc(s_yt, 1)
            act.wait_ge(s_oh, 1)
            act.activation(gexp[:], lsub[:], ACT.Exp).then_inc(s_ge, 1)
            with act.Fori(2 * G, 4 * G) as k:
                root(act, k)

        def back_end_dve(dve, ch):
            def compact(q):
                hold(dve, s_s2, q + 1, s_passed_dve)
                dve.tensor_tensor(SM[:], ps[:, 0:4, :].rearrange("p a (t f) -> p (a t) f", f=P),
                                  bcast(same_row[:], 16), MUL).then_inc(s_msk, 1)
                hold(dve, s_msk, q + 1, s_passed_dve)
                ch.done(dve.tensor_reduce(SC[:, q], SM[:].rearrange("p a (m n) -> p a m n", n=16), AX.X, ADD))
                ch.wait()
                ch.done(dve.tensor_reduce(mx[:, q], SC[:, q], AX.X, MAX))
                ch.wait()
                dve.tensor_tensor(SC[:, q], SC[:, q], mx[:, q].rearrange("p (a o) -> p a o", o=1).broadcast_to([P, 16, B]),
                                  SUB).then_inc(s_sub, 1)

            def normalise(q):
                hold(dve, s_e2, q + 1, s_passed_dve)
                ch.done(dve.tensor_reduce(sm2[:, q], PC[:, q], AX.X, ADD))
                ch.wait()
                ch.done(dve.reciprocal(sm2[:, q], sm2[:, q]))
                ch.wait()
                dve.tensor_tensor(PC[:, q], PC[:, q], sm2[:, q].rearrange("p (a o) -> p a o", o=1).broadcast_to([P, 16, B]),
                                  MUL).then_inc(s_soft, 1)

            with dve.Fori(0, 2 * G) as q:
                ch.enter(q, 4)
                compact(q)
                normalise(q)
            ch.leave(2 * G)
            for g in range(G):
                dve.wait_ge(s_op, g + 1)
                ch.done(dve.tensor_tensor(same(A[:, g]), ps[:, 2 * g:2 * g + 2, :].rearrange("p a b -> p (a b)"), same(XN[:, g]), ADD))
                ch.wait()
                norm(dve, ch, g + 1 * G, tiles(A, g), tiles(A, g)).then_inc(s_n3, 1)
            dve.wait_ge(s_lg, 1)
            L = ps[:, 0, 0:T * E].rearrange("p (t e) -> p t e", e=E)
            over_e = lambda v: v[:].rearrange("p (t o) -> p t o", o=1).broadcast_to([P, T, E])
            ch.done(dve.tensor_reduce(lmax[:], L, AX.X, MAX))
            ch.wait()
            ch.done(dve.tensor_tensor(lsub[:].rearrange("p (t e) -> p t e", e=E), L, over_e(lmax), SUB))
            ch.wait()
            ch.done(dve.tensor_scalar(eq[:], lsub[:], 0.0, None, ALU.is_equal))
            ch.wait()
            ch.done(dve.tensor_tensor_scan(cum[:], first_e[:], eq[:], 0.0, MUL, ADD))
            ch.wait()
            dve.scalar_tensor_tensor(mask1[:], cum[:], 1.0, eq[:], ALU.is_equal, MUL).then_inc(s_oh, 1)
            dve.wait_ge(s_ge, 1)
            ch.done(dve.tensor_reduce(gate[:], gexp[:].rearrange("p (t e) -> p t e", e=E), AX.X, ADD))
            ch.wait()
            ch.done(dve.reciprocal(gate[:], gate[:]))
            dve.wait_ge(s_cnt, 1)
            tot_src = ps[:, 2, 0:T * E].rearrange("p (g b e) -> p e b g", g=G, e=E)
            for e in range(E):
                ins = dve.tensor_copy(tot[:, e], tot_src[:, e])
            ch.done(ins)
            ch.wait()
            flat = lambda v: v[:].rearrange("p e b g -> p (e b g)")
            ch.done(dve.tensor_tensor_scan(flat(incl), first_t[:], flat(tot), 0.0, MUL, ADD))
            ch.wait()
            ch.done(dve.tensor_tensor(flat(incl), flat(incl), flat(tot), SUB))
            ch.wait()
            for g in range(G):
                ins = dve.tensor_tensor(place[:].rearrange("p (g b e) -> p g b e", g=G, e=E)[:, g],
                                        ps[:, 1, 0:T * E].rearrange("p (g b e) -> p g b e", g=G, e=E)[:, g],
                                        incl[:, :, :, g].rearrange("p e b -> p b e"), ADD)
            ch.done(ins)
            ch.wait()
            ch.done(dve.scalar_tensor_tensor(place[:], place[:], CAP + 0.5, mask1[:], ALU.is_lt, MUL))
            ch.wait()
            dve.tensor_tensor(weight[:].rearrange("p (t e) -> p t e", e=E), place[:].rearrange("p (t e) -> p t e", e=E),
                              over_e(gate), MUL).then_inc(s_gate, 1)
            dve.wait_ge(s_gate, 1)
            for t in range(T):
                dve.wait_ge(s_xp, t + 1)
                if t >= 4:
                    dve.wait_ge(s_moe, t - 3)
                bank = 2 * ((t + 2) % 4)
                dve.tensor_tensor(SE[:, t % 4], ps[:, bank:bank + 2, :].rearrange("p a (e d) -> p (a e) d", d=D),
                                  weight[:, t * E:(t + 1) * E].rearrange("p (e o) -> p e o", o=1).broadcast_to([P, E, D]),
                                  MUL).then_inc(s_we, 1)
            with dve.Fori(0, G) as g:
                ch.enter(g, NORM)
                dve.wait_ge(s_moe, B * g + B)
                norm(dve, ch, g + 2 * G, tiles(A, g), tiles(A, g)).then_inc(s_n4, 1)
            ch.leave(G)
            with dve.Fori(0, G) as g:
                ch.enter(g, NORM)
                dve.wait_ge(s_aff, g + 1)
                norm(dve, ch, g + 3 * G, tiles(A, g), tiles(A, g)).then_inc(s_n5, 1)
            ch.leave(G)

        block = ctx.enter_context(nc.Block())

        @block.sync
        def _(sp):
            for u, unit in enumerate(UNITS):
                for g, b in (unit[0], unit[QB]):
                    sp.dma_start(X[:, g, b:b + QB], x_tok[g][:, b:b + QB]).then_inc(s_x[u], 16)
            for j, row in enumerate((bq, bk, bv)):
                sp.dma_start(bias_col[:, j:j + 1], row.rearrange("(p o) -> p o", o=1)).then_inc(s_b, 16)
            sp.dma_start(bv_row[:], bv.rearrange("(o f) -> o f", o=1).broadcast_to([P, D])).then_inc(s_bc, 16)

            def load_weights(r):
                es = slice(E2 * r, E2 * r + E2)
                sp.dma_start(w1_sb[r], w1[es].rearrange("e p f -> p e f")).then_inc(s_w12[r], 16)
                if r == 0:
                    sp.dma_start(view(space4, E2 * FF, [E2, FC, D]),
                                 w2[es].rearrange("e (c p) d -> p e c d", p=P)).then_inc(s_w12[r], 16)
                else:
                    for j in (0, 2):
                        sp.dma_start(view(space3, 1024 * (1 + j), [2, FC, D]),
                                     w2[E2 + j:E2 + j + 2].rearrange("e (c p) d -> p e c d", p=P)).then_inc(s_w12[r], 16)

            sp.dma_start(b1_sb[:], b1).then_inc(s_b1, 16)
            load_weights(0)
            for j in range(3):
                sp.dma_start(bias_col[:, 3 + j:4 + j], bin_[j * P:(j + 1) * P].rearrange("(p o) -> p o", o=1)).then_inc(s_bin, 16)
            load_weights(1)
            sp.wait_ge(s_ks, 1)
            for r, (_, part) in enumerate(PRODUCTS):
                sp.dma_start(k_dram[:, r * DH:(r + 1) * DH, :].rearrange("h d t -> h d t"),
                             k_parts[:, part, :]).then_inc(s_kst, 16)
            sp.wait_ge(s_const, 8)
            for j in range(E2):
                sp.dma_start(b2_sb[32 * j:32 * j + 1], b2.rearrange("(r j o) d -> j o r d", r=2, o=1)[j]).then_inc(s_b2, 16)
            for j, r in enumerate((ln1g, ln1b, ln2g, ln2b, bout)):
                sp.dma_start(rows[:, j, :], r.rearrange("(o f) -> o f", o=1).broadcast_to([P, D])).then_inc(s_rows, 16)
            sp.dma_start(wg_sb[:], wg).then_inc(s_rows, 16)

            def store_q(half):
                sp.wait_ge(s_qs, QB * (half + 1))
                cols = slice(half * QB * S, (half + 1) * QB * S)
                sp.dma_start(q_dram[:, :, cols].rearrange("r p s -> p r s"), q_parts[:, :, cols]).then_inc(s_qst[half], 16)

            def load_stack(head, half, buf):
                lo = head * DH
                qs = slice(half * QB * S, (half + 1) * QB * S)
                r = 0
                for n in (3, 2, 1):
                    src = q_dram[0:n, bass_ds(lo, DH), qs]
                    sp.dma_start(q_stack[r * DH:(r + n) * DH, buf, :], src).then_inc(s_ql[buf], 16)
                    r += n
                src = k_dram[bass_ds(head, 1), :, :].rearrange("o r t -> (o r) t")
                sp.dma_start(k_plain[0:KROWS, buf, :], src).then_inc(s_ql[buf], 16)
                sp.dma_start(k_shift[0:KROWS, buf, :], src).then_inc(s_ql[buf], 16)

            def load_shift(par, buf):
                sp.dma_start(q_stack[SHIFT_ROW:SHIFT_ROW + PARTS, buf, :].rearrange("r (c s) -> r c s", s=P),
                             max_turned[:, par, :]).then_inc(s_shift, 16)

            def store_attended(head, half, par):
                for bb in range(QB):
                    dst = a_dram[half * QB + bb, bass_ds(head, 1), :, :].rearrange("o r s -> (o r) s")
                    sp.dma_start(dst, attended[32 * bb:32 * bb + DH + 1, par, :]).then_inc(s_ast[par], 16)

            def load_attended(g):
                for par in range(2):
                    sp.wait_ge(s_ast[par], 64 * 4 * (g + 1))
                for h in range(NH // G):
                    src = a_dram[:, bass_ds(g * (NH // G) + h, 1), 0:DH, :]
                    sp.dma_start(A[32 * h:32 * h + 32, bass_ds(g, 1)].rearrange("p o b f -> p (o b) f"),
                                 src.rearrange("b o d (j f) -> (o d j) b f", f=D)).then_inc(s_al, 16)
                    den = a_dram[:, bass_ds(g * (NH // G) + h, 1), DH:DH + 1, :]
                    sp.dma_start(den_sb[32 * h:32 * h + 32], den.rearrange("b h o (j f) -> (h o j) b f", f=D)).then_inc(s_dl, 16)

            def store_inverses(g):
                sp.wait_ge(s_rc, g + 1)
                sp.dma_start(inv_dram.rearrange("h j b f -> (h j b) f"), den_sb[:]).then_inc(s_rs, 16)

            def load_inverses(g):
                sp.wait_ge(s_rs, 16 * (g + 1))
                for h in range(NH // G):
                    src = inv_dram[h:h + 1].rearrange("o j b f -> o j (b f)").broadcast_to([DH, S // D, B * D])
                    sp.dma_start(same(INV[32 * h:32 * h + 32]), src).then_inc(s_rb, 16)

            store_q(0)
            sp.wait_ge(s_kst, 16 * len(PRODUCTS))
            sp.wait_ge(s_const, 8)
            sp.wait_ge(s_qst[0], 16)
            load_stack(0, 0, 0)
            load_stack(1, 0, 2)
            store_q(1)
            sp.wait_ge(s_q13, 2)
            sp.wait_ge(s_qst[1], 16)
            load_stack(0, 1, 1)
            sp.wait_ge(s_csplit, 1)
            c_rows = c_stack[0:PARTS, :].rearrange("q (r j d) -> q r j d", r=2, d=D)
            for j in range(E2):
                sp.dma_start(c_rows[:, :, j, :], c_parts[32 * j:32 * j + 1]).then_inc(s_cl, 16)
            sp.wait_ge(s_free, 8 + 3)
            load_shift(0, 0)
            def slot(i, kk, last):
                kappa = 4 * i + kk
                if not last or kk == 0:
                    if not (isinstance(i, int) and kappa == 0):
                        sp.wait_ge(s_sc, 64 * i + 16 * kk)
                    load_stack(2 * i + (kk + 3) // 2, (kk + 3) % 2, (kk + 3) % 4)
                if not (isinstance(i, int) and kappa == 0):
                    sp.wait_ge(s_pve, 4 * i + kk)
                    store_attended(2 * i + (kk - 1) // 2, (kk - 1) % 2, (kk - 1) % 2)
                if not last or kk < 3:
                    sp.wait_ge(s_free, 36 * i + 17 + 9 * kk + (1 if last and kk == 2 else 3))
                    load_shift((kk + 1) % 2, (kk + 1) % 4)

            def group(g):
                for c in range(8):
                    if c == 1 and not (isinstance(g, int) and g == 0):
                        load_attended(g - 1)
                    if c == 3 and not (isinstance(g, int) and g == 0):
                        load_inverses(g - 1)
                    slot(2 * g + c // 4, c % 4, isinstance(g, int) and g == G - 1 and c >= 4)
                    if c == 2 and not (isinstance(g, int) and g == 0):
                        store_inverses(g - 1)

            group(0)
            with sp.Fori(1, G - 1) as g:
                group(g)
            group(G - 1)
            sp.wait_ge(s_pve, NQ)
            store_attended(NH - 1, 1, 1)
            load_attended(G - 1)
            store_inverses(G - 1)
            load_inverses(G - 1)
            back_end_sp(sp)

        @block.gpsimd
        def _(pool):
            ch = Chain(pool, s_pc, s_passed_pool)
            ch.done(pool.memset(ident[:], 0.0))
            ch.done(pool.memset(upper[:], 1.0))
            ch.done(pool.memset(same_row[:], 0.0))
            ch.done(pool.memset(neg_half[:], -0.5))
            pool.memset(all_ones[:], 1.0).then_inc(s_const, 1)
            pool.memset(ones_stack[:], 1.0).then_inc(s_const, 1)
            ch.wait()
            ch.done(pool.affine_select(out=ident[:], in_=ident[:], compare_op=ALU.not_equal, fill=1.0, base=0,
                                       pattern=[[-1, P]], channel_multiplier=1))
            pool.affine_select(out=upper[:], in_=upper[:], compare_op=ALU.is_ge, fill=0.0, base=0,
                               pattern=[[1, P]], channel_multiplier=-1).then_inc(s_const, 1)
            ch.wait()
            pool.tensor_copy(ident16[:], ident[:]).then_inc(s_const, 1)
            pool.memset(v_heads[:], 0.0).then_inc(s_vset, 1)
            pool.wait_ge(s_vset, 1)
            pool.memset(v_heads[:, :, :, DH:DH + 1], 1.0).then_inc(s_vset, 1)
            for j in (0, 2):
                ins = pool.memset(view(space3, 1024 * j, [1024], F32, KPAD), 0.0)
            ins.then_inc(s_const, 1)
            pool.memset(b1T[:], 0.0)
            pool.memset(b2_sb[:], 0.0)
            pool.memset(k_plain, 0.0).then_inc(s_const, 1)
            ch.done(pool.memset(k_shift[:], 0.0))
            ch.wait()
            ch.done(pool.affine_select(out=k_shift[:], in_=k_shift[:], compare_op=ALU.is_gt, fill=-1.0, base=SHIFT_ROW,
                                       pattern=[[0, 4], [0, S]], channel_multiplier=-1))
            ch.wait()
            pool.affine_select(out=k_shift[:], in_=k_shift[:], compare_op=ALU.is_gt, fill=0.0, base=SHIFT_ROW + PARTS,
                               pattern=[[0, 4], [0, S]], channel_multiplier=-1).then_inc(s_const, 1)
            pool.memset(c_stack[:], 0.0).then_inc(s_const, 1)

            def split_max(count, par):
                hold(pool, s_free, count, s_passed_pool)
                m, r, parts = row_max[:, par], max_rest[:, par], max_parts[:, par]
                ch.done(pool.tensor_copy(parts[:, 0], m))
                ch.wait()
                ch.done(pool.tensor_tensor(r, m, parts[:, 0], SUB))
                ch.wait()
                ch.done(pool.tensor_copy(parts[:, 1], r))
                ch.wait()
                pool.tensor_tensor(parts[:, 2], r, parts[:, 1], SUB).then_inc(s_split, 1)

            def pick_v(head, par):
                pool.tensor_copy(v_head[:, par], v_heads[:, :, head, :]).then_inc(s_v, 1)

            for m in range(-7, 8):
                ch.done(pool.affine_select(out=same_row[:], in_=same_row[:], compare_op=ALU.not_equal, fill=1.0,
                                           base=16 * m, pattern=[[-1, P]], channel_multiplier=1))
                ch.wait()
            ch.done(pool.memset(first_e[:], 1.0))
            ch.done(pool.memset(first_t[:], 1.0))
            ch.wait()
            pool.memset(first_e[:].rearrange("p (t e) -> p t e", e=E)[:, :, 0:1], 0.0).then_inc(s_const, 1)
            pool.memset(first_t[:].rearrange("p (e t) -> p e t", t=T)[:, :, 0:1], 0.0).then_inc(s_const, 1)

            pool.wait_ge(s_bw, 2)
            for j in (1, 3):
                pool.memset(view(space3, 1024 * j, [1024], F32, KPAD), 0.0).then_inc(s_q13, 1)
            pool.wait_ge(s_vb, TC)
            pool.wait_ge(s_vset, 2)
            pick_v(0, 0)
            split_max(8, 0)
            pool.wait_ge(s_rows, 16 * 6)
            pool.wait_ge(s_csum, 1)
            ch.done(pool.tensor_copy(c_parts[:, 0], c_row[:]))
            ch.wait()
            ch.done(pool.tensor_tensor(c_rest[:], c_row[:], c_parts[:, 0], SUB))
            ch.wait()
            ch.done(pool.tensor_copy(c_parts[:, 1], c_rest[:]))
            ch.wait()
            pool.tensor_tensor(c_parts[:, 2], c_rest[:], c_parts[:, 1], SUB).then_inc(s_csplit, 1)

            def slot(i, kk, last):
                if not last or kk < 3:
                    split_max(36 * i + 9 * (kk + 1) + 8, (kk + 1) % 2)
                if kk % 2 == 0 and not (last and kk == 2):
                    if not (isinstance(i, int) and 4 * i + kk == 0):
                        hold(pool, s_pv, 4 * i + kk, s_passed_pool)
                    pick_v(2 * i + kk // 2 + 1, (kk // 2 + 1) % 2)

            def group(g):
                for c in range(8):
                    slot(2 * g + c // 4, c % 4, isinstance(g, int) and g == G - 1 and c >= 4)
                    if not (isinstance(g, int) and g == 0):
                        if c == 4:
                            pool_divide(pool, ch, g - 1)
                        if c == 5:
                            pool_residual(pool, ch, g - 1)
                        if c == 6:
                            pool_input(pool, ch, g - 1)

            group(0)
            with pool.Fori(1, G - 1) as g:
                ch.enter(g - 1, 46)
                group(g)
            ch.leave(G - 2)
            group(G - 1)
            pool_divide(pool, ch, G - 1)
            pool_residual(pool, ch, G - 1)
            pool_input(pool, ch, G - 1)
            back_end_pool(pool, ch)

        def ring(n):
            return ps[:, 2 * (n % 2):2 * (n % 2) + 2, :]

        col_bank = lambda u: 4 + u % 3
        PV = 7

        @block.tensor
        def _(pe):
            pe.wait_ge(s_const, 4)
            pe.wait_ge(s_w, 16 * 5)
            for j in range(7):
                mm = pe.transpose(ps[:, 4 + j // 4, (j % 4) * P:(j % 4 + 1) * P], w_in[:, j, :], ident[:])
            mm.then_inc(s_wt, 1)
            pe.wait_ge(s_kv, 32)
            for a in range(2):
                for c in range(TC):
                    mm = pe.transpose(ps[:, 6 + a, c * P:(c + 1) * P], kv_in[:, a, c, :], ident[:])
            mm.then_inc(s_kvt, 1)
            pe.wait_ge(s_wtc, 1)
            pe.wait_ge(s_kvtc, 1)
            pe.matmul(ps[:, 4, :], wT[:, 1, :], kvT[:, 0, :], start=True, stop=True).then_inc(s_kp, 1)
            for c in range(TC):
                mm = pe.matmul(ps[:, 5, c * P:(c + 1) * P], kvT[:, 1, c * P:(c + 1) * P], wT[:, 2, :],
                               start=True, stop=True)
            mm.then_inc(s_vp, 1)

            def turn_unit(u):
                pe.wait_ge(s_xn, u + 1)
                for g, b in UNITS[u]:
                    mm = pe.transpose(ps[:, b % QB, g * P:(g + 1) * P], XN[:, g, b, :], ident[:])
                mm.then_inc(s_xt, 1)

            def project_half(half):
                for b in range(QB * half, QB * half + QB):
                    pe.wait_ge(s_xtc, b + 1)
                    pe.matmul(ps[:, b % QB, :], wT[:, 0, :], featT[:, b, :], start=True, stop=True).then_inc(s_qp, 1)

            turn_unit(0)
            turn_unit(1)
            project_half(0)
            pe.wait_ge(s_kpe, 1)
            pe.wait_ge(s_vpe, 1)
            pe.wait_ge(s_b1, 16)
            turn_b1(pe)
            pe.wait_ge(s_qe, QB)
            turn_unit(2)
            fold_weights(pe, 0)
            turn_unit(3)
            project_half(1)
            fold_weights(pe, 1)

            def score_rows(n, quad_buf, bb, pair, waits):
                if waits is not None:
                    pe.wait_ge(s_free, waits)
                for j in range(2):
                    lo = bb * S + (2 * pair + j) * P
                    mm = pe.matmul(ring(n)[:, j, :], q_stack[:, quad_buf, lo:lo + P], k_plain[:, quad_buf, :],
                                   start=True, stop=True)
                mm.then_inc(s_full, 1)

            def turn_max(n, par, waits, split):
                pe.wait_ge(s_free, waits)
                hold(pe, s_split, split, s_passed_pe)
                dst = ps[0:PARTS * QB * TC, 2 * (n % 2), 0:P // 2].bitcast(BF16)
                pe.transpose(dst, max_parts[:, par].rearrange("p r c -> p (r c)"), ident16[:]).then_inc(s_full, 1)

            def score_columns(u, quad_buf, tc, bb, waits):
                if waits is not None:
                    pe.wait_ge(s_pr, waits)
                pe.matmul(ps[:, col_bank(u), :], k_shift[:, quad_buf, tc * P:(tc + 1) * P],
                          q_stack[:, quad_buf, bb * S:(bb + 1) * S], start=True, stop=True).then_inc(s_sc, 1)

            def multiply_v(par, head_par, tc):
                for bb in range(QB):
                    mm = pe.matmul(ps[32 * bb:32 * bb + 32, PV, :], v_head[:, head_par, tc, :],
                                   probs[:, par, bb, :], start=(tc == 0), stop=(tc == TC - 1))
                if tc == TC - 1:
                    mm.then_inc(s_pv, 1)

            pe.wait_ge(s_ql[0], 80)
            pe.wait_ge(s_qe, B)
            n = 0
            for bb in range(QB):
                for pair in range(2):
                    score_rows(n, 0, bb, pair, n - 1 if n >= 2 else None)
                    n += 1
            pe.wait_ge(s_ql[1], 80)
            for bb in range(QB):
                for pair in range(2):
                    score_rows(n, 1, bb, pair, n - 1)
                    n += 1
                if bb == 0:
                    turn_max(n, 0, n - 1, 1)
                    n += 1
            assert n == 17
            pe.wait_ge(s_shift, 16)
            pe.wait_ge(s_Wc, 2)
            pe.wait_ge(s_csum, 1)
            for bb in range(QB):
                score_columns(bb, 0, 0, bb, None if bb < 3 else 1)

            def slot(i, kk, last):
                n0 = 17 + 9 * kk
                rows_too = not (last and kk >= 2)
                n = n0
                for tc in range(TC):
                    final = last and kk == 3 and tc == TC - 1
                    for pair in range(2):
                        if rows_too:
                            if tc == 0 and pair == 0:
                                pe.wait_ge(s_ql[(kk + 2) % 4], 80 * (i + (kk + 2) // 4 + 1))
                            score_rows(n, (kk + 2) % 4, tc, pair, 36 * i + n - 1)
                            n += 1
                        if final:
                            continue
                        if tc == TC - 1 and pair == 0:
                            pe.wait_ge(s_shift, 64 * i + 16 * (kk + 2))
                        for bb in (2 * pair, 2 * pair + 1):
                            u = 16 * kk + 4 * (tc + 1) + bb
                            before = u - 3 + {64: 2, 65: -1, 66: -1}.get(u, 0)
                            score_columns(u % 64, (kk + 1) % 4 if tc == TC - 1 else kk % 4, (tc + 1) % TC, bb,
                                          64 * i + before + 1)
                    if tc == 0 and not (last and kk == 3):
                        turn_max(n, (kk + 1) % 2, 36 * i + n - 1, 4 * i + kk + 2)
                        n += 1
                    if tc == 0:
                        pe.wait_ge(s_v, 2 * i + kk // 2 + 1)
                        if not (isinstance(i, int) and 4 * i + kk == 0):
                            pe.wait_ge(s_pve, 4 * i + kk)
                    pe.wait_ge(s_pr, 64 * i + 16 * kk + 4 * tc + 4)
                    multiply_v(tc % 2, (kk // 2) % 2, tc)

            for kk in range(4):
                slot(0, kk, False)
            with pe.Fori(1, IT - 1) as i:
                for kk in range(4):
                    slot(i, kk, False)
            for kk in range(4):
                slot(IT - 1, kk, True)
            back_end_pe(pe)

        @block.scalar
        def _(act):
            w_row = [wq, wk, wv]
            for j in range(3):
                act.dma_start(w_in[:, j, :], w_row[j]).then_inc(s_w, 16)
            act.dma_start(kv_in[:, 0], keys.rearrange("o (c p) f -> p (o c) f", p=P)).then_inc(s_kv, 16)
            act.dma_start(kv_in[:, 1], values.rearrange("o (c p) f -> p (o c) f", p=P)).then_inc(s_kv, 16)
            act.dma_start(w_in[:, 3:6, :], win.rearrange("(j p) f -> p j f", p=P)).then_inc(s_w, 16)
            act.dma_start(w_in[:, 6, :], wout).then_inc(s_w, 16)
            root(act, 0)
            act.wait_ge(s_wt, 1)
            act.copy(wT[:].rearrange("p j f -> p (j f)"),
                     ps[:, 4:6, :].rearrange("p a b -> p (a b)")[:, 0:7 * P]).then_inc(s_wtc, 1)
            act.wait_ge(s_kvt, 1)
            act.copy(kvT, ps[:, 6:8, :]).then_inc(s_kvtc, 1)
            root(act, 1)
            act.wait_ge(s_b, 16 * 3)
            act.wait_ge(s_kp, 1)
            act.activation(k_rest[:, 0], ps[:, 4, :], ACT.Relu, bias=bias_col[:, 1:2]).then_inc(s_kpe, 1)

            def project_half(half):
                act.wait_ge(s_xt, 2 * (half + 1))
                for b in range(QB * half, QB * half + QB):
                    act.copy(featT[:, b], ps[:, b % QB, :]).then_inc(s_xtc, 1)
                    if b % QB in (1, 2):
                        project_q(act, b - 1)
                if half == 0:
                    root(act, 2)
                for b in range(QB * half + QB - 2, QB * half + QB):
                    project_q(act, b)

            project_half(0)
            copy_weights(act, 0)
            copy_folded(act, 0)
            project_half(1)
            copy_weights(act, 1)
            copy_folded(act, 1)
            act.wait_ge(s_bin, 16 * 3)

            def exps(par, tc, u, waits):
                for bb in range(QB):
                    act.wait_ge(s_sc, waits + bb + 1)
                    act.activation(probs[:, par, bb, :], ps[:, col_bank((u + bb) % 64), :], ACT.Exp,
                                   scale=1.0 / math.sqrt(DH)).then_inc(s_pr, 1)

            exps(0, 0, 0, 0)

            def slot(i, kk, last):
                for tc in range(TC):
                    u = 16 * kk + 4 * (tc + 1)
                    if not (last and kk == 3 and tc == TC - 1):
                        exps((tc + 1) % 2, (tc + 1) % TC, u, 64 * i + u)
                act.wait_ge(s_pv, 4 * i + kk + 1)
                if not (isinstance(i, int) and 4 * i + kk < 2):
                    act.wait_ge(s_ast[kk % 2], 64 * (2 * i + kk // 2))
                act.copy(attended[:, kk % 2, :], ps[:, PV, :]).then_inc(s_pve, 1)

            for kk in range(4):
                slot(0, kk, False)
            with act.Fori(1, IT - 1) as i:
                for kk in range(4):
                    slot(i, kk, False)
            for kk in range(4):
                slot(IT - 1, kk, True)
            back_end_act(act)


        @block.vector
        def _(dve):
            ch = Chain(dve, s_dc, s_passed_dve)

            def norm_unit(u):
                dve.wait_ge(s_x[u], 32)
                at = lambda t: lambda j: t[:, UNITS[u][j][0], UNITS[u][j][1], :]
                norm(dve, ch, u, at(X), at(XN)).then_inc(s_xn, 1)

            norm_unit(0)
            norm_unit(1)
            dve.wait_ge(s_kpe, 1)
            ch.done(dve.tensor_copy(k_parts[:, 0], k_rest[:, 0]))
            ch.wait()
            ch.done(dve.tensor_tensor(k_rest[:, 1], k_rest[:, 0], k_parts[:, 0], SUB))
            ch.wait()
            ch.done(dve.tensor_copy(k_parts[:, 1], k_rest[:, 1]))
            ch.wait()
            dve.tensor_tensor(k_parts[:, 2], k_rest[:, 1], k_parts[:, 1], SUB).then_inc(s_ks, 1)
            dve.wait_ge(s_vp, 1)
            dve.wait_ge(s_bc, 16)
            dve.tensor_tensor(v_tmp[:], ps[:, 5, :].rearrange("p (c f) -> p c f", c=TC),
                              bv_row[:].rearrange("p (o f) -> p o f", o=1).broadcast_to([P, TC, D]), ADD).then_inc(s_vpe, 1)
            dve.wait_ge(s_vpe, 1)
            dve.wait_ge(s_vset, 2)
            for c in range(TC):
                dve.tensor_scalar(v_heads[:, c, :, 0:DH], v_tmp[:, c, :].rearrange("p (h d) -> p h d", d=DH),
                                  0.0, None, MAX).then_inc(s_vb, 1)

            def split_q(b):
                cols = slice(b * S, (b + 1) * S)
                dve.wait_ge(s_qe, b + 1)
                ch.done(dve.tensor_tensor(rest[:, b % 2], qf[:, b % 2], q_parts[:, 0, cols], SUB))
                ch.wait()
                ch.done(dve.tensor_copy(q_parts[:, 1, cols], rest[:, b % 2]))
                ch.wait()
                dve.tensor_tensor(q_parts[:, 2, cols], rest[:, b % 2], q_parts[:, 1, cols], SUB).then_inc(s_qs, 1)

            norm_unit(2)
            for b in range(QB):
                split_q(b)
            norm_unit(3)
            for b in range(QB, B):
                split_q(b)

            def reduce_rows(n, par, bb, pair, waits):
                dve.wait_ge(s_full, waits)
                c = bb * TC + 2 * pair
                dve.tensor_reduce(row_max[:, par, c:c + 2], ring(n), AX.X, MAX).then_inc(s_free, 1)

            def copy_turned(n, par, waits):
                dve.wait_ge(s_full, waits)
                src = ps[0:PARTS * QB * TC, 2 * (n % 2), 0:P // 2].bitcast(BF16)
                dve.tensor_copy(max_turned[:, par, :], src).then_inc(s_free, 1)

            n = 0
            for bb in range(QB):
                for pair in range(2):
                    reduce_rows(n, 0, bb, pair, n + 1)
                    n += 1
            dve.wait_ge(s_bw, 2)
            dve.wait_ge(s_b2, 16 * E2)
            dve.tensor_tensor(c_row[:], ps[:, C_BANK, P:3 * P].rearrange("p (r d) -> p r d", d=D), b2_sb[:],
                              ADD).then_inc(s_csum, 1)
            for bb in range(QB):
                for pair in range(2):
                    reduce_rows(n, 1, bb, pair, n + 1)
                    n += 1
                if bb == 0:
                    copy_turned(n, 0, n + 1)
                    n += 1

            def slot(i, kk, last):
                n = 17 + 9 * kk
                for tc in range(TC):
                    if not (last and kk >= 2):
                        if tc == 0:
                            dve.wait_ge(s_split, 4 * i + kk + 1)
                        for pair in range(2):
                            reduce_rows(n, kk % 2, tc, pair, 36 * i + n + 1)
                            n += 1
                    if tc == 0 and not (last and kk == 3):
                        if not (isinstance(i, int) and 4 * i + kk == 0):
                            dve.wait_ge(s_shift, 64 * i + 16 * kk)
                        copy_turned(n, (kk + 1) % 2, 36 * i + n + 1)
                        n += 1

            def group(g):
                for c in range(8):
                    slot(2 * g + c // 4, c % 4, isinstance(g, int) and g == G - 1 and c >= 4)
                    if not (isinstance(g, int) and g == 0):
                        if c == 1:
                            dve_invert(dve, g - 1)
                        if c == 4:
                            dve_statistics(dve, s_r1, g - 1, A)
                        if c == 5:
                            dve_statistics(dve, s_r2, g - 1, X)

            group(0)
            with dve.Fori(1, G - 1) as g:
                group(g)
            group(G - 1)
            dve_invert(dve, G - 1)
            dve_statistics(dve, s_r1, G - 1, A)
            dve_statistics(dve, s_r2, G - 1, X)
            back_end_dve(dve, ch)



NAMES = ["L0_attn_queries", "L0_attn_keys", "L0_attn_values", "L0_attn_Wq_w", "L0_attn_Wq_b", "L0_attn_Wk_w",
         "L0_attn_Wk_b", "L0_attn_Wv_w", "L0_attn_Wv_b", "L0_ffn_in_proj_w", "L0_ffn_in_proj_b", "L0_ffn_out_proj_w",
         "L0_ffn_out_proj_b", "L0_ffn_ln1_g", "L0_ffn_ln1_b", "L0_ffn_ln2_g", "L0_ffn_ln2_b", "L0_ffn_wg",
         "L0_ffn_w1", "L0_ffn_b1", "L0_ffn_w2", "L0_ffn_b2"]


def kernel(**inputs):
    import concourse.bacc as bacc
    from concourse import mybir
    from concourse.bass_utils import run_bass_kernel_spmd

    nc = bacc.Bacc("TRN2", target_bir_lowering=False, num_devices=1)
    arrays, args = {}, []
    for name in NAMES:
        a = np.ascontiguousarray(inputs[name])
        arrays[f"in_{name}"] = a
        args.append(nc.dram_tensor(f"in_{name}", a.shape, mybir.dt.from_np(a.dtype), kind="ExternalInput").ap())
    args.append(nc.dram_tensor("out_0", (B, S, D), mybir.dt.float32, kind="ExternalOutput").ap())
    build(nc, *args)
    r = run_bass_kernel_spmd(nc, [arrays], core_ids=[0])
    return r.results[0]["out_0"]
```

```python
import math

import numpy as np

P = 128
D = 128
B = 8
S = 512
G = S // P
NH, DH = 16, 8
NH2, HD2 = 4, 32
E, FF = 8, 512
E2 = E // 2
FC = FF // P
CAP = B * S // E
T = G * B
QB = 4
NQ = NH * B // QB
TC = S // P
PARTS = 3
PRODUCTS = [(0, 0), (1, 0), (2, 0), (0, 1), (1, 1), (0, 2)]
KROWS = DH * len(PRODUCTS)
SHIFT_ROW = KROWS
KPAD = 96
EPS = 1e-5
IT = NQ // 4
NT = P // 16
QPG = 2
ACT_WEIGHS, POOL_SUMS = [0, 2, 4, 6], [0, 3, 5, 6]
DVE_WEIGHS = [b for b in range(B) if b not in ACT_WEIGHS]
DVE_SUMS = [b for b in range(B) if b not in POOL_SUMS]


def count(of, g, b):
    return len(of) * g + of.index(b) + 1


def four_back(g, b):
    return (g, b - 4) if b >= 4 else (g - 1, b + 4)


def hold(engine, sem, value, passed):
    engine.wait_ge(sem, value)
    engine.sem_inc(passed, 1)


class Chain:

    def __init__(self, engine, sem, passed):
        self.engine, self.sem, self.passed, self.base, self.n = engine, sem, passed, 0, 0

    def done(self, ins):
        ins.then_inc(self.sem, 1)
        self.n += 1
        return ins

    def wait(self):
        if isinstance(self.base, int):
            self.engine.wait_ge(self.sem, self.base + self.n)
        else:
            hold(self.engine, self.sem, self.base + self.n, self.passed)

    def enter(self, i, per):
        self.fixed, self.per, self.base, self.n = self.base + self.n, per, i * per + (self.base + self.n), 0

    def leave(self, times):
        assert self.n == self.per, (self.n, self.per)
        self.base, self.n = self.fixed + times * self.per, 0


def build(nc, x, keys, values, wq, bq, wk, bk, wv, bv, win, bin_, wout, bout,
          ln1g, ln1b, ln2g, ln2b, wg, w1, b1, w2, b2, out):
    from contextlib import ExitStack
    from concourse import mybir
    from concourse.bass import ds as bass_ds

    F32, BF16 = mybir.dt.float32, mybir.dt.bfloat16
    ALU, ACT, AX = mybir.AluOpType, mybir.ActivationFunctionType, mybir.AxisListType
    ADD, SUB, MUL, MAX = ALU.add, ALU.subtract, ALU.mult, ALU.max

    with ExitStack() as ctx:
        def sb(name, shape, dt=F32):
            return ctx.enter_context(nc.sbuf_tensor(name, shape, dt))

        def sem(name):
            return ctx.enter_context(nc.semaphore(name))

        q_dram = nc.dram_tensor("q_parts_dram", (PARTS, P, B * S), BF16, kind="Internal").ap()
        k_dram = nc.dram_tensor("k_rows_dram", (NH, KROWS, S), BF16, kind="Internal").ap()
        a_dram = nc.dram_tensor("attended_dram", (B, NH, DH + 1, S), F32, kind="Internal").ap()
        inv_dram = nc.dram_tensor("inverses_dram", (NH // G, S // D, B, D), F32, kind="Internal").ap()

        ps = ctx.enter_context(nc.psum_tensor("ps", [P, 8, 512], F32))

        X = sb("X", [P, G, B, D])
        XN = sb("XN", [P, G, B, D])
        w_in = sb("w_in", [P, 7, D])
        wT = sb("wT", [P, 7, D])
        bias_col = sb("bias_col", [P, 6])
        bv_row = sb("bv_row", [P, D])
        rows = sb("rows", [P, 5, D])
        wg_sb = sb("wg_sb", [P, E])
        w1T = sb("w1T", [P, 2, FC, D])
        b1_sb = sb("b1_sb", [E, FF])
        b1T = sb("b1T", [P, FC, E, 32])
        W = sb("W", [P, E, D])
        b2_sb = sb("b2_sb", [P, 2, D])
        c_row = sb("c_row", [P, 2, D])
        c_rest = sb("c_rest", [P, 2, D])
        c_parts = sb("c_parts", [P, PARTS, 2, D], BF16)
        c_stack = sb("c_stack", [KPAD, E * D], BF16)
        ones_stack = sb("ones_stack", [KPAD, P], BF16)
        ident = sb("ident", [P, P])
        ident16 = sb("ident16", [P, P], BF16)
        upper = sb("upper", [P, P], BF16)
        all_ones = sb("all_ones", [P, P], BF16)
        same_row = sb("same_row", [P, P])
        first_e = sb("first_e", [P, T * E])
        first_t = sb("first_t", [P, T * E])

        space1, space2, space3 = sb("space1", [P, 4096]), sb("space2", [P, 6144]), sb("space3", [P, 4096])
        space4, space5, space6 = sb("space4", [P, 4096]), sb("space5", [P, 4096]), sb("space6", [P, 4096])
        space7, space8 = sb("space7", [P, 2048]), sb("space8", [P, 2048])

        def view(space, lo, dims, dt=F32, parts=P):
            n = int(np.prod(dims))
            words = n if dt == F32 else n // 2
            v = space[0:parts, lo:lo + words]
            if dt != F32:
                v = v.bitcast(dt)
            names = "abcd"[:len(dims)]
            if len(dims) == 1:
                return v
            return v.rearrange(f"p ({' '.join(names)}) -> p {' '.join(names)}", **dict(zip(names[1:], dims[1:])))

        featT = view(space1, 0, [B, S])
        INV = view(space1, 3072, [B, D])
        YT = view(space1, 0, [G, B, P])
        YT_tiles = view(space1, 0, [G, NT, B, 16])
        q_parts = view(space2, 0, [PARTS, B * S], BF16)
        QF, KF, VT = (view(space2, k * 2 * B * P, [2, NT, P]) for k in range(3))
        SE = view(space2, 0, [4, E, D])
        e_sum = view(space2, 4 * E * D, [len(DVE_SUMS), D])
        q_stack = view(space3, 0, [4, QB * S], BF16, KPAD)
        EX = view(space3, 0, [QPG, 16, P])
        w1_sb = [view(space4, 0, [E2, FF]), view(space8, 0, [E2, FF])]
        w2_sb = [[view(space4, E2 * FF, [E2, FC, D])[:, j] for j in range(E2)],
                 [view(space3, 1024 * (1 + j // 2 * 2) + (j % 2) * FC * D, [FC, D]) for j in range(E2)]]
        probs = view(space4, 0, [2, QB, S])
        ET = view(space4, 0, [QPG, 16, P])
        qf = [view(space5, 0, [S]), view(space5, S, [S]), view(space6, 0, [S]), view(space6, S, [S])]
        rest = view(space5, 1024, [2, S])
        v_heads = view(space5, 2048, [TC, NH, 32])
        OT = view(space5, 0, [G, B, P])
        kv_in = view(space6, 0, [2, TC, D])
        kvT = view(space6, 1024, [2, S])
        k_rest = view(space6, 2048, [2, S])
        k_parts = view(space6, 3072, [PARTS, S], BF16)
        A = view(space6, 0, [G, B, D])
        k_plain = view(space7, 0, [4, S], BF16, KPAD)
        k_shift = view(space7, 1024, [4, S], BF16, KPAD)
        SM = view(space8, 0, [16, P])
        lsub, gexp, eq, cum, place = (view(space8, k * T * E, [T * E]) for k in range(5))
        tot, incl = (view(space8, k * T * E, [E, B, G]) for k in (5, 6))
        den_sb = sb("den_sb", [P, D])
        st6p = sb("st6p", [P, B, 6])
        smallp = sb("smallp", [P, 5, B])
        neg_half = sb("neg_half", [P, B])

        v_tmp = sb("v_tmp", [P, TC, D])
        v_head = sb("v_head", [P, 2, TC, 32])
        row_max = sb("row_max", [P, 2, QB * TC])
        max_rest = sb("max_rest", [P, 2, QB * TC])
        max_parts = sb("max_parts", [P, 2, PARTS, QB * TC], BF16)
        max_turned = sb("max_turned", [PARTS * QB * TC, 2, P], BF16)
        attended = sb("attended", [P, 2, S])
        st6 = sb("st6", [P, B, 6])
        small = sb("small", [P, 5, B])
        SC = sb("SC", [P, 2 * G, 16, B])
        PC = sb("PC", [P, 2 * G, 16, B])
        mx, sm2 = sb("mx", [P, 2 * G, 16]), sb("sm2", [P, 2 * G, 16])
        lmax, gate = sb("lmax", [P, T]), sb("gate", [P, T])
        weight = sb("weight", [P, T * E])
        mask1 = sb("mask1", [P, T * E], BF16)
        logits = sb("logits", [P, T * E])

        s_x = [sem(f"x_loaded{u}") for u in range(4)]
        s_kv, s_w, s_b, s_bc = (sem(n) for n in ("kv_loaded", "w_loaded", "b_loaded", "bv_row_loaded"))
        s_w12 = [sem("w12_loaded0"), sem("w12_loaded1")]
        s_bin, s_b1, s_b2, s_rows = sem("in_proj_b_loaded"), sem("b1_loaded"), sem("b2_loaded"), sem("rows_loaded")
        s_passed_pool, s_passed_dve, s_passed_pe, s_passed_act = (sem(f"passed_{n}") for n in ("pool", "dve", "pe", "act"))
        s_const = sem("constants_set")
        s_pc, s_dc = sem("pool_chain"), sem("dve_chain")
        s_wt, s_wtc = sem("w_turned"), sem("wT_copied")
        s_kvt, s_kvtc = sem("kv_turned"), sem("kvT_copied")
        s_kp, s_kpe = sem("k_projected"), sem("k_evacuated")
        s_vp, s_vpe = sem("v_projected"), sem("v_evacuated")
        s_ks, s_kst = sem("k_split"), sem("k_stored")
        s_xn, s_xt, s_xtc = sem("x_normed"), sem("x_turned"), sem("xT_copied")
        s_qp, s_qe, s_qs, s_qst = sem("q_projected"), sem("q_evacuated"), sem("q_split"), [sem("q_stored0"), sem("q_stored1")]
        s_var, s_sd = sem("variance_ready"), sem("deviation_ready")
        s_vb = sem("v_biased")
        s_vset = sem("v_heads_set")
        s_ql = [sem(f"stack_loaded{j}") for j in range(4)]
        s_full, s_free = sem("rows_scored"), sem("rows_reduced")
        s_split, s_shift = sem("max_split"), sem("shift_loaded")
        s_sc, s_pr = sem("columns_scored"), sem("probs_ready")
        s_v = sem("v_head_ready")
        s_pv, s_pve = sem("pv_ready"), sem("pv_evacuated")
        s_ast = [sem("attended_stored0"), sem("attended_stored1")]

        (s_al, s_dl, s_rc, s_rs, s_rb, s_r1, s_st, s_r2, s_n2, s_n2l, s_r3) = (sem(n) for n in
            ("attended_loaded", "denominators_loaded", "inverses_ready", "inverses_stored", "inverses_loaded",
             "residual1_added", "statistics_ready", "residual2_added", "encoder_input_ready", "last_encoder_input_ready", "out_bias_added"))
        (s_b1t, s_b1c, s_w1t, s_w1c, s_wu, s_Wc) = (sem(n) for n in
            ("b1_turned", "b1T_copied", "w1_turned", "w1T_copied", "w12_multiplied", "W_copied"))
        (s_bw, s_csum, s_csplit, s_cl, s_q13) = (sem(n) for n in
            ("b1_w2_multiplied", "c_row_ready", "c_split", "c_loaded", "q_stack13_cleared"))
        (s_t, s_yt, s_pj, s_qkv) = (sem(n) for n in ("tokens_turned", "tokensT_copied", "qkv_projected", "qkv_copied"))
        (s_s2, s_msk, s_sub, s_e2, s_soft) = (sem(n) for n in
            ("scores2_ready", "scores2_masked", "scores2_less_max", "exp2_done", "softmax2_done"))
        (s_ex, s_ext, s_et, s_av, s_ot) = (sem(n) for n in
            ("probs2_spread", "probs2_turned", "probs2T_copied", "attended2_ready", "attended2_copied"))
        (s_op, s_res, s_n3, s_y1, s_y1l, s_y1t, s_y1c, s_lg, s_lgc, s_oh, s_ge, s_cnt, s_gate) = (sem(n) for n in
            ("out_projected", "residual3_added", "norm3_done", "y1_ready", "y1_last_ready", "y1_turned", "y1T_copied",
             "logits_ready", "logits_copied", "expert_masks_ready", "gate_exp_done", "tokens_counted", "weights_ready"))
        (s_xp, s_wd, s_wa, s_sp, s_sv, s_i4, s_n4, s_aff, s_i5, s_n5, s_y2, s_y2l, s_out) = (sem(n) for n in
            ("experts_done", "weighed_by_dve", "weighed_by_act", "summed_by_pool", "summed_by_dve", "norm4_scale_ready",
             "norm4_done", "affine2_done", "norm5_scale_ready", "norm5_done", "output_ready", "last_output_ready", "output_stored"))

        same = lambda t: t.rearrange("p a b -> p (a b)")

        UNITS = [[(g, b) for g in gs for b in bs] for bs in (range(0, QB), range(QB, B)) for gs in (range(0, 2), range(2, 4))]
        x_tok = x.rearrange("b (g p) f -> g p b f", p=P)
        out_tok = out.rearrange("b (g p) f -> g p b f", p=P)

        def norm_variance(dve, ch, src, st6, small):
            for b in range(B):
                ins = dve.bn_stats(st6[:, b, :], src(b))
            ch.done(ins)
            ch.wait()
            me, m2e, mo, m2o = (st6[:, :, j] for j in (1, 2, 4, 5))
            mean, diff, var = (small[:, j, :] for j in range(3))
            ch.done(dve.tensor_tensor(mean, me, mo, ADD))
            ch.done(dve.tensor_tensor(diff, me, mo, SUB))
            ch.done(dve.tensor_tensor(var, m2e, m2o, ADD))
            ch.wait()
            ch.done(dve.scalar_tensor_tensor(small[:, 4, :], diff, D / 4.0, diff, MUL, MUL))
            ch.done(dve.tensor_scalar(mean, mean, 0.5, None, MUL))
            ch.wait()
            ch.done(dve.tensor_tensor(var, var, small[:, 4, :], ADD))
            ch.wait()
            dve.tensor_scalar(var, var, 1.0 / D, EPS, MUL, ADD).then_inc(s_var, 1)

        def norm_invert(dve, ch, k, small):
            dve.wait_ge(s_sd, k + 1)
            ch.done(dve.reciprocal(small[:, 3, :], small[:, 2, :]))
            ch.wait()

        def norm_apply(dve, src, dst, small, which=range(B)):
            for b in which:
                ins = dve.tensor_scalar(dst(b), src(b), small[:, 0, b:b + 1], small[:, 3, b:b + 1], SUB, MUL)
            return ins

        def norm(dve, ch, k, src, dst):
            norm_variance(dve, ch, src, st6, small)
            norm_invert(dve, ch, k, small)
            return norm_apply(dve, src, dst, small)

        def tiles(t, g):
            return lambda b: t[:, g, b, :]

        LAST1, LAST2, NORM4 = G + 1, G + 2, 2 * G + 2
        LN1 = [G] + [G + 2 + g for g in range(1, G)]
        NORM = 8

        def root(act, k, small=small):
            act.wait_ge(s_var, k + 1)
            act.activation(small[:, 2, :], small[:, 2, :], ACT.Sqrt).then_inc(s_sd, 1)


        def project_q(act, b):
            act.wait_ge(s_qp, b + 1)
            if b >= QB:
                act.wait_ge(s_qs, b - QB + 1)
            act.activation(qf[b % QB], ps[:, b % QB, :], ACT.Relu, bias=bias_col[:, 0:1])
            act.activation(q_parts[:, 0, b * S:(b + 1) * S], ps[:, b % QB, :], ACT.Relu,
                           bias=bias_col[:, 0:1]).then_inc(s_qe, 1)

        W1T_BANK, W_BANK, C_BANK = 6, 5, 4

        def turn_b1(pe):
            for c in range(FC):
                mm = pe.transpose(ps[:, C_BANK, c * E:(c + 1) * E], b1_sb[:, c * P:(c + 1) * P], ident[0:E, 0:E])
            mm.then_inc(s_b1t, 1)

        def fold_weights(pe, r):
            pe.wait_ge(s_w12[r], 32 + 16 * r)

            def turn_w1(e):
                if e >= 2:
                    pe.wait_ge(s_w1c, e - 1)
                for c in range(FC):
                    mm = pe.transpose(ps[:, W1T_BANK + e % 2, c * P:(c + 1) * P],
                                      w1_sb[r][:, e % E2, c * P:(c + 1) * P], ident[:])
                mm.then_inc(s_w1t, 1)

            turn_w1(E2 * r)
            pe.wait_ge(s_b1c, 1)
            for j in range(E2):
                e = E2 * r + j
                if j + 1 < E2:
                    turn_w1(e + 1)
                pe.wait_ge(s_w1c, e + 1)
                if j == 0 and r:
                    pe.wait_ge(s_Wc, r)
                for c in range(FC):
                    mm = pe.matmul(ps[:, W_BANK, j * D:(j + 1) * D], w1T[:, e % 2, c, :], w2_sb[r][j][:, c, :],
                                   start=(c == 0), stop=(c == FC - 1))
                mm.then_inc(s_wu, 1)
            for c in range(FC):
                for j in range(E2):
                    mm = pe.matmul(ps[32 * j:32 * j + 32, C_BANK, P * (1 + r):P * (2 + r)], b1T[:, c, E2 * r + j, :],
                                   w2_sb[r][j][:, c, :], start=(c == 0), stop=(c == FC - 1))
            mm.then_inc(s_bw, 1)

        def copy_weights(act, r):
            if r == 0:
                act.wait_ge(s_b1t, 1)
                act.wait_ge(s_const, 8)
                act.copy(b1T[:].rearrange("p c e z -> p (c e) z")[:, :, 0:1],
                         ps[:, C_BANK, 0:FC * E].rearrange("p (k o) -> p k o", o=1)).then_inc(s_b1c, 1)
            for e in range(E2 * r, E2 * r + E2):
                act.wait_ge(s_w1t, e + 1)
                if e >= 2:
                    act.wait_ge(s_wu, e - 1)
                act.copy(w1T[:, e % 2], ps[:, W1T_BANK + e % 2, :]).then_inc(s_w1c, 1)
                if e == 5:
                    root(act, 3)

        def copy_folded(act, r):
            act.wait_ge(s_wu, E2 * (r + 1))
            act.copy(W[:, E2 * r:E2 * r + E2].rearrange("p e d -> p (e d)"), ps[:, W_BANK, :]).then_inc(s_Wc, 1)

        def bcast(row, k):
            return row.rearrange("p (o f) -> p o f", o=1).broadcast_to([P, k, D])

        def back_end_sp(sp):
            for g in range(G):
                if g < G - 1:
                    sp.wait_ge(s_y2, g + 1)
                else:
                    sp.wait_ge(s_y2l, 1)
                sp.dma_start(out_tok[g], A[:, g]).then_inc(s_out, 16)
            sp.wait_ge(s_out, 16 * G)

        def pool_norm(pool, ch, src, dst):
            me, m2e, mo, m2o = (st6p[:, :, j] for j in (1, 2, 4, 5))
            mean, diff, var, inv, square = (smallp[:, j, :] for j in range(5))
            ch.done(pool.tensor_tensor(mean, me, mo, ADD))
            ch.done(pool.tensor_tensor(diff, me, mo, SUB))
            ch.done(pool.tensor_tensor(var, m2e, m2o, ADD))
            ch.wait()
            ch.done(pool.tensor_tensor(square, diff, diff, MUL))
            ch.done(pool.tensor_scalar(mean, mean, 0.5, None, MUL))
            ch.wait()
            ch.done(pool.tensor_scalar(square, square, D / 4.0, None, MUL))
            ch.wait()
            ch.done(pool.tensor_tensor(var, var, square, ADD))
            ch.wait()
            ch.done(pool.tensor_scalar(var, var, 1.0 / D, EPS, MUL, ADD))
            ch.wait()
            ch.done(pool.tensor_tensor(inv, var, neg_half[:], ALU.pow))
            ch.wait()
            over_f = lambda v: v.rearrange("p (b o) -> p b o", o=1).broadcast_to([P, B, D])
            ch.done(pool.tensor_tensor(dst, src, over_f(mean), SUB))
            ch.wait()
            return pool.tensor_tensor(dst, dst, over_f(inv), MUL)

        def pool_divide(pool, ch, g):
            hold(pool, s_al, 64 * (g + 1), s_passed_pool)
            hold(pool, s_rb, 64 * (g + 1), s_passed_pool)
            ch.done(pool.tensor_tensor(A[:, g], A[:, g], INV, MUL))
            ch.wait()
            pool.tensor_tensor(A[:, g], A[:, g], XN[:, g], ADD).then_inc(s_r1, 1)

        def pool_residual(pool, ch, g):
            hold(pool, s_st, 2 * g + 1, s_passed_pool)
            ch.done(pool_norm(pool, ch, A[:, g], A[:, g]))
            ch.wait()
            pool.tensor_tensor(X[:, g], X[:, g], A[:, g], ADD).then_inc(s_r2, 1)

        def pool_input(pool, ch, g):
            hold(pool, s_st, 2 * g + 2, s_passed_pool)
            pool_norm(pool, ch, X[:, g], A[:, g]).then_inc(s_n2, 1)
            hold(pool, s_n2, g + 1, s_passed_pool)
            pool.tensor_tensor(XN[:, g], A[:, g], bcast(rows[:, 4, :], B), ADD).then_inc(s_r3, 1)

        def dve_invert(dve, g):
            dve.wait_ge(s_dl, 64 * (g + 1))
            dve.reciprocal(den_sb[:], den_sb[:]).then_inc(s_rc, 1)

        def dve_statistics(dve, ready, g, src, tc):
            if tc == 0:
                hold(dve, ready, g + 1, s_passed_dve)
            for b in (2 * tc, 2 * tc + 1):
                ins = dve.bn_stats(st6p[:, b, :], src[:, g, b, :])
            if tc == TC - 1:
                ins.then_inc(s_st, 1)

        def back_end_pool(pool, ch):

            def spread(g, half):
                q = QPG * g + half
                hold(pool, s_soft, q + 1, s_passed_pool)
                if not isinstance(g, int):
                    hold(pool, s_ext, 2 * q - 2, s_passed_pool)
                for h in range(NH2):
                    pool.tensor_tensor(
                        EX[:, half, 4 * h:4 * h + 4, :].rearrange("p t (m n) -> p t m n", n=16),
                        PC[:, q, 4 * h:4 * h + 4, :].rearrange("p t (m o) -> p t m o", o=1).broadcast_to([P, 4, B, 16]),
                        same_row[:].rearrange("p (o m n) -> p o m n", o=1, n=16).broadcast_to([P, 4, B, 16]),
                        MUL).then_inc(s_ex, 1)

            spread(0, 0)
            pool_divide(pool, ch, G - 1)
            spread(0, 1)
            with pool.Fori(1, G) as g:
                ch.enter(g - 1, 1)
                spread(g, 0)
                spread(g, 1)
                hold(pool, s_n3, g, s_passed_pool)
                ch.done(pool.tensor_tensor(A[:, g - 1], A[:, g - 1], bcast(rows[:, 0, :], B), MUL))
                ch.wait()
                pool.tensor_tensor(A[:, g - 1], A[:, g - 1], bcast(rows[:, 1, :], B), ADD).then_inc(s_y1, 1)
            ch.leave(G - 1)
            pool.wait_ge(s_n2l, 1)
            pool.tensor_tensor(XN[:, G - 1], A[:, G - 1], bcast(rows[:, 4, :], B), ADD).then_inc(s_r3, 1)

            def add_up(g, b):
                if b in DVE_WEIGHS:
                    hold(pool, s_wd, count(DVE_WEIGHS, g, b), s_passed_pool)
                else:
                    hold(pool, s_wa, count(ACT_WEIGHS, g, b), s_passed_pool)
                e = SE[:, b % 4]
                ch.done(pool.tensor_tensor(e[:, 0:4, :], e[:, 0:4, :], e[:, 4:8, :], ADD))
                ch.wait()
                ch.done(pool.tensor_tensor(e[:, 0:2, :], e[:, 0:2, :], e[:, 2:4, :], ADD))
                ch.wait()
                ch.done(pool.tensor_tensor(e[:, 0, :], e[:, 0, :], e[:, 1, :], ADD))
                ch.wait()
                pool.tensor_tensor(A[:, g, b, :], A[:, g, b, :], e[:, 0, :], ADD).then_inc(s_sp, 1)

            def affine(g):
                hold(pool, s_n4, g + 1, s_passed_pool)
                ch.done(pool.tensor_tensor(A[:, g], A[:, g], bcast(rows[:, 2, :], B), MUL))
                ch.wait()
                pool.tensor_tensor(A[:, g], A[:, g], bcast(rows[:, 3, :], B), ADD).then_inc(s_aff, 1)

            def last_residual(g):
                hold(pool, s_n5, g + 1, s_passed_pool)
                pool.tensor_tensor(same(A[:, g]), same(A[:, g]), same(X[:, g]), ADD).then_inc(s_y2, 1)

            def group(g, norm4, norm5):
                for b in POOL_SUMS:
                    add_up(g, b)
                    if b == 5 and norm4 and g < G - 1:
                        affine(g - 1)
                if norm5:
                    last_residual(g - 2)

            group(0, False, False)
            group(1, True, False)
            for g in range(2, G):
                group(g, True, True)
            last_residual(G - 2)

        EXPERT_BANKS = [4, 6, 2, 0]

        def back_end_pe(pe):
            def turn(src, banks, done):
                for b in range(B):
                    mm = pe.transpose(ps[:, banks + b // 4, (b % 4) * P:(b % 4 + 1) * P], src[:, b, :], ident[:])
                mm.then_inc(done, 1)

            def turn_tokens(g, bank=4):
                if g < G - 1:
                    pe.wait_ge(s_n2, g + 1)
                else:
                    pe.wait_ge(s_n2l, 1)
                turn(A[:, g], bank, s_t)

            def project(g, bank=4):
                pe.wait_ge(s_yt, 2 * g + 2)
                if g >= 2:
                    pe.wait_ge(s_res, g - 1)
                for j, first in ((3, bank + 2), (4, bank)):
                    for half in range(2):
                        mm = pe.matmul(ps[:, first + half, :], wT[:, j, :], same(YT[:, g])[:, half * 512:half * 512 + 512],
                                       start=True, stop=True)
                    mm.then_inc(s_pj, 1)
                pe.wait_ge(s_qkv, 3 * g + 1)
                for t in range(NT):
                    mm = pe.matmul(ps[:, bank + 2 + t // 4, (t % 4) * P:(t % 4 + 1) * P], YT[:, g, t, :],
                                   wT[:, 5, :], start=True, stop=True)
                mm.then_inc(s_pj, 1)

            def scores2(q):
                g, half = q // QPG, q % QPG
                if q >= 1:
                    pe.wait_ge(s_msk, q)
                for t in range(4):
                    for h in range(NH2):
                        rows_h = slice(HD2 * h, HD2 * h + HD2)
                        mm = pe.matmul(ps[:, h, t * P:(t + 1) * P], QF[rows_h, g % 2, 4 * half + t, :],
                                       KF[rows_h, g % 2, 4 * half + t, :], start=True, stop=True)
                mm.then_inc(s_s2, 1)

            def route(g, bank):
                pe.wait_ge(s_y1c, 2 * g + 2)
                for b in range(B):
                    mm = pe.matmul(ps[:, bank, b * E:(b + 1) * E], YT[:, g, b, :], wg_sb[:], start=True, stop=True)
                mm.then_inc(s_lg, 1)

            pe.wait_ge(s_rows, 16 * 6)
            pe.wait_ge(s_pve, NQ)
            pe.wait_ge(s_pr, NQ * 16)
            turn_tokens(0)
            turn_tokens(1, 0)
            project(0)
            project(1, 0)
            pe.wait_ge(s_qkv, 3 * 2)
            scores2(0)
            scores2(1)
            for q in range(2 * G):
                g, half = q // QPG, q % QPG
                for pair in range(2):
                    pe.wait_ge(s_ex, NH2 * q + 2 * (pair + 1))
                    if pair == 0 and q >= 1:
                        pe.wait_ge(s_ot, q)
                    if pair == 0 and q >= 4 and q % 2 == 0:
                        pe.wait_ge(s_lgc, q // 2 - 1)
                    if pair == 1 and q >= 2 and q % 2 == 0:
                        pe.wait_ge(s_res, q // 2)
                    if pair == 1 and q >= 3 and q % 2 == 1:
                        pe.wait_ge(s_y1c, 2 * (q // 2))
                    for k in range(8):
                        mm = pe.transpose(ps[:, 4 + 2 * pair + k // 4, (k % 4) * P:(k % 4 + 1) * P],
                                          EX[:, half, 8 * pair + k, :], ident[:])
                    mm.then_inc(s_ext, 1)
                if q + 2 < 2 * G:
                    scores2(q + 2)
                pe.wait_ge(s_et, 2 * q + 2)
                for t in range(4):
                    for h in range(NH2):
                        mm = pe.matmul(ps[HD2 * h:HD2 * h + HD2, 4, t * P:(t + 1) * P],
                                       VT[:, g % 2, 4 * half + t, HD2 * h:HD2 * h + HD2], ET[:, half, 4 * h + t, :],
                                       start=True, stop=True)
                mm.then_inc(s_av, 1)
                if half == 0 and g >= 1:
                    pe.wait_ge(s_y1, g)
                    turn(A[:, g - 1], 6, s_y1t)
                if half == 1:
                    pe.wait_ge(s_ot, q + 1)
                    for b in range(B):
                        mm = pe.matmul(ps[:, 6 + b // 4, (b % 4) * P:(b % 4 + 1) * P], OT[:, g, b, :], wT[:, 6, :],
                                       start=True, stop=True)
                    mm.then_inc(s_op, 1)
                    if g + 2 < G:
                        turn_tokens(g + 2)
                        project(g + 2)
                        pe.wait_ge(s_qkv, 3 * (g + 2) + 3)
                    if g >= 1:
                        route(g - 1, 5)

            def experts(t):
                bank = EXPERT_BANKS[t % 4]
                for half in range(2):
                    pe.matmul(ps[:, bank + half, :], ones_stack[:], c_stack[:, half * 512:half * 512 + 512],
                              start=True, stop=False)
                    mm = pe.matmul(ps[:, bank + half, :], YT[:, t // B, t % B, :],
                                   W[:].rearrange("p e d -> p (e d)")[:, half * 512:half * 512 + 512],
                                   start=False, stop=True)
                mm.then_inc(s_xp, 1)

            pe.wait_ge(s_cl, 16 * E2)
            pe.wait_ge(s_lgc, G - 1)
            experts(0)
            pe.wait_ge(s_res, G)
            experts(1)
            pe.wait_ge(s_msk, 2 * G)
            experts(2)
            for half in range(2):
                pe.wait_ge(s_y1l, half + 1)
                for b in range(QB):
                    mm = pe.transpose(ps[:, half, b * P:(b + 1) * P], A[:, G - 1, QB * half + b, :], ident[:])
                mm.then_inc(s_y1t, 1)
            route(G - 1, 0)
            pe.wait_ge(s_lgc, G)
            pe.wait_ge(s_oh, 1)
            pe.matmul(ps[:, 0, 0:T * E], upper[:], mask1[:], start=True, stop=True)
            pe.matmul(ps[:, 1, 0:T * E], all_ones[:], mask1[:], start=True, stop=True).then_inc(s_cnt, 1)
            pe.wait_ge(s_gate, 1)
            for t in range(3, T):
                if t >= 4:
                    g, b = four_back(t // B, t % B)
                    if b in DVE_WEIGHS:
                        pe.wait_ge(s_wd, count(DVE_WEIGHS, g, b))
                    else:
                        pe.wait_ge(s_wa, count(ACT_WEIGHS, g, b))
                experts(t)

        def back_end_act(act):
            def copy_tokens(g, bank=4):
                act.wait_ge(s_t, g + 1)
                for half in range(2):
                    act.copy(YT_tiles[:, g, :, 4 * half:4 * half + 4, :].rearrange("p t b n -> p b t n"),
                             ps[:, bank + half, :].rearrange("p (b t n) -> p b t n", b=4, n=16)).then_inc(s_yt, 1)

            def project(g, between=None, bank=4):
                for j, dst, first in ((0, QF, bank + 2), (1, KF, bank)):
                    act.wait_ge(s_pj, 3 * g + j + 1)
                    act.activation(same(dst[:, g % 2]), ps[:, first:first + 2, :].rearrange("p a b -> p (a b)"),
                                   ACT.Identity, bias=bias_col[:, 3 + j:4 + j]).then_inc(s_qkv, 1)
                    if j == 0 and between:
                        between()
                act.wait_ge(s_pj, 3 * g + 3)
                act.copy(same(VT[:, g % 2]), ps[:, bank + 2:bank + 4, :].rearrange("p a b -> p (a b)")).then_inc(s_qkv, 1)

            copy_tokens(0)
            copy_tokens(1, 0)
            project(0)
            project(1, bank=0)

            def copy_y1(g, bank):
                act.wait_ge(s_y1t, g + 1)
                for half in range(2):
                    act.copy(same(YT[:, g, 4 * half:4 * half + 4]), ps[:, bank + half, :]).then_inc(s_y1c, 1)

            def copy_logits(g, bank):
                act.wait_ge(s_lg, g + 1)
                act.copy(logits[:, g * B * E:(g + 1) * B * E], ps[:, bank, 0:B * E]).then_inc(s_lgc, 1)

            def softmax_exp(q):
                act.wait_ge(s_sub, q + 1)
                act.activation(PC[:, q].rearrange("p a b -> p (a b)"), SC[:, q].rearrange("p a b -> p (a b)"),
                               ACT.Exp, scale=1.0 / math.sqrt(HD2)).then_inc(s_e2, 1)

            softmax_exp(0)
            softmax_exp(1)
            for q in range(2 * G):
                g, half = q // QPG, q % QPG

                for pair in range(2):
                    act.wait_ge(s_ext, 2 * q + pair + 1)
                    act.copy(ET[:, half, 8 * pair:8 * pair + 8, :].rearrange("p a b -> p (a b)"),
                             ps[:, 4 + 2 * pair:6 + 2 * pair, :].rearrange("p a b -> p (a b)")).then_inc(s_et, 1)
                act.wait_ge(s_av, q + 1)
                for t in range(4):
                    n0 = 16 * (4 * half + t)
                    ins = act.activation(OT[:, g, :, n0:n0 + 16], ps[:, 4, t * P:(t + 1) * P].rearrange("p (l n) -> p l n", n=16),
                                         ACT.Identity, bias=bias_col[:, 5:6])
                ins.then_inc(s_ot, 1)
                if q == 2:
                    root(act, LAST2)
                if half == 0 and g >= 1:
                    copy_y1(g - 1, 6)
                if q + 2 < 2 * G:
                    softmax_exp(q + 2)
                if half == 1:
                    if g + 2 < G:
                        copy_tokens(g + 2)
                        project(g + 2, lambda: root(act, LN1[g]))
                    else:
                        root(act, LN1[g])
                    if g == 0:
                        root(act, LAST1)
                    if g >= 1:
                        copy_logits(g - 1, 5)
            for half in range(2):
                act.wait_ge(s_y1t, G + half)
                act.copy(same(YT[:, G - 1, QB * half:QB * half + QB]), ps[:, half, :]).then_inc(s_y1c, 1)
            copy_logits(G - 1, 0)
            act.wait_ge(s_oh, 1)
            act.activation(gexp[:], lsub[:], ACT.Exp).then_inc(s_ge, 1)
            act.wait_ge(s_gate, 1)

            def weigh(g, b):
                hold(act, s_xp, B * g + b + 1, s_passed_act)
                g4, b4 = four_back(g, b)
                if not (isinstance(g4, int) and g4 < 0):
                    if b4 in POOL_SUMS:
                        hold(act, s_sp, count(POOL_SUMS, g4, b4), s_passed_act)
                    else:
                        hold(act, s_sv, count(DVE_SUMS, g4, b4), s_passed_act)
                bank = EXPERT_BANKS[b % 4]
                for e in range(E):
                    ins = act.activation(SE[:, b % 4, e, :], ps[:, bank + e // 4, (e % 4) * D:(e % 4 + 1) * D],
                                         ACT.Copy, scale=weight[:, bass_ds((g * B + b) * E + e, 1)])
                ins.then_inc(s_wa, 1)

            def apply(g, ready, scale, done, which=range(B)):
                hold(act, ready, g + 1, s_passed_act)
                for b in which:
                    ins = act.activation(A[:, g, b, :], A[:, g, b, :], ACT.Identity, scale=scale[:, 3, b:b + 1],
                                         bias=scale[:, 4, b:b + 1])
                ins.then_inc(done, 1)

            k4 = lambda g: NORM4 + 2 * g
            k5 = lambda g: NORM4 + 2 * g + 1

            def group(g, norm4, norm5):
                for b in ACT_WEIGHS:
                    weigh(g, b)
                    if b == ACT_WEIGHS[1] and norm5:
                        root(act, k5(g - 2), smallp)
                    if b == ACT_WEIGHS[1] and norm4:
                        root(act, k4(g - 1))
                    if b == ACT_WEIGHS[2] and norm4:
                        apply(g - 1, s_i4, small, s_n4)
                if norm5:
                    apply(g - 2, s_i5, smallp, s_n5)

            group(0, False, False)
            group(1, True, False)
            with act.Fori(2, G) as g:
                group(g, True, True)
            root(act, k5(G - 2), smallp)
            root(act, k4(G - 1))
            apply(G - 1, s_i4, small, s_n4, range(0, B, 2))
            apply(G - 2, s_i5, smallp, s_n5)
            root(act, k5(G - 1), smallp)
            apply(G - 1, s_i5, smallp, s_n5, range(0, B, 2))

        def back_end_dve(dve, ch):
            def compact(q):
                hold(dve, s_s2, q + 1, s_passed_dve)
                dve.tensor_tensor(SM[:], ps[:, 0:4, :].rearrange("p a (t f) -> p (a t) f", f=P),
                                  bcast(same_row[:], 16), MUL).then_inc(s_msk, 1)
                hold(dve, s_msk, q + 1, s_passed_dve)
                ch.done(dve.tensor_reduce(SC[:, q], SM[:].rearrange("p a (m n) -> p a m n", n=16), AX.X, ADD))
                ch.wait()
                ch.done(dve.tensor_reduce(mx[:, q], SC[:, q], AX.X, MAX))
                ch.wait()
                dve.tensor_tensor(SC[:, q], SC[:, q], mx[:, q].rearrange("p (a o) -> p a o", o=1).broadcast_to([P, 16, B]),
                                  SUB).then_inc(s_sub, 1)

            def normalise(q):
                hold(dve, s_e2, q + 1, s_passed_dve)
                ch.done(dve.tensor_reduce(sm2[:, q], PC[:, q], AX.X, ADD))
                ch.wait()
                ch.done(dve.reciprocal(sm2[:, q], sm2[:, q]))
                ch.wait()
                dve.tensor_tensor(PC[:, q], PC[:, q], sm2[:, q].rearrange("p (a o) -> p a o", o=1).broadcast_to([P, 16, B]),
                                  MUL).then_inc(s_soft, 1)

            def ln1(g, k):
                hold(dve, s_op, g + 1, s_passed_dve)
                dve.tensor_tensor(same(A[:, g]), ps[:, 6:8, :].rearrange("p a b -> p (a b)"), same(XN[:, g]),
                                  ADD).then_inc(s_res, 1)
                hold(dve, s_res, g + 1, s_passed_dve)
                return norm(dve, ch, k, tiles(A, g), tiles(A, g))

            for q in range(2 * QPG):
                compact(q)
                normalise(q)
            ln1(0, LN1[0]).then_inc(s_n3, 1)
            last = G - 1
            dve.wait_ge(s_r1, G)
            ch.done(norm(dve, ch, LAST1, tiles(A, last), tiles(A, last)))
            ch.wait()
            ch.done(dve.tensor_tensor(X[:, last], X[:, last], A[:, last], ADD))
            ch.wait()
            norm(dve, ch, LAST2, tiles(X, last), tiles(A, last)).then_inc(s_n2l, 1)
            for g in range(2, G):
                for half in range(QPG):
                    compact(2 * g + half)
                    normalise(2 * g + half)
                ln1(g - 1, LN1[g - 1]).then_inc(s_n3, 1)
            g = G - 1
            dve.wait_ge(s_r3, G)
            dve.wait_ge(s_op, G)
            dve.tensor_tensor(same(A[:, g]), ps[:, 6:8, :].rearrange("p a b -> p (a b)"), same(XN[:, g]),
                              ADD).then_inc(s_res, 1)
            dve.wait_ge(s_res, G)
            norm_variance(dve, ch, tiles(A, g), st6, small)
            norm_invert(dve, ch, LN1[g], small)
            for lo in (0, QB):
                bs = range(lo, lo + QB)
                half = A[:, g, lo:lo + QB]
                ch.done(norm_apply(dve, tiles(A, g), tiles(A, g), small, bs))
                ch.wait()
                ch.done(dve.tensor_tensor(half, half, bcast(rows[:, 0, :], QB), MUL))
                ch.wait()
                dve.tensor_tensor(half, half, bcast(rows[:, 1, :], QB), ADD).then_inc(s_y1l, 1)
            dve.wait_ge(s_lgc, G)
            L = logits[:].rearrange("p (t e) -> p t e", e=E)
            over_e = lambda v: v[:].rearrange("p (t o) -> p t o", o=1).broadcast_to([P, T, E])
            ch.done(dve.tensor_reduce(lmax[:], L, AX.X, MAX))
            ch.wait()
            ch.done(dve.tensor_tensor(lsub[:].rearrange("p (t e) -> p t e", e=E), L, over_e(lmax), SUB))
            ch.wait()
            ch.done(dve.tensor_scalar(eq[:], lsub[:], 0.0, None, ALU.is_equal))
            ch.wait()
            ch.done(dve.tensor_tensor_scan(cum[:], first_e[:], eq[:], 0.0, MUL, ADD))
            ch.wait()
            dve.scalar_tensor_tensor(mask1[:], cum[:], 1.0, eq[:], ALU.is_equal, MUL).then_inc(s_oh, 1)
            dve.wait_ge(s_ge, 1)
            ch.done(dve.tensor_reduce(gate[:], gexp[:].rearrange("p (t e) -> p t e", e=E), AX.X, ADD))
            ch.wait()
            ch.done(dve.reciprocal(gate[:], gate[:]))
            dve.wait_ge(s_cnt, 1)
            tot_src = ps[:, 1, 0:T * E].rearrange("p (g b e) -> p e b g", g=G, e=E)
            for e in range(E):
                ins = dve.tensor_copy(tot[:, e], tot_src[:, e])
            ch.done(ins)
            ch.wait()
            flat = lambda v: v[:].rearrange("p e b g -> p (e b g)")
            ch.done(dve.tensor_tensor_scan(flat(incl), first_t[:], flat(tot), 0.0, MUL, ADD))
            ch.wait()
            ch.done(dve.tensor_tensor(flat(incl), flat(incl), flat(tot), SUB))
            ch.wait()
            for g in range(G):
                ins = dve.tensor_tensor(place[:].rearrange("p (g b e) -> p g b e", g=G, e=E)[:, g],
                                        ps[:, 0, 0:T * E].rearrange("p (g b e) -> p g b e", g=G, e=E)[:, g],
                                        incl[:, :, :, g].rearrange("p e b -> p b e"), ADD)
            ch.done(ins)
            ch.wait()
            ch.done(dve.scalar_tensor_tensor(place[:], place[:], CAP + 0.5, mask1[:], ALU.is_lt, MUL))
            ch.wait()
            dve.tensor_tensor(weight[:].rearrange("p (t e) -> p t e", e=E), place[:].rearrange("p (t e) -> p t e", e=E),
                              over_e(gate), MUL).then_inc(s_gate, 1)
            dve.wait_ge(s_gate, 1)

            def tile(g, b):
                if b in DVE_WEIGHS:
                    hold(dve, s_xp, B * g + b + 1, s_passed_dve)
                    g4, b4 = four_back(g, b)
                    if b4 in POOL_SUMS and not (isinstance(g4, int) and g4 < 0):
                        hold(dve, s_sp, count(POOL_SUMS, g4, b4), s_passed_dve)
                    bank = EXPERT_BANKS[b % 4]
                    dve.tensor_tensor(SE[:, b % 4], ps[:, bank:bank + 2, :].rearrange("p a (e d) -> p (a e) d", d=D),
                                      weight[:, bass_ds((g * B + b) * E, E)].rearrange("p (e o) -> p e o", o=1).broadcast_to([P, E, D]),
                                      MUL).then_inc(s_wd, 1)

            def sum_up(g, b):
                if b in DVE_WEIGHS:
                    hold(dve, s_wd, count(DVE_WEIGHS, g, b), s_passed_dve)
                else:
                    hold(dve, s_wa, count(ACT_WEIGHS, g, b), s_passed_dve)
                ch.done(dve.tensor_reduce(e_sum[:, DVE_SUMS.index(b)], SE[:, b % 4].rearrange("p e d -> p d e"), AX.X, ADD))
                ch.wait()
                dve.tensor_tensor(A[:, g, b, :], A[:, g, b, :], e_sum[:, DVE_SUMS.index(b)], ADD).then_inc(s_sv, 1)

            def shift(small):
                return dve.scalar_tensor_tensor(small[:, 4, :], small[:, 0, :], -1.0, small[:, 3, :], MUL, MUL)

            def variance4(g):
                hold(dve, s_sp, len(POOL_SUMS) * (g + 1), s_passed_dve)
                hold(dve, s_sv, len(DVE_SUMS) * (g + 1), s_passed_dve)
                if g >= 1:
                    dve.wait_ge(s_n4, g)
                norm_variance(dve, ch, tiles(A, g), st6, small)

            def scale4(g):
                norm_invert(dve, ch, NORM4 + 2 * g, small)
                shift(small).then_inc(s_i4, 1)

            def variance5(g, others_applied):
                hold(dve, s_aff, g + 1, s_passed_dve)
                if others_applied:
                    dve.wait_ge(s_n5, g)
                norm_variance(dve, ch, tiles(A, g), st6p, smallp)

            def scale5(g):
                norm_invert(dve, ch, NORM4 + 2 * g + 1, smallp)
                shift(smallp).then_inc(s_i5, 1)

            def group(g, norm4, norm5, others_applied=False):
                for b in range(B):
                    tile(g, b)
                    if b - 1 in DVE_SUMS:
                        sum_up(g, b - 1)
                    if b == 1 and norm5:
                        variance5(g - 2, others_applied)
                    if b == 2 and norm4:
                        variance4(g - 1)
                    if b == 3 and norm5:
                        scale5(g - 2)
                    if b == 4 and norm4:
                        scale4(g - 1)
                if B - 1 in DVE_SUMS:
                    sum_up(g, B - 1)

            group(0, False, False)
            group(1, True, False)
            for g in range(2, G):
                group(g, True, True, g > 2)
            def affine(g):
                ch.done(dve.tensor_tensor(A[:, g], A[:, g], bcast(rows[:, 2, :], B), MUL))
                ch.wait()
                dve.tensor_tensor(A[:, g], A[:, g], bcast(rows[:, 3, :], B), ADD).then_inc(s_aff, 1)

            g, odd = G - 1, range(1, B, 2)
            dve.wait_ge(s_n4, g)
            affine(g - 1)
            variance5(g - 1, True)
            variance4(g)
            scale5(g - 1)
            scale4(g)
            ch.done(norm_apply(dve, tiles(A, g), tiles(A, g), small, odd))
            ch.wait()
            dve.wait_ge(s_n4, G)
            affine(g)
            variance5(g, True)
            scale5(g)
            ch.done(norm_apply(dve, tiles(A, g), tiles(A, g), smallp, odd))
            ch.wait()
            dve.wait_ge(s_n5, G)
            dve.tensor_tensor(same(A[:, g]), same(A[:, g]), same(X[:, g]), ADD).then_inc(s_y2l, 1)

        block = ctx.enter_context(nc.Block())

        @block.sync
        def _(sp):
            for u, unit in enumerate(UNITS):
                for g, b in (unit[0], unit[QB]):
                    sp.dma_start(X[:, g, b:b + QB], x_tok[g][:, b:b + QB]).then_inc(s_x[u], 16)
            for j, row in enumerate((bq, bk, bv)):
                sp.dma_start(bias_col[:, j:j + 1], row.rearrange("(p o) -> p o", o=1)).then_inc(s_b, 16)
            sp.dma_start(bv_row[:], bv.rearrange("(o f) -> o f", o=1).broadcast_to([P, D])).then_inc(s_bc, 16)

            def load_weights(r):
                es = slice(E2 * r, E2 * r + E2)
                sp.dma_start(w1_sb[r], w1[es].rearrange("e p f -> p e f")).then_inc(s_w12[r], 16)
                if r == 0:
                    sp.dma_start(view(space4, E2 * FF, [E2, FC, D]),
                                 w2[es].rearrange("e (c p) d -> p e c d", p=P)).then_inc(s_w12[r], 16)
                else:
                    for j in (0, 2):
                        sp.dma_start(view(space3, 1024 * (1 + j), [2, FC, D]),
                                     w2[E2 + j:E2 + j + 2].rearrange("e (c p) d -> p e c d", p=P)).then_inc(s_w12[r], 16)

            sp.dma_start(b1_sb[:], b1).then_inc(s_b1, 16)
            load_weights(0)
            for j in range(3):
                sp.dma_start(bias_col[:, 3 + j:4 + j], bin_[j * P:(j + 1) * P].rearrange("(p o) -> p o", o=1)).then_inc(s_bin, 16)
            load_weights(1)
            sp.wait_ge(s_ks, 1)
            for r, (_, part) in enumerate(PRODUCTS):
                sp.dma_start(k_dram[:, r * DH:(r + 1) * DH, :].rearrange("h d t -> h d t"),
                             k_parts[:, part, :]).then_inc(s_kst, 16)
            sp.wait_ge(s_const, 8)
            for j in range(E2):
                sp.dma_start(b2_sb[32 * j:32 * j + 1], b2.rearrange("(r j o) d -> j o r d", r=2, o=1)[j]).then_inc(s_b2, 16)
            for j, r in enumerate((ln1g, ln1b, ln2g, ln2b, bout)):
                sp.dma_start(rows[:, j, :], r.rearrange("(o f) -> o f", o=1).broadcast_to([P, D])).then_inc(s_rows, 16)
            sp.dma_start(wg_sb[:], wg).then_inc(s_rows, 16)

            def store_q(half):
                sp.wait_ge(s_qs, QB * (half + 1))
                cols = slice(half * QB * S, (half + 1) * QB * S)
                sp.dma_start(q_dram[:, :, cols].rearrange("r p s -> p r s"), q_parts[:, :, cols]).then_inc(s_qst[half], 16)

            def load_stack(head, half, buf):
                lo = head * DH
                qs = slice(half * QB * S, (half + 1) * QB * S)
                r = 0
                for n in (3, 2, 1):
                    src = q_dram[0:n, bass_ds(lo, DH), qs]
                    sp.dma_start(q_stack[r * DH:(r + n) * DH, buf, :], src).then_inc(s_ql[buf], 16)
                    r += n
                src = k_dram[bass_ds(head, 1), :, :].rearrange("o r t -> (o r) t")
                sp.dma_start(k_plain[0:KROWS, buf, :], src).then_inc(s_ql[buf], 16)
                sp.dma_start(k_shift[0:KROWS, buf, :], src).then_inc(s_ql[buf], 16)

            def load_shift(par, buf):
                sp.dma_start(q_stack[SHIFT_ROW:SHIFT_ROW + PARTS, buf, :].rearrange("r (c s) -> r c s", s=P),
                             max_turned[:, par, :]).then_inc(s_shift, 16)

            def store_attended(head, half, par):
                for bb in range(QB):
                    dst = a_dram[half * QB + bb, bass_ds(head, 1), :, :].rearrange("o r s -> (o r) s")
                    sp.dma_start(dst, attended[32 * bb:32 * bb + DH + 1, par, :]).then_inc(s_ast[par], 16)

            def load_attended(g):
                for par in range(2):
                    sp.wait_ge(s_ast[par], 64 * 4 * (g + 1))
                for h in range(NH // G):
                    src = a_dram[:, bass_ds(g * (NH // G) + h, 1), 0:DH, :]
                    sp.dma_start(A[32 * h:32 * h + 32, bass_ds(g, 1)].rearrange("p o b f -> p (o b) f"),
                                 src.rearrange("b o d (j f) -> (o d j) b f", f=D)).then_inc(s_al, 16)
                    den = a_dram[:, bass_ds(g * (NH // G) + h, 1), DH:DH + 1, :]
                    sp.dma_start(den_sb[32 * h:32 * h + 32], den.rearrange("b h o (j f) -> (h o j) b f", f=D)).then_inc(s_dl, 16)

            def store_inverses(g):
                sp.wait_ge(s_rc, g + 1)
                sp.dma_start(inv_dram.rearrange("h j b f -> (h j b) f"), den_sb[:]).then_inc(s_rs, 16)

            def load_inverses(g):
                sp.wait_ge(s_rs, 16 * (g + 1))
                for h in range(NH // G):
                    src = inv_dram[h:h + 1].rearrange("o j b f -> o j (b f)").broadcast_to([DH, S // D, B * D])
                    sp.dma_start(same(INV[32 * h:32 * h + 32]), src).then_inc(s_rb, 16)

            store_q(0)
            sp.wait_ge(s_kst, 16 * len(PRODUCTS))
            sp.wait_ge(s_const, 8)
            sp.wait_ge(s_qst[0], 16)
            load_stack(0, 0, 0)
            load_stack(1, 0, 2)
            store_q(1)
            sp.wait_ge(s_q13, 2)
            sp.wait_ge(s_qst[1], 16)
            load_stack(0, 1, 1)
            sp.wait_ge(s_csplit, 1)
            c_rows = c_stack[0:PARTS, :].rearrange("q (r j d) -> q r j d", r=2, d=D)
            for j in range(E2):
                sp.dma_start(c_rows[:, :, j, :], c_parts[32 * j:32 * j + 1]).then_inc(s_cl, 16)
            sp.wait_ge(s_free, 8 + 3)
            load_shift(0, 0)
            def slot(i, kk, last):
                kappa = 4 * i + kk
                if not last or kk == 0:
                    if not (isinstance(i, int) and kappa == 0):
                        sp.wait_ge(s_sc, 64 * i + 16 * kk)
                    load_stack(2 * i + (kk + 3) // 2, (kk + 3) % 2, (kk + 3) % 4)
                if not (isinstance(i, int) and kappa == 0):
                    sp.wait_ge(s_pve, 4 * i + kk)
                    store_attended(2 * i + (kk - 1) // 2, (kk - 1) % 2, (kk - 1) % 2)
                if not last or kk < 3:
                    sp.wait_ge(s_free, 36 * i + 17 + 9 * kk + (1 if last and kk == 2 else 3))
                    load_shift((kk + 1) % 2, (kk + 1) % 4)

            def group(g):
                for c in range(8):
                    if c == 1 and not (isinstance(g, int) and g == 0):
                        load_attended(g - 1)
                    if c == 2 and not (isinstance(g, int) and g == 0):
                        store_inverses(g - 1)
                    if c == 3 and not (isinstance(g, int) and g == 0):
                        load_inverses(g - 1)
                    slot(2 * g + c // 4, c % 4, isinstance(g, int) and g == G - 1 and c >= 4)

            group(0)
            with sp.Fori(1, G - 1) as g:
                group(g)
            group(G - 1)
            sp.wait_ge(s_pve, NQ)
            store_attended(NH - 1, 1, 1)
            load_attended(G - 1)
            store_inverses(G - 1)
            load_inverses(G - 1)
            back_end_sp(sp)

        @block.gpsimd
        def _(pool):
            ch = Chain(pool, s_pc, s_passed_pool)
            ch.done(pool.memset(ident[:], 0.0))
            ch.done(pool.memset(upper[:], 1.0))
            ch.done(pool.memset(same_row[:], 0.0))
            ch.done(pool.memset(neg_half[:], -0.5))
            pool.memset(all_ones[:], 1.0).then_inc(s_const, 1)
            pool.memset(ones_stack[:], 1.0).then_inc(s_const, 1)
            ch.wait()
            ch.done(pool.affine_select(out=ident[:], in_=ident[:], compare_op=ALU.not_equal, fill=1.0, base=0,
                                       pattern=[[-1, P]], channel_multiplier=1))
            pool.affine_select(out=upper[:], in_=upper[:], compare_op=ALU.is_ge, fill=0.0, base=0,
                               pattern=[[1, P]], channel_multiplier=-1).then_inc(s_const, 1)
            ch.wait()
            pool.tensor_copy(ident16[:], ident[:]).then_inc(s_const, 1)
            pool.memset(v_heads[:], 0.0).then_inc(s_vset, 1)
            pool.wait_ge(s_vset, 1)
            pool.memset(v_heads[:, :, :, DH:DH + 1], 1.0).then_inc(s_vset, 1)
            for j in (0, 2):
                ins = pool.memset(view(space3, 1024 * j, [1024], F32, KPAD), 0.0)
            ins.then_inc(s_const, 1)
            pool.memset(b1T[:], 0.0)
            pool.memset(b2_sb[:], 0.0)
            pool.memset(k_plain, 0.0).then_inc(s_const, 1)
            ch.done(pool.memset(k_shift[:], 0.0))
            ch.wait()
            ch.done(pool.affine_select(out=k_shift[:], in_=k_shift[:], compare_op=ALU.is_gt, fill=-1.0, base=SHIFT_ROW,
                                       pattern=[[0, 4], [0, S]], channel_multiplier=-1))
            ch.wait()
            pool.affine_select(out=k_shift[:], in_=k_shift[:], compare_op=ALU.is_gt, fill=0.0, base=SHIFT_ROW + PARTS,
                               pattern=[[0, 4], [0, S]], channel_multiplier=-1).then_inc(s_const, 1)
            pool.memset(c_stack[:], 0.0).then_inc(s_const, 1)

            def split_max(count, par):
                hold(pool, s_free, count, s_passed_pool)
                m, r, parts = row_max[:, par], max_rest[:, par], max_parts[:, par]
                ch.done(pool.tensor_copy(parts[:, 0], m))
                ch.wait()
                ch.done(pool.tensor_tensor(r, m, parts[:, 0], SUB))
                ch.wait()
                ch.done(pool.tensor_copy(parts[:, 1], r))
                ch.wait()
                pool.tensor_tensor(parts[:, 2], r, parts[:, 1], SUB).then_inc(s_split, 1)

            def pick_v(head, par):
                pool.tensor_copy(v_head[:, par], v_heads[:, :, head, :]).then_inc(s_v, 1)

            for m in range(-7, 8):
                ch.done(pool.affine_select(out=same_row[:], in_=same_row[:], compare_op=ALU.not_equal, fill=1.0,
                                           base=16 * m, pattern=[[-1, P]], channel_multiplier=1))
                ch.wait()
            ch.done(pool.memset(first_e[:], 1.0))
            ch.done(pool.memset(first_t[:], 1.0))
            ch.wait()
            pool.memset(first_e[:].rearrange("p (t e) -> p t e", e=E)[:, :, 0:1], 0.0).then_inc(s_const, 1)
            pool.memset(first_t[:].rearrange("p (e t) -> p e t", t=T)[:, :, 0:1], 0.0).then_inc(s_const, 1)

            pool.wait_ge(s_bw, 2)
            for j in (1, 3):
                pool.memset(view(space3, 1024 * j, [1024], F32, KPAD), 0.0).then_inc(s_q13, 1)
            pool.wait_ge(s_vb, TC)
            pool.wait_ge(s_vset, 2)
            pick_v(0, 0)
            split_max(8, 0)
            pool.wait_ge(s_rows, 16 * 6)
            pool.wait_ge(s_csum, 1)
            ch.done(pool.tensor_copy(c_parts[:, 0], c_row[:]))
            ch.wait()
            ch.done(pool.tensor_tensor(c_rest[:], c_row[:], c_parts[:, 0], SUB))
            ch.wait()
            ch.done(pool.tensor_copy(c_parts[:, 1], c_rest[:]))
            ch.wait()
            pool.tensor_tensor(c_parts[:, 2], c_rest[:], c_parts[:, 1], SUB).then_inc(s_csplit, 1)

            def slot(i, kk, last):
                if not last or kk < 3:
                    split_max(36 * i + 9 * (kk + 1) + 8, (kk + 1) % 2)
                if kk % 2 == 0 and not (last and kk == 2):
                    if not (isinstance(i, int) and 4 * i + kk == 0):
                        hold(pool, s_pv, 4 * i + kk, s_passed_pool)
                    pick_v(2 * i + kk // 2 + 1, (kk // 2 + 1) % 2)

            def group(g):
                for c in range(8):
                    slot(2 * g + c // 4, c % 4, isinstance(g, int) and g == G - 1 and c >= 4)
                    if not (isinstance(g, int) and g == 0):
                        if c == 3:
                            pool_divide(pool, ch, g - 1)
                        if c == 5:
                            pool_residual(pool, ch, g - 1)
                        if c == 7:
                            pool_input(pool, ch, g - 1)

            POOL_CHAIN = 46
            group(0)
            with pool.Fori(1, G - 1) as g:
                ch.enter(g - 1, POOL_CHAIN)
                group(g)
            ch.leave(G - 2)
            group(G - 1)
            back_end_pool(pool, ch)

        def ring(n):
            return ps[:, 2 * (n % 2):2 * (n % 2) + 2, :]

        col_bank = lambda u: 4 + u % 3
        PV = 7

        @block.tensor
        def _(pe):
            pe.wait_ge(s_const, 4)
            pe.wait_ge(s_w, 16 * 5)
            for j in range(7):
                mm = pe.transpose(ps[:, 4 + j // 4, (j % 4) * P:(j % 4 + 1) * P], w_in[:, j, :], ident[:])
            mm.then_inc(s_wt, 1)
            pe.wait_ge(s_kv, 32)
            for a in range(2):
                for c in range(TC):
                    mm = pe.transpose(ps[:, 6 + a, c * P:(c + 1) * P], kv_in[:, a, c, :], ident[:])
            mm.then_inc(s_kvt, 1)
            pe.wait_ge(s_wtc, 1)
            pe.wait_ge(s_kvtc, 1)
            pe.matmul(ps[:, 4, :], wT[:, 1, :], kvT[:, 0, :], start=True, stop=True).then_inc(s_kp, 1)
            for c in range(TC):
                mm = pe.matmul(ps[:, 5, c * P:(c + 1) * P], kvT[:, 1, c * P:(c + 1) * P], wT[:, 2, :],
                               start=True, stop=True)
            mm.then_inc(s_vp, 1)

            def turn_unit(u):
                pe.wait_ge(s_xn, u + 1)
                for g, b in UNITS[u]:
                    mm = pe.transpose(ps[:, b % QB, g * P:(g + 1) * P], XN[:, g, b, :], ident[:])
                mm.then_inc(s_xt, 1)

            def project_half(half):
                for b in range(QB * half, QB * half + QB):
                    pe.wait_ge(s_xtc, b + 1)
                    pe.matmul(ps[:, b % QB, :], wT[:, 0, :], featT[:, b, :], start=True, stop=True).then_inc(s_qp, 1)

            turn_unit(0)
            turn_unit(1)
            project_half(0)
            pe.wait_ge(s_kpe, 1)
            pe.wait_ge(s_vpe, 1)
            pe.wait_ge(s_b1, 16)
            turn_b1(pe)
            fold_weights(pe, 0)
            pe.wait_ge(s_qe, QB)
            turn_unit(2)
            fold_weights(pe, 1)
            turn_unit(3)
            project_half(1)

            def score_rows(n, quad_buf, bb, pair, waits):
                if waits is not None:
                    pe.wait_ge(s_free, waits)
                for j in range(2):
                    lo = bb * S + (2 * pair + j) * P
                    mm = pe.matmul(ring(n)[:, j, :], q_stack[:, quad_buf, lo:lo + P], k_plain[:, quad_buf, :],
                                   start=True, stop=True)
                mm.then_inc(s_full, 1)

            def turn_max(n, par, waits, split):
                pe.wait_ge(s_free, waits)
                hold(pe, s_split, split, s_passed_pe)
                dst = ps[0:PARTS * QB * TC, 2 * (n % 2), 0:P // 2].bitcast(BF16)
                pe.transpose(dst, max_parts[:, par].rearrange("p r c -> p (r c)"), ident16[:]).then_inc(s_full, 1)

            def score_columns(u, quad_buf, tc, bb, waits):
                if waits is not None:
                    pe.wait_ge(s_pr, waits)
                pe.matmul(ps[:, col_bank(u), :], k_shift[:, quad_buf, tc * P:(tc + 1) * P],
                          q_stack[:, quad_buf, bb * S:(bb + 1) * S], start=True, stop=True).then_inc(s_sc, 1)

            def multiply_v(par, head_par, tc):
                for bb in range(QB):
                    mm = pe.matmul(ps[32 * bb:32 * bb + 32, PV, :], v_head[:, head_par, tc, :],
                                   probs[:, par, bb, :], start=(tc == 0), stop=(tc == TC - 1))
                if tc == TC - 1:
                    mm.then_inc(s_pv, 1)

            pe.wait_ge(s_ql[0], 80)
            pe.wait_ge(s_qe, B)
            n = 0
            for bb in range(QB):
                for pair in range(2):
                    score_rows(n, 0, bb, pair, n - 1 if n >= 2 else None)
                    n += 1
            pe.wait_ge(s_ql[1], 80)
            for bb in range(QB):
                for pair in range(2):
                    score_rows(n, 1, bb, pair, n - 1)
                    n += 1
                if bb == 0:
                    turn_max(n, 0, n - 1, 1)
                    n += 1
            assert n == 17
            pe.wait_ge(s_shift, 16)
            pe.wait_ge(s_Wc, 2)
            pe.wait_ge(s_csum, 1)
            for bb in range(QB):
                score_columns(bb, 0, 0, bb, None if bb < 3 else 1)

            def slot(i, kk, last):
                n0 = 17 + 9 * kk
                rows_too = not (last and kk >= 2)
                n = n0
                for tc in range(TC):
                    final = last and kk == 3 and tc == TC - 1
                    for pair in range(2):
                        if rows_too:
                            if tc == 0 and pair == 0:
                                pe.wait_ge(s_ql[(kk + 2) % 4], 80 * (i + (kk + 2) // 4 + 1))
                            score_rows(n, (kk + 2) % 4, tc, pair, 36 * i + n - 1)
                            n += 1
                        if final:
                            continue
                        if tc == TC - 1 and pair == 0:
                            pe.wait_ge(s_shift, 64 * i + 16 * (kk + 2))
                        for bb in (2 * pair, 2 * pair + 1):
                            u = 16 * kk + 4 * (tc + 1) + bb
                            before = u - 3 + {64: 2, 65: -1, 66: -1}.get(u, 0)
                            score_columns(u % 64, (kk + 1) % 4 if tc == TC - 1 else kk % 4, (tc + 1) % TC, bb,
                                          64 * i + before + 1)
                    if tc == 0 and not (last and kk == 3):
                        turn_max(n, (kk + 1) % 2, 36 * i + n - 1, 4 * i + kk + 2)
                        n += 1
                    if tc == 0:
                        pe.wait_ge(s_v, 2 * i + kk // 2 + 1)
                        if not (isinstance(i, int) and 4 * i + kk == 0):
                            pe.wait_ge(s_pve, 4 * i + kk)
                    pe.wait_ge(s_pr, 64 * i + 16 * kk + 4 * tc + 4)
                    multiply_v(tc % 2, (kk // 2) % 2, tc)

            for kk in range(4):
                slot(0, kk, False)
            with pe.Fori(1, IT - 1) as i:
                for kk in range(4):
                    slot(i, kk, False)
            for kk in range(4):
                slot(IT - 1, kk, True)
            back_end_pe(pe)

        @block.scalar
        def _(act):
            w_row = [wq, wk, wv]
            for j in range(3):
                act.dma_start(w_in[:, j, :], w_row[j]).then_inc(s_w, 16)
            act.dma_start(kv_in[:, 0], keys.rearrange("o (c p) f -> p (o c) f", p=P)).then_inc(s_kv, 16)
            act.dma_start(kv_in[:, 1], values.rearrange("o (c p) f -> p (o c) f", p=P)).then_inc(s_kv, 16)
            act.dma_start(w_in[:, 3:6, :], win.rearrange("(j p) f -> p j f", p=P)).then_inc(s_w, 16)
            act.dma_start(w_in[:, 6, :], wout).then_inc(s_w, 16)
            root(act, 0)
            act.wait_ge(s_wt, 1)
            act.copy(wT[:].rearrange("p j f -> p (j f)"),
                     ps[:, 4:6, :].rearrange("p a b -> p (a b)")[:, 0:7 * P]).then_inc(s_wtc, 1)
            act.wait_ge(s_kvt, 1)
            act.copy(kvT, ps[:, 6:8, :]).then_inc(s_kvtc, 1)
            root(act, 1)
            act.wait_ge(s_b, 16 * 3)
            act.wait_ge(s_kp, 1)
            act.activation(k_rest[:, 0], ps[:, 4, :], ACT.Relu, bias=bias_col[:, 1:2]).then_inc(s_kpe, 1)

            def project_half(half):
                act.wait_ge(s_xt, 2 * (half + 1))
                for b in range(QB * half, QB * half + QB):
                    act.copy(featT[:, b], ps[:, b % QB, :]).then_inc(s_xtc, 1)
                    if b % QB in (1, 2):
                        project_q(act, b - 1)
                if half == 0:
                    root(act, 2)
                for b in range(QB * half + QB - 2, QB * half + QB):
                    project_q(act, b)

            project_half(0)
            copy_weights(act, 0)
            copy_folded(act, 0)
            copy_weights(act, 1)
            copy_folded(act, 1)
            project_half(1)
            act.wait_ge(s_bin, 16 * 3)

            def exps(par, tc, u, waits):
                for bb in range(QB):
                    act.wait_ge(s_sc, waits + bb + 1)
                    act.activation(probs[:, par, bb, :], ps[:, col_bank((u + bb) % 64), :], ACT.Exp,
                                   scale=1.0 / math.sqrt(DH)).then_inc(s_pr, 1)

            exps(0, 0, 0, 0)

            def slot(i, kk, last):
                for tc in range(TC):
                    u = 16 * kk + 4 * (tc + 1)
                    if not (last and kk == 3 and tc == TC - 1):
                        exps((tc + 1) % 2, (tc + 1) % TC, u, 64 * i + u)
                act.wait_ge(s_pv, 4 * i + kk + 1)
                if not (isinstance(i, int) and 4 * i + kk < 2):
                    act.wait_ge(s_ast[kk % 2], 64 * (2 * i + kk // 2))
                act.copy(attended[:, kk % 2, :], ps[:, PV, :]).then_inc(s_pve, 1)

            for kk in range(4):
                slot(0, kk, False)
            with act.Fori(1, IT - 1) as i:
                for kk in range(4):
                    slot(i, kk, False)
            for kk in range(4):
                slot(IT - 1, kk, True)
            back_end_act(act)


        @block.vector
        def _(dve):
            ch = Chain(dve, s_dc, s_passed_dve)

            def norm_unit(u):
                dve.wait_ge(s_x[u], 32)
                at = lambda t: lambda j: t[:, UNITS[u][j][0], UNITS[u][j][1], :]
                norm(dve, ch, u, at(X), at(XN)).then_inc(s_xn, 1)

            norm_unit(0)
            norm_unit(1)
            dve.wait_ge(s_kpe, 1)
            ch.done(dve.tensor_copy(k_parts[:, 0], k_rest[:, 0]))
            ch.wait()
            ch.done(dve.tensor_tensor(k_rest[:, 1], k_rest[:, 0], k_parts[:, 0], SUB))
            ch.wait()
            ch.done(dve.tensor_copy(k_parts[:, 1], k_rest[:, 1]))
            ch.wait()
            dve.tensor_tensor(k_parts[:, 2], k_rest[:, 1], k_parts[:, 1], SUB).then_inc(s_ks, 1)
            dve.wait_ge(s_vp, 1)
            dve.wait_ge(s_bc, 16)
            dve.tensor_tensor(v_tmp[:], ps[:, 5, :].rearrange("p (c f) -> p c f", c=TC),
                              bv_row[:].rearrange("p (o f) -> p o f", o=1).broadcast_to([P, TC, D]), ADD).then_inc(s_vpe, 1)
            dve.wait_ge(s_vpe, 1)
            dve.wait_ge(s_vset, 2)
            for c in range(TC):
                dve.tensor_scalar(v_heads[:, c, :, 0:DH], v_tmp[:, c, :].rearrange("p (h d) -> p h d", d=DH),
                                  0.0, None, MAX).then_inc(s_vb, 1)

            def split_q(b):
                cols = slice(b * S, (b + 1) * S)
                dve.wait_ge(s_qe, b + 1)
                ch.done(dve.tensor_tensor(rest[:, b % 2], qf[b % QB], q_parts[:, 0, cols], SUB))
                ch.wait()
                ch.done(dve.tensor_copy(q_parts[:, 1, cols], rest[:, b % 2]))
                ch.wait()
                dve.tensor_tensor(q_parts[:, 2, cols], rest[:, b % 2], q_parts[:, 1, cols], SUB).then_inc(s_qs, 1)

            norm_unit(2)
            for b in range(QB):
                split_q(b)
            norm_unit(3)
            for b in range(QB, B):
                split_q(b)

            def reduce_rows(n, par, bb, pair, waits):
                dve.wait_ge(s_full, waits)
                c = bb * TC + 2 * pair
                dve.tensor_reduce(row_max[:, par, c:c + 2], ring(n), AX.X, MAX).then_inc(s_free, 1)

            def copy_turned(n, par, waits):
                dve.wait_ge(s_full, waits)
                src = ps[0:PARTS * QB * TC, 2 * (n % 2), 0:P // 2].bitcast(BF16)
                dve.tensor_copy(max_turned[:, par, :], src).then_inc(s_free, 1)

            n = 0
            for bb in range(QB):
                for pair in range(2):
                    reduce_rows(n, 0, bb, pair, n + 1)
                    n += 1
            dve.wait_ge(s_bw, 2)
            dve.wait_ge(s_b2, 16 * E2)
            dve.tensor_tensor(c_row[:], ps[:, C_BANK, P:3 * P].rearrange("p (r d) -> p r d", d=D), b2_sb[:],
                              ADD).then_inc(s_csum, 1)
            for bb in range(QB):
                for pair in range(2):
                    reduce_rows(n, 1, bb, pair, n + 1)
                    n += 1
                if bb == 0:
                    copy_turned(n, 0, n + 1)
                    n += 1

            def slot(i, kk, last, between):
                n = 17 + 9 * kk
                for tc in range(TC):
                    if not (last and kk >= 2):
                        if tc == 0:
                            dve.wait_ge(s_split, 4 * i + kk + 1)
                        for pair in range(2):
                            reduce_rows(n, kk % 2, tc, pair, 36 * i + n + 1)
                            n += 1
                    if tc == 0 and not (last and kk == 3):
                        if not (isinstance(i, int) and 4 * i + kk == 0):
                            dve.wait_ge(s_shift, 64 * i + 16 * kk)
                        copy_turned(n, (kk + 1) % 2, 36 * i + n + 1)
                        n += 1
                    if between:
                        between(tc)

            def group(g):
                first = isinstance(g, int) and g == 0
                for c in range(8):
                    between = None
                    if c == 1 and not first:
                        between = lambda tc: dve_invert(dve, g - 1) if tc == 2 else None
                    if c == 4 and not first:
                        between = lambda tc: dve_statistics(dve, s_r1, g - 1, A, tc)
                    if c == 6 and not first:
                        between = lambda tc: dve_statistics(dve, s_r2, g - 1, X, tc)
                    slot(2 * g + c // 4, c % 4, isinstance(g, int) and g == G - 1 and c >= 4, between)
            group(0)
            with dve.Fori(1, G - 1) as g:
                group(g)
            group(G - 1)
            dve_invert(dve, G - 1)
            back_end_dve(dve, ch)


NAMES = ["L0_attn_queries", "L0_attn_keys", "L0_attn_values", "L0_attn_Wq_w", "L0_attn_Wq_b", "L0_attn_Wk_w",
         "L0_attn_Wk_b", "L0_attn_Wv_w", "L0_attn_Wv_b", "L0_ffn_in_proj_w", "L0_ffn_in_proj_b", "L0_ffn_out_proj_w",
         "L0_ffn_out_proj_b", "L0_ffn_ln1_g", "L0_ffn_ln1_b", "L0_ffn_ln2_g", "L0_ffn_ln2_b", "L0_ffn_wg",
         "L0_ffn_w1", "L0_ffn_b1", "L0_ffn_w2", "L0_ffn_b2"]


def kernel(**inputs):
    import concourse.bacc as bacc
    from concourse import mybir
    from concourse.bass_utils import run_bass_kernel_spmd

    nc = bacc.Bacc("TRN2", target_bir_lowering=False, num_devices=1)
    arrays, args = {}, []
    for name in NAMES:
        a = np.ascontiguousarray(inputs[name])
        arrays[f"in_{name}"] = a
        args.append(nc.dram_tensor(f"in_{name}", a.shape, mybir.dt.from_np(a.dtype), kind="ExternalInput").ap())
    args.append(nc.dram_tensor("out_0", (B, S, D), mybir.dt.float32, kind="ExternalOutput").ap())
    build(nc, *args)
    r = run_bass_kernel_spmd(nc, [arrays], core_ids=[0])
    return r.results[0]["out_0"]
```
